# Optimizing a Trainium2 kernel written in Bass

```python
import numpy as np
import jax
import jax.numpy as jnp

def _softmax(x, axis=-1):
    return jax.nn.softmax(x, axis=axis)

def _gelu(x):
    return jax.nn.gelu(x, approximate=True)

def _silu(x):
    return jax.nn.silu(x)

def _sigmoid(x):
    return jax.nn.sigmoid(x)

def _layernorm(x, axis=-1, eps=1e-05):
    m = jnp.mean(x, axis=axis, keepdims=True)
    v = jnp.var(x, axis=axis, keepdims=True)
    return (x - m) / jnp.sqrt(v + eps)

def _scatter_add(tgt, idx, src, axis=0):
    return tgt.at[idx].add(src)

def _segment_sum(src, seg, n):
    return jax.ops.segment_sum(src, seg, n)
kernel_name = 'mk_xattn_ffn_d4_seqx_r4_c5ddf2'

def setup_inputs(seed: int=0):
    np.random.seed(seed)
    _w = jnp.asarray

    def _rec_inputs():
        import jax
        import jax.numpy as jnp
        _rk = jax.random.key(seed)
        x = -0.0003929 + 0.9999 * jax.random.normal(jax.random.fold_in(_rk, 1), (8, 256, 256), jnp.float32)
        _lenS = 256 - jax.random.randint(jax.random.fold_in(_rk, 7), (8,), 0, max(1, 256 // 4) + 1, jnp.int32)
        _lenS2 = 256 - jax.random.randint(jax.random.fold_in(_rk, 8), (8,), 0, max(1, 256 // 4) + 1, jnp.int32)
        _ctx_768P = jax.random.normal(jax.random.fold_in(_rk, 11), (8, 16, 192), jnp.float32)
        _ctx_768c = jax.random.dirichlet(jax.random.fold_in(_rk, 511), 0.3 * jnp.ones((16,), jnp.float32), (8, 256))
        _ctx_768t = jnp.einsum('bsk,bkd->bsd', _ctx_768c, _ctx_768P)
        _ctx_768t = _ctx_768t * jax.lax.rsqrt(jnp.mean(jnp.square(_ctx_768t)) + 1e-12) * 0.953939
        ctx_768 = -7.36909e-05 + 0.999899 * (_ctx_768t + 0.3 * jax.random.normal(jax.random.fold_in(_rk, 611), (8, 256, 192), jnp.float32))
        return (x, ctx_768)
    x, ctx_768 = _rec_inputs()

    def _L0_xattn_setup():
        import jax, jax.numpy as jnp
        import numpy as np
        EPS = 1e-08
        key = jax.random.key(seed)
        kv, kt, k1, k2, k3, k4 = jax.random.split(key, 6)
        B, S = (16, 256)
        VD, TD, H = (256, 192, 128)
        visual_features = jax.random.normal(kv, (B, S, VD), dtype=jnp.float32)
        text_features = jax.random.normal(kt, (B, S, TD), dtype=jnp.float32)
        Wv = jax.random.normal(k1, (H, VD), dtype=jnp.float32) * (1.0 / np.sqrt(VD))
        bv = jax.random.normal(k2, (H,), dtype=jnp.float32) * 0.01
        Wt = jax.random.normal(k3, (H, TD), dtype=jnp.float32) * (1.0 / np.sqrt(TD))
        bt = jax.random.normal(k4, (H,), dtype=jnp.float32) * 0.01
        return {'visual_features': visual_features, 'text_features': text_features, 'Wv': Wv, 'bv': bv, 'Wt': Wt, 'bt': bt}
    _L0_xattn_all = _L0_xattn_setup()
    _L0_xattn_in = {k: v for k, v in _L0_xattn_all.items() if k in ('Wv', 'bv', 'Wt', 'bt')}
    del _L0_xattn_all

    def _L0_ffn_setup():
        import jax, jax.numpy as jnp
        import numpy as np
        H_DIM, E_DIM = (256, 128)
        N_SHARED, N_ROUTED, TOP_K = (2, 16, 4)
        B, S = (4, 512)
        key = jax.random.key(seed)
        ks = jax.random.split(key, 6)
        sc = 1.0 / np.sqrt(H_DIM)
        ec = 1.0 / np.sqrt(E_DIM)
        return {'x': jax.random.normal(ks[0], (B, S, H_DIM), dtype=jnp.float32), 'shared_up': jax.random.uniform(ks[1], (N_SHARED, E_DIM, H_DIM), jnp.float32, -sc, sc), 'shared_down': jax.random.uniform(ks[2], (N_SHARED, H_DIM, E_DIM), jnp.float32, -ec, ec), 'routed_up': jax.random.uniform(ks[3], (N_ROUTED, E_DIM, H_DIM), jnp.float32, -sc, sc), 'routed_down': jax.random.uniform(ks[4], (N_ROUTED, H_DIM, E_DIM), jnp.float32, -ec, ec), 'router_w': jax.random.uniform(ks[5], (N_ROUTED, H_DIM), jnp.float32, -sc, sc)}
    _L0_ffn_all = _L0_ffn_setup()
    _L0_ffn_in = {k: v for k, v in _L0_ffn_all.items() if k in ('shared_up', 'shared_down', 'routed_up', 'routed_down', 'router_w')}
    del _L0_ffn_all

    def _L1_xattn_setup():
        import jax, jax.numpy as jnp
        import numpy as np
        HEADS = 16
        DIM_HEAD = 64
        SCALE = DIM_HEAD ** (-0.5)
        key = jax.random.key(seed)
        ks = jax.random.split(key, 6)
        B, N, C = (4, 1024, 256)
        M, Cc = (128, 192)
        inner = HEADS * DIM_HEAD
        s = lambda d: d ** (-0.5)
        return {'x': jax.random.normal(ks[0], (B, N, C), jnp.float32), 'context': jax.random.normal(ks[1], (B, M, Cc), jnp.float32), 'Wq': jax.random.normal(ks[2], (C, inner), jnp.float32) * s(C), 'Wk': jax.random.normal(ks[3], (Cc, inner), jnp.float32) * s(Cc), 'Wv': jax.random.normal(ks[4], (Cc, inner), jnp.float32) * s(Cc), 'Wo': jax.random.normal(ks[5], (inner, C), jnp.float32) * s(inner), 'bo': jnp.zeros((C,), jnp.float32)}
    _L1_xattn_all = _L1_xattn_setup()
    _L1_xattn_in = {k: v for k, v in _L1_xattn_all.items() if k in ('Wq', 'Wk', 'Wv', 'Wo', 'bo')}
    del _L1_xattn_all

    def _L1_ffn_setup():
        import jax, jax.numpy as jnp
        import numpy as np
        HIDDEN = 256
        INNER = 1024

        def _weight_quant(w):
            scale = 1.0 / jnp.clip(jnp.mean(jnp.abs(w)), 1e-05)
            wq = jnp.clip(jnp.round(w * scale), -1.0, 1.0) / scale
            return w + jax.lax.stop_gradient(wq - w)

        def _act_quant(x):
            scale = 127.0 / jnp.clip(jnp.max(jnp.abs(x), axis=-1, keepdims=True), 1e-05)
            xq = jnp.clip(jnp.round(x * scale), -128.0, 127.0) / scale
            return x + jax.lax.stop_gradient(xq - x)

        def _bitlinear(x, w):
            return jnp.einsum('bsi,oi->bso', _act_quant(x), _weight_quant(w))
        key = jax.random.key(seed)
        k0, k1, k2, k3 = jax.random.split(key, 4)
        x = jax.random.normal(k0, (4, 512, HIDDEN), dtype=jnp.float32)
        w_gate = jax.random.normal(k1, (INNER, HIDDEN), dtype=jnp.float32) / np.sqrt(HIDDEN)
        w_up = jax.random.normal(k2, (INNER, HIDDEN), dtype=jnp.float32) / np.sqrt(HIDDEN)
        w_down = jax.random.normal(k3, (HIDDEN, INNER), dtype=jnp.float32) / np.sqrt(INNER)
        return {'x': x, 'w_gate': w_gate, 'w_up': w_up, 'w_down': w_down}
    _L1_ffn_all = _L1_ffn_setup()
    _L1_ffn_in = {k: v for k, v in _L1_ffn_all.items() if k in ('w_gate', 'w_up', 'w_down')}
    del _L1_ffn_all

    def _L2_xattn_setup():
        import jax, jax.numpy as jnp
        import numpy as np
        HEADS = 8
        DIM_HEAD = 64
        SCALE = DIM_HEAD ** (-0.5)
        key = jax.random.key(seed)
        ks = jax.random.split(key, 7)
        B, Nq, Nc = (4, 512, 512)
        Dq, Dc = (256, 192)
        inner = HEADS * DIM_HEAD
        x = jax.random.normal(ks[0], (B, Nq, Dq), dtype=jnp.float32)
        context = jax.random.normal(ks[1], (B, Nc, Dc), dtype=jnp.float32)
        Wq = jax.random.normal(ks[2], (Dq, inner), dtype=jnp.float32) * Dq ** (-0.5)
        Wk = jax.random.normal(ks[3], (Dc, inner), dtype=jnp.float32) * Dc ** (-0.5)
        Wv = jax.random.normal(ks[4], (Dc, inner), dtype=jnp.float32) * Dc ** (-0.5)
        Wo = jax.random.normal(ks[5], (inner, Dq), dtype=jnp.float32) * inner ** (-0.5)
        bo = jax.random.normal(ks[6], (Dq,), dtype=jnp.float32) * 0.01
        return {'x': x, 'context': context, 'Wq': Wq, 'Wk': Wk, 'Wv': Wv, 'Wo': Wo, 'bo': bo}
    _L2_xattn_all = _L2_xattn_setup()
    _L2_xattn_in = {k: v for k, v in _L2_xattn_all.items() if k in ('Wq', 'Wk', 'Wv', 'Wo', 'bo')}
    del _L2_xattn_all

    def _L2_ffn_setup():
        import jax, jax.numpy as jnp
        import numpy as np
        B, S, H, DV = (4, 1024, 256, 256)
        E, INNER, P, K = (8, 32, 8, 2)

        def _ln(v, g, b, eps=1e-05):
            m = jnp.mean(v, axis=-1, keepdims=True)
            var = jnp.var(v, axis=-1, keepdims=True)
            return (v - m) * jax.lax.rsqrt(var + eps) * g + b
        key = jax.random.key(seed)
        ks = jax.random.split(key, 8)
        sc = lambda d: 1.0 / np.sqrt(d)
        return {'x': jax.random.normal(ks[0], (B, S, H), jnp.float32), 'Wv': jax.random.normal(ks[1], (DV, H), jnp.float32) * sc(H), 'bv': jnp.zeros((DV,), jnp.float32), 'Wg': jax.random.normal(ks[2], (E, DV), jnp.float32) * sc(DV), 'bg': jnp.zeros((E,), jnp.float32), 'Wp': jax.random.normal(ks[3], (E, P, DV), jnp.float32) * sc(DV), 'alpha': jnp.zeros((), jnp.float32), 'g_r': jnp.ones((E,), jnp.float32), 'b_r': jnp.zeros((E,), jnp.float32), 'g_c': jnp.ones((E,), jnp.float32), 'b_c': jnp.zeros((E,), jnp.float32), 'W1': jax.random.normal(ks[4], (E, INNER, DV), jnp.float32) * sc(DV), 'b1': jnp.zeros((E, INNER), jnp.float32), 'W2': jax.random.normal(ks[5], (E, DV, INNER), jnp.float32) * sc(INNER), 'b2': jnp.zeros((E, DV), jnp.float32)}
    _L2_ffn_all = _L2_ffn_setup()
    _L2_ffn_in = {k: v for k, v in _L2_ffn_all.items() if k in ('Wv', 'bv', 'Wg', 'bg', 'Wp', 'alpha', 'g_r', 'b_r', 'g_c', 'b_c', 'W1', 'b1', 'W2', 'b2')}
    del _L2_ffn_all

    def _L3_xattn_setup():
        import jax, jax.numpy as jnp
        import numpy as np
        import math
        E = 256
        EV = 256
        FFN = 1024
        DINO = 192
        B, S, P = (64, 128, 64)

        def bitnet_linear(x, W, b):
            w_scale = jnp.maximum(jnp.mean(jnp.abs(W)), 1e-05)
            qW = jnp.sign(W) * (jnp.abs(W) > 0.5 * w_scale).astype(W.dtype)
            i_scale = jnp.maximum(jnp.max(jnp.abs(x)), 1e-08) / 127.0
            qx = jnp.clip(jnp.round(x / i_scale), -128.0, 127.0)
            out = jnp.einsum('...i,oi->...o', qx, qW) * (w_scale * i_scale)
            return out + b
        key = jax.random.key(seed)
        ks = iter(jax.random.split(key, 32))

        def lin_w(fin, fout):
            return jax.random.normal(next(ks), (fout, fin), jnp.float32) * math.sqrt(2.0 / fin)
        return {'text_embeddings': jax.random.normal(next(ks), (B, S, E), jnp.float32), 'dinov2_features': jax.random.normal(next(ks), (B, P, DINO), jnp.float32), 'W_d2v': lin_w(DINO, EV), 'b_d2v': jnp.zeros((EV,), jnp.float32), 'W_img': lin_w(EV, E), 'b_img': jnp.zeros((E,), jnp.float32), 'W_txt': lin_w(E, E), 'b_txt': jnp.zeros((E,), jnp.float32), 'W_att0': lin_w(E, E // 2), 'b_att0': jnp.zeros((E // 2,), jnp.float32), 'W_att1': lin_w(E, E // 2), 'b_att1': jnp.zeros((E // 2,), jnp.float32), 'W_f1': lin_w(2 * E, FFN), 'b_f1': jnp.zeros((FFN,), jnp.float32), 'W_f2': lin_w(FFN, E), 'b_f2': jnp.zeros((E,), jnp.float32)}
    _L3_xattn_all = _L3_xattn_setup()
    _L3_xattn_in = {k: v for k, v in _L3_xattn_all.items() if k in ('W_d2v', 'b_d2v', 'W_img', 'b_img', 'W_txt', 'b_txt', 'W_att0', 'b_att0', 'W_att1', 'b_att1', 'W_f1', 'b_f1', 'W_f2', 'b_f2')}
    del _L3_xattn_all

    def _L3_ffn_setup():
        import jax, jax.numpy as jnp
        import numpy as np
        D = 256
        H = 1024
        O = 256
        E = 8
        K = 2
        key = jax.random.key(seed)
        ks = jax.random.split(key, 8)
        B, S = (2, 512)
        x = jax.random.normal(ks[0], (B, S, D), dtype=jnp.float32)
        s = 0.02
        Wr = jax.random.normal(ks[1], (D, E), dtype=jnp.float32) * s
        br = jnp.zeros((E,), dtype=jnp.float32)
        W1 = jax.random.normal(ks[2], (E, D, H), dtype=jnp.float32) * s
        b1 = jnp.zeros((E, H), dtype=jnp.float32)
        W2 = jax.random.normal(ks[3], (E, H, O), dtype=jnp.float32) * s
        b2 = jnp.zeros((E, O), dtype=jnp.float32)
        return {'x': x, 'Wr': Wr, 'br': br, 'W1': W1, 'b1': b1, 'W2': W2, 'b2': b2}
    _L3_ffn_all = _L3_ffn_setup()
    _L3_ffn_in = {k: v for k, v in _L3_ffn_all.items() if k in ('Wr', 'br', 'W1', 'b1', 'W2', 'b2')}
    del _L3_ffn_all
    return {'x': x, 'ctx_768': ctx_768, 'L0_xattn_Wv': _L0_xattn_in['Wv'], 'L0_xattn_bv': _L0_xattn_in['bv'], 'L0_xattn_Wt': _L0_xattn_in['Wt'], 'L0_xattn_bt': _L0_xattn_in['bt'], 'L0_ffn_shared_up': _L0_ffn_in['shared_up'], 'L0_ffn_shared_down': _L0_ffn_in['shared_down'], 'L0_ffn_routed_up': _L0_ffn_in['routed_up'], 'L0_ffn_routed_down': _L0_ffn_in['routed_down'], 'L0_ffn_router_w': _L0_ffn_in['router_w'], 'L1_xattn_Wq': _L1_xattn_in['Wq'], 'L1_xattn_Wk': _L1_xattn_in['Wk'], 'L1_xattn_Wv': _L1_xattn_in['Wv'], 'L1_xattn_Wo': _L1_xattn_in['Wo'], 'L1_xattn_bo': _L1_xattn_in['bo'], 'L1_ffn_w_gate': _L1_ffn_in['w_gate'], 'L1_ffn_w_up': _L1_ffn_in['w_up'], 'L1_ffn_w_down': _L1_ffn_in['w_down'], 'L2_xattn_Wq': _L2_xattn_in['Wq'], 'L2_xattn_Wk': _L2_xattn_in['Wk'], 'L2_xattn_Wv': _L2_xattn_in['Wv'], 'L2_xattn_Wo': _L2_xattn_in['Wo'], 'L2_xattn_bo': _L2_xattn_in['bo'], 'L2_ffn_Wv': _L2_ffn_in['Wv'], 'L2_ffn_bv': _L2_ffn_in['bv'], 'L2_ffn_Wg': _L2_ffn_in['Wg'], 'L2_ffn_bg': _L2_ffn_in['bg'], 'L2_ffn_Wp': _L2_ffn_in['Wp'], 'L2_ffn_alpha': _L2_ffn_in['alpha'], 'L2_ffn_g_r': _L2_ffn_in['g_r'], 'L2_ffn_b_r': _L2_ffn_in['b_r'], 'L2_ffn_g_c': _L2_ffn_in['g_c'], 'L2_ffn_b_c': _L2_ffn_in['b_c'], 'L2_ffn_W1': _L2_ffn_in['W1'], 'L2_ffn_b1': _L2_ffn_in['b1'], 'L2_ffn_W2': _L2_ffn_in['W2'], 'L2_ffn_b2': _L2_ffn_in['b2'], 'L3_xattn_W_d2v': _L3_xattn_in['W_d2v'], 'L3_xattn_b_d2v': _L3_xattn_in['b_d2v'], 'L3_xattn_W_img': _L3_xattn_in['W_img'], 'L3_xattn_b_img': _L3_xattn_in['b_img'], 'L3_xattn_W_txt': _L3_xattn_in['W_txt'], 'L3_xattn_b_txt': _L3_xattn_in['b_txt'], 'L3_xattn_W_att0': _L3_xattn_in['W_att0'], 'L3_xattn_b_att0': _L3_xattn_in['b_att0'], 'L3_xattn_W_att1': _L3_xattn_in['W_att1'], 'L3_xattn_b_att1': _L3_xattn_in['b_att1'], 'L3_xattn_W_f1': _L3_xattn_in['W_f1'], 'L3_xattn_b_f1': _L3_xattn_in['b_f1'], 'L3_xattn_W_f2': _L3_xattn_in['W_f2'], 'L3_xattn_b_f2': _L3_xattn_in['b_f2'], 'L3_ffn_Wr': _L3_ffn_in['Wr'], 'L3_ffn_br': _L3_ffn_in['br'], 'L3_ffn_W1': _L3_ffn_in['W1'], 'L3_ffn_b1': _L3_ffn_in['b1'], 'L3_ffn_W2': _L3_ffn_in['W2'], 'L3_ffn_b2': _L3_ffn_in['b2']}

def reference(x, ctx_768, L0_xattn_Wv, L0_xattn_bv, L0_xattn_Wt, L0_xattn_bt, L0_ffn_shared_up, L0_ffn_shared_down, L0_ffn_routed_up, L0_ffn_routed_down, L0_ffn_router_w, L1_xattn_Wq, L1_xattn_Wk, L1_xattn_Wv, L1_xattn_Wo, L1_xattn_bo, L1_ffn_w_gate, L1_ffn_w_up, L1_ffn_w_down, L2_xattn_Wq, L2_xattn_Wk, L2_xattn_Wv, L2_xattn_Wo, L2_xattn_bo, L2_ffn_Wv, L2_ffn_bv, L2_ffn_Wg, L2_ffn_bg, L2_ffn_Wp, L2_ffn_alpha, L2_ffn_g_r, L2_ffn_b_r, L2_ffn_g_c, L2_ffn_b_c, L2_ffn_W1, L2_ffn_b1, L2_ffn_W2, L2_ffn_b2, L3_xattn_W_d2v, L3_xattn_b_d2v, L3_xattn_W_img, L3_xattn_b_img, L3_xattn_W_txt, L3_xattn_b_txt, L3_xattn_W_att0, L3_xattn_b_att0, L3_xattn_W_att1, L3_xattn_b_att1, L3_xattn_W_f1, L3_xattn_b_f1, L3_xattn_W_f2, L3_xattn_b_f2, L3_ffn_Wr, L3_ffn_br, L3_ffn_W1, L3_ffn_b1, L3_ffn_W2, L3_ffn_b2):
    import jax
    import jax.numpy as jnp

    def _L0_xattn_ref(visual_features, text_features, Wv, bv, Wt, bt):
        import jax, jax.numpy as jnp
        import numpy as np
        EPS = 1e-08
        v = jnp.einsum('bsd,hd->bsh', visual_features, Wv) + bv
        t = jnp.einsum('bsd,hd->bsh', text_features, Wt) + bt
        dots = jnp.einsum('bih,bjh->bij', v, t)
        vn = jnp.linalg.norm(v, axis=-1)
        tn = jnp.linalg.norm(t, axis=-1)
        denom = jnp.maximum(vn[:, :, None] * tn[:, None, :], EPS)
        return dots / denom

    def _L0_ffn_ref(x, shared_up, shared_down, routed_up, routed_down, router_w):
        import jax, jax.numpy as jnp
        import numpy as np
        H_DIM, E_DIM = (256, 128)
        N_SHARED, N_ROUTED, TOP_K = (2, 16, 4)
        B, S = (4, 512)
        b, s, h = x.shape
        xt = x.reshape(-1, h)
        up_s = jnp.einsum('th,seh->tse', xt, shared_up)
        shared = jnp.einsum('tse,she->th', jax.nn.gelu(up_s, approximate=False), shared_down)
        probs = jax.nn.softmax(xt @ router_w.T, axis=-1)
        topk_p, topk_i = jax.lax.top_k(probs, TOP_K)
        gate = jnp.zeros_like(probs).at[jnp.arange(xt.shape[0])[:, None], topk_i].add(topk_p)
        up_r = jnp.einsum('th,reh->tre', xt, routed_up)
        act = jax.nn.gelu(up_r, approximate=False) * gate[:, :, None]
        routed = jnp.einsum('tre,rhe->th', act, routed_down)
        return (shared + routed).reshape(b, s, h)

    def _L1_xattn_ref(x, context, Wq, Wk, Wv, Wo, bo):
        import jax, jax.numpy as jnp
        import numpy as np
        HEADS = 16
        DIM_HEAD = 64
        SCALE = DIM_HEAD ** (-0.5)
        B, N, _ = x.shape
        M = context.shape[1]
        q = (x @ Wq).reshape(B, N, HEADS, DIM_HEAD).transpose(0, 2, 1, 3)
        k = (context @ Wk).reshape(B, M, HEADS, DIM_HEAD).transpose(0, 2, 1, 3)
        v = (context @ Wv).reshape(B, M, HEADS, DIM_HEAD).transpose(0, 2, 1, 3)
        dots = jnp.einsum('bhnd,bhmd->bhnm', q, k) * SCALE
        attn = jax.nn.softmax(dots, axis=-1)
        out = jnp.einsum('bhnm,bhmd->bhnd', attn, v)
        out = out.transpose(0, 2, 1, 3).reshape(B, N, HEADS * DIM_HEAD)
        return out @ Wo + bo

    def _L1_ffn_ref(x, w_gate, w_up, w_down):
        import jax, jax.numpy as jnp
        import numpy as np
        HIDDEN = 256
        INNER = 1024

        def _weight_quant(w):
            scale = 1.0 / jnp.clip(jnp.mean(jnp.abs(w)), 1e-05)
            wq = jnp.clip(jnp.round(w * scale), -1.0, 1.0) / scale
            return w + jax.lax.stop_gradient(wq - w)

        def _act_quant(x):
            scale = 127.0 / jnp.clip(jnp.max(jnp.abs(x), axis=-1, keepdims=True), 1e-05)
            xq = jnp.clip(jnp.round(x * scale), -128.0, 127.0) / scale
            return x + jax.lax.stop_gradient(xq - x)

        def _bitlinear(x, w):
            return jnp.einsum('bsi,oi->bso', _act_quant(x), _weight_quant(w))
        gate = jax.nn.silu(_bitlinear(x, w_gate))
        up = _bitlinear(x, w_up)
        return _bitlinear(gate * up, w_down)

    def _L2_xattn_ref(x, context, Wq, Wk, Wv, Wo, bo):
        import jax, jax.numpy as jnp
        import numpy as np
        HEADS = 8
        DIM_HEAD = 64
        SCALE = DIM_HEAD ** (-0.5)
        B, Nq, _ = x.shape
        q = (x @ Wq).reshape(B, Nq, HEADS, DIM_HEAD)
        k = (context @ Wk).reshape(B, context.shape[1], HEADS, DIM_HEAD)
        v = (context @ Wv).reshape(B, context.shape[1], HEADS, DIM_HEAD)
        sim = jnp.einsum('bihd,bjhd->bhij', q, k) * SCALE
        attn = jax.nn.softmax(sim, axis=-1)
        out = jnp.einsum('bhij,bjhd->bihd', attn, v)
        out = out.reshape(B, Nq, HEADS * DIM_HEAD)
        return out @ Wo + bo

    def _L2_ffn_ref(x, Wv, bv, Wg, bg, Wp, alpha, g_r, b_r, g_c, b_c, W1, b1, W2, b2):
        import jax, jax.numpy as jnp
        import numpy as np
        B, S, H, DV = (4, 1024, 256, 256)
        E, INNER, P, K = (8, 32, 8, 2)

        def _ln(v, g, b, eps=1e-05):
            m = jnp.mean(v, axis=-1, keepdims=True)
            var = jnp.var(v, axis=-1, keepdims=True)
            return (v - m) * jax.lax.rsqrt(var + eps) * g + b
        V = jnp.einsum('bsh,dh->bsd', x, Wv) + bv
        Vf = V.reshape(-1, DV)
        r = Vf @ Wg.T + bg
        pv = jnp.einsum('epd,nd->nep', Wp, Vf)
        c = jnp.sqrt(jnp.sum(pv * pv, axis=-1)) / np.sqrt(P)
        s = _ln(r, g_r, b_r) + jax.nn.sigmoid(alpha) * _ln(c, g_c, b_c)
        topv, sel = jax.lax.top_k(s, K)
        w = jax.nn.softmax(topv, axis=-1)
        delta = jnp.zeros_like(Vf)
        for e in range(E):
            h = jax.nn.silu(Vf @ W1[e].T + b1[e])
            out = h @ W2[e].T + b2[e]
            we = jnp.sum(jnp.where(sel == e, w, 0.0), axis=-1)
            delta = delta + out * we[:, None]
        return (Vf + delta).reshape(V.shape)

    def _L3_xattn_ref(text_embeddings, dinov2_features, W_d2v, b_d2v, W_img, b_img, W_txt, b_txt, W_att0, b_att0, W_att1, b_att1, W_f1, b_f1, W_f2, b_f2):
        import jax, jax.numpy as jnp
        import numpy as np
        import math
        E = 256
        EV = 256
        FFN = 1024
        DINO = 192
        B, S, P = (64, 128, 64)

        def bitnet_linear(x, W, b):
            w_scale = jnp.maximum(jnp.mean(jnp.abs(W)), 1e-05)
            qW = jnp.sign(W) * (jnp.abs(W) > 0.5 * w_scale).astype(W.dtype)
            i_scale = jnp.maximum(jnp.max(jnp.abs(x)), 1e-08) / 127.0
            qx = jnp.clip(jnp.round(x / i_scale), -128.0, 127.0)
            out = jnp.einsum('...i,oi->...o', qx, qW) * (w_scale * i_scale)
            return out + b
        b, s, e = text_embeddings.shape
        vis = bitnet_linear(dinov2_features, W_d2v, b_d2v)
        image_embeds = bitnet_linear(vis, W_img, b_img)
        fused = bitnet_linear(text_embeddings, W_txt, b_txt)
        inv_sqrt_e = 1.0 / math.sqrt(e)
        for Wa, ba in ((W_att0, b_att0), (W_att1, b_att1)):
            kv = bitnet_linear(image_embeds, Wa, ba)
            k = jnp.concatenate([kv, kv], axis=-1)
            scores = jnp.einsum('bse,bpe->bsp', fused, k) * inv_sqrt_e
            attn = jax.nn.softmax(scores, axis=-1)
            fused = fused + 0.1 * jnp.einsum('bsp,bpe->bse', attn, k)
        avg_img = jnp.mean(image_embeds, axis=1, keepdims=True)
        concatenated = jnp.concatenate([fused, jnp.broadcast_to(avg_img, (b, s, e))], axis=-1)
        h = jax.nn.relu(bitnet_linear(concatenated, W_f1, b_f1))
        return bitnet_linear(h, W_f2, b_f2)

    def _L3_ffn_ref(x, Wr, br, W1, b1, W2, b2):
        import jax, jax.numpy as jnp
        import numpy as np
        D = 256
        H = 1024
        O = 256
        E = 8
        K = 2
        B, S, _ = x.shape
        T = B * S
        xf = x.reshape(T, D)
        logits = xf @ Wr + br
        topk_logits, topk_idx = jax.lax.top_k(logits, K)
        gates = jax.nn.softmax(topk_logits, axis=1)
        dense_gates = jnp.zeros((T, E), dtype=logits.dtype).at[jnp.arange(T)[:, None], topk_idx].set(gates)
        h = jax.nn.relu(jnp.einsum('td,edh->teh', xf, W1) + b1)
        y = jnp.einsum('teh,eho->teo', h, W2) + b2
        out = jnp.einsum('te,teo->to', dense_gates, y)
        return out.reshape(B, S, O)
    x = x + _L0_xattn_ref(_layernorm(x, axis=-1), ctx_768, L0_xattn_Wv, L0_xattn_bv, L0_xattn_Wt, L0_xattn_bt)
    x = x + _L0_ffn_ref(_layernorm(x, axis=-1), L0_ffn_shared_up, L0_ffn_shared_down, L0_ffn_routed_up, L0_ffn_routed_down, L0_ffn_router_w)
    x = x + _L1_xattn_ref(_layernorm(x, axis=-1), ctx_768, L1_xattn_Wq, L1_xattn_Wk, L1_xattn_Wv, L1_xattn_Wo, L1_xattn_bo)
    x = x + _L1_ffn_ref(_layernorm(x, axis=-1), L1_ffn_w_gate, L1_ffn_w_up, L1_ffn_w_down)
    x = x + _L2_xattn_ref(_layernorm(x, axis=-1), ctx_768, L2_xattn_Wq, L2_xattn_Wk, L2_xattn_Wv, L2_xattn_Wo, L2_xattn_bo)
    x = x + _L2_ffn_ref(_layernorm(x, axis=-1), L2_ffn_Wv, L2_ffn_bv, L2_ffn_Wg, L2_ffn_bg, L2_ffn_Wp, L2_ffn_alpha, L2_ffn_g_r, L2_ffn_b_r, L2_ffn_g_c, L2_ffn_b_c, L2_ffn_W1, L2_ffn_b1, L2_ffn_W2, L2_ffn_b2)
    x = x + _L3_xattn_ref(_layernorm(x, axis=-1), ctx_768, L3_xattn_W_d2v, L3_xattn_b_d2v, L3_xattn_W_img, L3_xattn_b_img, L3_xattn_W_txt, L3_xattn_b_txt, L3_xattn_W_att0, L3_xattn_b_att0, L3_xattn_W_att1, L3_xattn_b_att1, L3_xattn_W_f1, L3_xattn_b_f1, L3_xattn_W_f2, L3_xattn_b_f2)
    x = x + _L3_ffn_ref(_layernorm(x, axis=-1), L3_ffn_Wr, L3_ffn_br, L3_ffn_W1, L3_ffn_b1, L3_ffn_W2, L3_ffn_b2)
    return x

_drawn_inputs = setup_inputs


def setup_inputs(seed=0):
    import zlib

    import numpy as np

    out = dict(_drawn_inputs(seed))
    spreads = {'L1_xattn_bo': (0.0, 0.1),
     'L2_ffn_bv': (0.0, 0.1),
     'L2_ffn_bg': (0.0, 0.1),
     'L2_ffn_g_r': (1.0, 0.2),
     'L2_ffn_b_r': (0.0, 0.1),
     'L2_ffn_g_c': (1.0, 0.2),
     'L2_ffn_b_c': (0.0, 0.1),
     'L2_ffn_b1': (0.0, 0.1),
     'L2_ffn_b2': (0.0, 0.1),
     'L3_xattn_b_d2v': (0.0, 0.317),
     'L3_xattn_b_img': (0.0, 0.302),
     'L3_xattn_b_txt': (0.0, 0.313),
     'L3_xattn_b_att0': (0.0, 2.0),
     'L3_xattn_b_att1': (0.0, 2.0),
     'L3_xattn_b_f1': (0.0, 0.1),
     'L3_xattn_b_f2': (0.0, 0.1),
     'L3_ffn_br': (0.0, 0.1),
     'L3_ffn_b1': (0.0, 0.453),
     'L3_ffn_b2': (0.0, 0.1)}
    factors = {'L0_xattn_bv': 15.078,
     'L0_xattn_bt': 32.234,
     'L2_xattn_bo': 3.227,
     'L3_xattn_W_att0': 4.44,
     'L3_xattn_W_att1': 4.419}
    for name, (base, spread) in spreads.items():
        noise = np.random.default_rng([zlib.crc32(name.encode()), seed]).standard_normal(out[name].shape)
        drawn = base * np.exp(spread * noise) if base else spread * noise
        out[name] = jnp.asarray(drawn.astype(out[name].dtype))
    for name, factor in factors.items():
        out[name] = (out[name] * factor).astype(out[name].dtype)
    return out
```

```python
import concourse.bass as bass
from concourse import mybir
from concourse.alu_op_type import AluOpType as ALU
from contextlib import ExitStack

F32 = mybir.dt.float32
BF16 = mybir.dt.bfloat16
ACT = mybir.ActivationFunctionType
AX = mybir.AxisListType.X
ds = bass.ds

P = 128
D = 256
KD = D // P
DC = 192
B, S = 8, 256
T = B * S
NT = T // P
CH = 512
NC = T // CH
TPC = CH // P
HALF_C = DC - P
LN_EPS = 1e-5
COS_EPS = 1e-8
ROUND = 12582912.0
NEG = -1.0e30


class Shared:
    pass


class Order:

    def __init__(self, sem):
        self.sem, self.n, self.loop = sem, 0, None

    def begin(self, index, per_trip):
        self.loop = (index, per_trip, self.n)

    def end(self, trips):
        index, per_trip, base = self.loop
        assert self.n - base == per_trip, (self.n - base, per_trip)
        self.n, self.loop = base + trips * per_trip, None

    def mark(self, ins):
        self.n += 1
        return ins.then_inc(self.sem, 1)

    def wait(self, eng):
        eng.wait_ge(self.sem, self.n if self.loop is None else self.loop[0] * self.loop[1] + self.n)

    def step(self, eng, ins):
        self.mark(ins)
        self.wait(eng)


def stage(emit):
    def scoped(K):
        taken = []

        def take(name):
            taken.append(K.nc.alloc_semaphore(name=name))
            return taken[-1]
        outer, K.sem = K.sem, take
        emit(K)
        K.sem = outer
        K.nc.clear_and_free_semaphores(taken)
        K.nc.all_engine_barrier()
    return scoped


def load_rows(eng, dst, src, sem):
    rows = src.shape[0]
    full = rows // P
    eng.dma_start(dst[:, 0:full, :], src[0:full * P, :].rearrange("(k p) n -> p k n", p=P)).then_inc(sem, 16)
    if rows % P:
        eng.dma_start(dst[0:rows % P, full, :], src[full * P:rows, :]).then_inc(sem, 16)
        return 32
    return 16


def start(K):
    nc, a = K.nc, K.a
    loaded, id0 = K.sem("start_loaded"), K.sem("start_ident")
    with nc.Block() as block:
        @block.sync
        def _(sp):
            sp.dma_start(K.X[:], a["x"].rearrange("b (h p) d -> p (b h) d", p=P)).then_inc(loaded, 16)
            n = 16 + load_rows(sp, K.CT, a["ctxT"], loaded)
            sp.wait_ge(loaded, n)

        @block.gpsimd
        def _(pool):
            pool.memset(K.ident[:], 0.0).then_inc(id0, 1)
            pool.memset(K.ones[:], 1.0)
            pool.memset(K.round[:], ROUND)
            pool.wait_ge(id0, 1)
            pool.affine_select(out=K.ident[:], in_=K.ident[:], compare_op=ALU.not_equal, fill=1.0, base=0,
                               pattern=[[-1, P]], channel_multiplier=1).then_inc(id0, 1)
            pool.wait_ge(id0, 2)
            pool.tensor_copy(K.identb[:], K.ident[:])


def finish(K):
    stored = K.sem("stored")
    with K.nc.Block() as block:
        @block.sync
        def _(sp):
            sp.dma_start(K.a["out"].rearrange("b (h p) d -> p (b h) d", p=P), K.X[:]).then_inc(stored, 16)
            sp.wait_ge(stored, 16)


def layernorm(K, name, load=None, quant=None):
    nc, X, XT = K.nc, K.X, K.XT
    with ExitStack() as ctx:
        def sb(n, shape, dt=F32):
            return ctx.enter_context(nc.sbuf_tensor(f"{name}_{n}", shape, dt))
        G = TPC
        st = sb("st", [P, NT, 6])
        small = sb("small", [P, 6, NT])
        mean2, dif, var, std, rstd, nmr = (small[:, i, :] for i in range(6))
        xn = sb("xn", [P, G, D])
        if quant:
            XQT, inv127 = quant
            xr = sb("xr", [P, G, D])
            xq = sb("xq", [P, G, D], BF16)
            amax = sb("amax", [P, G])
            scl = sb("scl", [P, G])
            big = sb("big", [P, 1])
        stats, std_ok, coef_ok = K.sem(name + "_stats"), K.sem(name + "_std"), K.sem(name + "_coef")
        xn_ready, t_done, t_read = K.sem(name + "_xn"), K.sem(name + "_tdone"), K.sem(name + "_tread")
        q_ready = K.sem(name + "_q") if quant else None
        with nc.Block() as block:
            if load:
                @block.sync
                def _(sp):
                    load(sp)

            @block.vector
            def _(dve):
                o = K.dve_order
                with dve.Fori(0, NT // G) as g:
                    for j in range(G):
                        dve.bn_stats(st[:, ds(g * G + j, 1), :], X[:, ds(g * G + j, 1), :]).then_inc(stats, 1)
                dve.wait_ge(stats, NT)
                me, mo, ve, vo = st[:, :, 1], st[:, :, 4], st[:, :, 2], st[:, :, 5]
                o.mark(dve.tensor_tensor(mean2, me, mo, ALU.add))
                o.mark(dve.tensor_tensor(dif, me, mo, ALU.subtract))
                o.step(dve, dve.tensor_tensor(var, ve, vo, ALU.add))
                o.mark(dve.tensor_scalar(var, var, 1.0 / D, LN_EPS, ALU.mult, ALU.add))
                o.step(dve, dve.scalar_tensor_tensor(dif, dif, 0.25, dif, ALU.mult, ALU.mult))
                dve.tensor_tensor(var, var, dif, ALU.add).then_inc(coef_ok, 1)
                dve.wait_ge(std_ok, 1)
                o.step(dve, dve.reciprocal(rstd, std))
                dve.scalar_tensor_tensor(nmr, mean2, -0.5, rstd, ALU.mult, ALU.mult).then_inc(coef_ok, 1)
                with dve.Fori(0, NT // G) as g:
                    if quant:
                        o.begin(g, 8)
                        dve.wait_ge(xn_ready, G * (g + 1))
                        o.step(dve, dve.tensor_reduce(amax[:], xn[:], AX, ALU.max, apply_absolute_value=True))
                        o.step(dve, dve.tensor_scalar(amax[:], amax[:], 1e-5, 1.0 / 127.0, ALU.max, ALU.mult))
                        o.mark(dve.tensor_copy(inv127[:, ds(g * G, G)], amax[:]))
                        o.step(dve, dve.reciprocal(scl[:], amax[:]))
                        for j in range(G):
                            o.mark(dve.tensor_scalar(xr[:, j, :], xn[:, j, :], scl[:, j:j + 1], ROUND, ALU.mult, ALU.add))
                        o.wait(dve)
                        dve.wait_ge(t_done, KD * g)
                        dve.tensor_scalar(xq[:], xr[:], ROUND, None, ALU.subtract).then_inc(q_ready, 1)
                        o.end(NT // G)
                    else:
                        for k in range(KD):
                            dve.wait_ge(t_done, KD * g + k + 1)
                            dve.tensor_copy(XT[:, k, ds(g * CH, CH)], K.bank[k][:]).then_inc(t_read, 1)

            @block.scalar
            def _(act):
                act.wait_ge(coef_ok, 1)
                act.activation(std, var, ACT.Sqrt).then_inc(std_ok, 1)
                act.wait_ge(coef_ok, 2)
                with act.Fori(0, NT // G) as g:
                    act.wait_ge(q_ready, g) if quant else act.wait_ge(t_done, KD * g)
                    for j in range(G):
                        act.activation(xn[:, j, :], X[:, ds(g * G + j, 1), :], ACT.Identity,
                                       bias=nmr[:, ds(g * G + j, 1)], scale=rstd[:, ds(g * G + j, 1)]).then_inc(xn_ready, 1)
                    if quant:
                        for k in range(KD):
                            act.wait_ge(t_done, KD * g + k + 1)
                            act.activation(XQT[:, k, ds(g * CH, CH)], K.bank[k][:, 0:CH // 2].bitcast(BF16), ACT.Copy).then_inc(t_read, 1)

            @block.tensor
            def _(pe):
                src, ident = (xq, K.identb) if quant else (xn, K.ident)
                with pe.Fori(0, NT // G) as g:
                    if quant:
                        pe.wait_ge(q_ready, g + 1)
                    else:
                        pe.wait_ge(xn_ready, G * (g + 1))
                    pe.wait_ge(t_read, KD * g)
                    for k in range(KD):
                        out = K.bank[k][:, 0:CH // 2].bitcast(BF16) if quant else K.bank[k][:]
                        for j in range(G):
                            last = pe.transpose(out[:, j * P:(j + 1) * P], src[:, j, k * P:(k + 1) * P], ident[:])
                        last.then_inc(t_done, 1)


@stage
def l0_cosine(K):
    nc, a, X, XT, CT, bank = K.nc, K.a, K.X, K.XT, K.CT, K.bank
    HV = 128
    with ExitStack() as ctx:
        def sb(n, shape, dt=F32):
            return ctx.enter_context(nc.sbuf_tensor("l0x_" + n, shape, dt))
        wv, wt, bv, bt = sb("wv", [P, KD, HV]), sb("wt", [P, 2, HV]), sb("bv", [P, 1]), sb("bt", [P, 1])
        vT, tT, sq = sb("vT", [P, CH]), sb("tT", [P, CH]), sb("sq", [P, 2, CH])
        norm, rn, lim, cos = sb("norm", [P, 2 * TPC]), sb("rn", [P, 2 * TPC]), sb("lim", [P, TPC, S]), sb("cos", [P, TPC, S])
        loaded = K.sem("l0x_loaded")

        def load(sp):
            load_rows(sp, wv, a["L0_xattn_WvT"], loaded)
            load_rows(sp, wt, a["L0_xattn_WtT"], loaded)
            sp.dma_start(bv[:], a["L0_xattn_bv"].rearrange("(p a) -> p a", a=1)).then_inc(loaded, 16)
            sp.dma_start(bt[:], a["L0_xattn_bt"].rearrange("(p a) -> p a", a=1)).then_inc(loaded, 16)
            sp.wait_ge(loaded, 80)
        layernorm(K, "ln0x", load)

        proj, sides, norms, roots, recips, dots, added = (
            K.sem("l0x_" + n) for n in ("proj", "sides", "norms", "roots", "recips", "dots", "added"))
        with nc.Block() as block:
            @block.tensor
            def _(pe):
                with pe.Fori(0, NC) as c:
                    pe.wait_ge(sides, 4 * c)
                    for k in range(KD):
                        pe.matmul(bank[0][:], wv[:, k, :], XT[:, k, ds(c * CH, CH)], start=k == 0, stop=k == 1)
                    pe.matmul(bank[1][:], wt[:, 0, :], CT[:, 0, ds(c * CH, CH)], start=True, stop=False)
                    pe.matmul(bank[1][:], wt[0:HALF_C, 1, :], CT[0:HALF_C, 1, ds(c * CH, CH)], start=False,
                              stop=True).then_inc(proj, 1)
                    pe.wait_ge(sides, 4 * c + 4)
                    for s in range(2):
                        for j in range(TPC):
                            n = s * TPC + j
                            last = pe.matmul(bank[2][:, n:n + 1], sq[:, s, j * P:(j + 1) * P], K.ones[:, 0:1], start=True, stop=True)
                    last.then_inc(norms, 1)
                    pe.wait_ge(recips, c + 1)
                    pe.wait_ge(added, TPC * c)
                    for j in range(TPC):
                        pe.matmul(bank[3][:, j * P:(j + 1) * P], rn[:, TPC + j:TPC + j + 1].to_broadcast([P, P]),
                                  K.ident[:], start=True, stop=True)
                    for j in range(TPC):
                        b, i = j // 2, j % 2
                        last = pe.matmul(bank[4 + b][:, i * S:(i + 1) * S], vT[:, j * P:(j + 1) * P],
                                         tT[:, b * S:(b + 1) * S], start=True, stop=True)
                    last.then_inc(dots, 1)

            @block.scalar
            def _(act):
                with act.Fori(0, NC) as c:
                    act.wait_ge(proj, c + 1)
                    act.wait_ge(dots, c)
                    act.activation(sq[:, 0, :], bank[0][:], ACT.Square, bias=bv[:]).then_inc(sides, 1)
                    act.activation(sq[:, 1, :], bank[1][:], ACT.Square, bias=bt[:]).then_inc(sides, 1)
                    act.activation(vT[:], bank[0][:], ACT.Identity, bias=bv[:]).then_inc(sides, 1)
                    act.activation(tT[:], bank[1][:], ACT.Identity, bias=bt[:]).then_inc(sides, 1)
                    act.wait_ge(norms, c + 1)
                    act.activation(norm[:], bank[2][:, 0:2 * TPC], ACT.Sqrt).then_inc(roots, 1)

            @block.vector
            def _(dve):
                o = K.dve_order
                with dve.Fori(0, NC) as c:
                    o.begin(c, 2 * TPC)
                    dve.wait_ge(roots, c + 1)
                    dve.reciprocal(rn[:], norm[:]).then_inc(recips, 1)
                    dve.wait_ge(dots, c + 1)
                    for j in range(TPC):
                        b = j // 2
                        o.mark(dve.tensor_scalar(lim[:, j, :], bank[3][:, b * S:(b + 1) * S], rn[:, j:j + 1],
                                                 1.0 / COS_EPS, ALU.mult, ALU.min))
                    o.wait(dve)
                    for j in range(TPC):
                        b, i = j // 2, j % 2
                        o.mark(dve.tensor_tensor(cos[:, j, :], bank[4 + b][:, i * S:(i + 1) * S], lim[:, j, :], ALU.mult))
                    o.wait(dve)
                    for j in range(TPC):
                        xt = X[:, ds(c * TPC + j, 1), :]
                        dve.tensor_tensor(xt, xt, cos[:, j:j + 1, :], ALU.add).then_inc(added, 1)
                    o.end(NC)


def select_top(K, dve, o, vals, top, rep, mask, E, k):
    n = vals.shape[1]
    o.mark(dve.memset(K.carry[:], 0.0))
    for t in range(n):
        o.mark(dve.max(top[:, t, :], vals[:, t, :]))
    o.wait(dve)
    o.step(dve, dve.memset(top[:, :, k:8], NEG))
    o.mark(dve.memset(K.carry[:], 0.0))
    for t in range(n):
        o.mark(dve.match_replace(out=rep[:, t, :], in_to_replace=top[:, t, :], in_values=vals[:, t, :], imm_value=2 * NEG))
    o.wait(dve)
    o.step(dve, dve.tensor_tensor(mask, vals[:, :, 0:E], rep[:, :, 0:E], ALU.is_gt))


def router(K, name, E, k, w, bias, gates, over_all):
    nc, XT, bank = K.nc, K.XT, K.bank
    with ExitStack() as ctx:
        def sb(n, shape, dt=F32):
            return ctx.enter_context(nc.sbuf_tensor(f"{name}_{n}", shape, dt))
        W = E + 8 - k
        lT, vals, top, rep = sb("lT", [E, T]), sb("vals", [P, NT, W]), sb("top", [P, NT, 8]), sb("rep", [P, NT, W])
        mask, ex, mx, sm = sb("mask", [P, NT, E]), sb("ex", [P, NT, E]), sb("mx", [P, NT, 1]), sb("sm", [P, NT, 1])
        lg, cp, tr, sh, xp = (K.sem(f"{name}_{n}") for n in ("logits", "copied", "turned", "shifted", "exp"))
        with nc.Block() as block:
            @block.tensor
            def _(pe):
                with pe.Fori(0, NC) as c:
                    pe.wait_ge(cp, c)
                    for kk in range(KD):
                        last = pe.matmul(bank[0][0:E, :], w[:, kk, :], XT[:, kk, ds(c * CH, CH)], start=kk == 0, stop=kk == 1)
                    last.then_inc(lg, 1)
                pe.wait_ge(cp, NC)
                for t in range(NT):
                    last = pe.transpose(bank[1][:, t * E:(t + 1) * E], lT[:, t * P:(t + 1) * P], K.ident[0:E, 0:E])
                last.then_inc(tr, 1)

            @block.scalar
            def _(act):
                with act.Fori(0, NC) as c:
                    act.wait_ge(lg, c + 1)
                    if bias is None:
                        act.activation(lT[:, ds(c * CH, CH)], bank[0][0:E, :], ACT.Copy).then_inc(cp, 1)
                    else:
                        act.activation(lT[:, ds(c * CH, CH)], bank[0][0:E, :], ACT.Identity, bias=bias).then_inc(cp, 1)
                act.wait_ge(sh, 1)
                act.activation(ex[:], ex[:], ACT.Exp).then_inc(xp, 1)

            @block.vector
            def _(dve):
                o = K.dve_order
                o.mark(dve.memset(vals[:, :, E:W], NEG))
                dve.wait_ge(tr, 1)
                lgt = bank[1][:, 0:NT * E].rearrange("p (t e) -> p t e", e=E)
                o.step(dve, dve.tensor_reduce(mx[:], lgt, AX, ALU.max))
                dve.tensor_tensor(ex[:], lgt, mx[:].to_broadcast([P, NT, E]), ALU.subtract).then_inc(sh, 1)
                if over_all:
                    dve.wait_ge(xp, 1)
                    o.step(dve, dve.tensor_reduce(sm[:], ex[:], AX, ALU.add))
                    o.step(dve, dve.reciprocal(sm[:], sm[:]))
                    o.step(dve, dve.tensor_tensor(vals[:, :, 0:E], ex[:], sm[:].to_broadcast([P, NT, E]), ALU.mult))
                    select_top(K, dve, o, vals, top, rep, mask[:], E, k)
                    dve.tensor_tensor(gates, vals[:, :, 0:E], mask[:], ALU.mult)
                else:
                    o.step(dve, dve.tensor_copy(vals[:, :, 0:E], lgt))
                    select_top(K, dve, o, vals, top, rep, mask[:], E, k)
                    dve.wait_ge(xp, 1)
                    o.step(dve, dve.tensor_tensor(ex[:], ex[:], mask[:], ALU.mult))
                    o.step(dve, dve.tensor_reduce(sm[:], ex[:], AX, ALU.add))
                    o.step(dve, dve.reciprocal(sm[:], sm[:]))
                    dve.tensor_tensor(gates, ex[:], sm[:].to_broadcast([P, NT, E]), ALU.mult)


def experts(K, name, E, HT, up, down, b1, func, gates):
    nc, X, XT, bank = K.nc, K.X, K.XT, K.bank
    H = HT * P
    small = HT == 1
    NP = 2 if small else 1
    UB = 2 if small else 4
    YB = bank[4:8]
    with ExitStack() as ctx:
        def sb(n, shape, dt=F32):
            return ctx.enter_context(nc.sbuf_tensor(f"{name}_{n}", shape, dt))
        wu = [sb(f"wu{s}", [P, KD, H]) for s in range(2)]
        wd = [sb(f"wd{s}", [P, HT, D]) for s in range(2)]
        h = sb("h", [P, NP, HT, CH])
        up_done, h_done, y_done, added = (K.sem(f"{name}_{n}") for n in ("updone", "hdone", "ydone", "added"))
        loaded = [K.sem(f"{name}_loaded{s}") for s in range(2)]

        def chunks(eng, body):
            if small:
                for c in range(NC):
                    body(c, c % 2)
            else:
                with eng.Fori(0, NC) as c:
                    body(c, 0)

        with nc.Block() as block:
            @block.sync
            def _(sp):
                def load(e, s):
                    sp.dma_start(wu[s][:], up[ds(e, 1), :, :].rearrange("e (k p) n -> p (e k) n", p=P)).then_inc(loaded[s], 16)
                    sp.dma_start(wd[s][:], down[ds(e, 1), :, :].rearrange("e (k p) n -> p (e k) n", p=P)).then_inc(loaded[s], 16)
                for s in range(2):
                    load(s, s)
                with sp.Fori(0, E // 2 - 1) as pair:
                    for s in range(2):
                        sp.wait_ge(y_done, 2 * NC * (pair * 2 + s + 1) + 2 * (NP - 1))
                        load(pair * 2 + 2 + s, s)

            @block.tensor
            def _(pe):
                pe.sem_inc(y_done, 2 * (NP - 1)) if NP > 1 else None
                with pe.Fori(0, E // 2) as pair:
                    for s in range(2):
                        def chunk(c, par):
                            n = (pair * 2 + s) * NC + c
                            pe.wait_ge(loaded[s], 32 * (pair + 1))
                            for m in range(HT):
                                b = par if small else m % UB
                                pe.wait_ge(h_done, n * HT + m + 1)
                                for k in range(KD):
                                    last = pe.matmul(bank[b][:], wu[s][:, k, m * P:(m + 1) * P], XT[:, k, ds(c * CH, CH)],
                                                     start=k == 0, stop=k == KD - 1)
                                last.then_inc(up_done, 1)
                            pe.wait_ge(h_done, (n + 1) * HT + UB)
                            for half in range(2):
                                yb = YB[par * 2 + half]
                                pe.wait_ge(added, n * TPC + 2 * half + 2)
                                for i in range(2):
                                    j = half * 2 + i
                                    for m in range(HT):
                                        last = pe.matmul(yb[:, i * D:(i + 1) * D], h[:, par, m, j * P:(j + 1) * P], wd[s][:, m, :],
                                                         start=m == 0, stop=m == HT - 1)
                                last.then_inc(y_done, 1)
                        chunks(pe, chunk)

            @block.scalar
            def _(act):
                act.sem_inc(h_done, UB)
                with act.Fori(0, E // 2) as pair:
                    for s in range(2):
                        def chunk(c, par):
                            n = (pair * 2 + s) * NC + c
                            act.wait_ge(y_done, 2 * n)
                            for m in range(HT):
                                b = par if small else m % UB
                                act.wait_ge(up_done, n * HT + m + 1)
                                bias = {} if b1 is None else {"bias": b1(m, pair * 2 + s)}
                                act.activation(h[:, par, m, :], bank[b][:], func, **bias).then_inc(h_done, 1)
                        chunks(act, chunk)

            @block.vector
            def _(dve):
                dve.sem_inc(added, TPC * NP)
                with dve.Fori(0, E // 2) as pair:
                    for s in range(2):
                        def chunk(c, par):
                            n = (pair * 2 + s) * NC + c
                            dve.wait_ge(added, (n + NP) * TPC)
                            for half in range(2):
                                dve.wait_ge(y_done, 2 * (n + NP - 1) + half + 1)
                                for i in range(2):
                                    t = c * TPC + half * 2 + i
                                    xt = X[:, ds(t, 1), :].rearrange("p a d -> p (a d)")
                                    dve.scalar_tensor_tensor(xt, YB[par * 2 + half][:, i * D:(i + 1) * D], gates(t, pair * 2 + s), xt,
                                                             ALU.mult, ALU.add).then_inc(added, 1)
                        chunks(dve, chunk)


@stage
def l0_ffn(K):
    nc, a = K.nc, K.a
    E, NS = 16, 2
    with ExitStack() as ctx:
        w = ctx.enter_context(nc.sbuf_tensor("l0f_wr", [P, KD, E], F32))
        gates = ctx.enter_context(nc.sbuf_tensor("l0f_gates", [P, NT, NS + E], F32))
        loaded = K.sem("l0f_loaded")

        def load(sp):
            load_rows(sp, w, a["L0_ffn_router_wT"], loaded)
            sp.wait_ge(loaded, 16)
        layernorm(K, "ln0f", load)
        with nc.Block() as block:
            @block.gpsimd
            def _(pool):
                pool.memset(gates[:, :, 0:NS], 1.0)
        router(K, "l0r", E, 4, w, None, gates[:, :, NS:NS + E], True)
        experts(K, "l0e", NS + E, 1, a["L0_ffn_upT"], a["L0_ffn_downT"], None, ACT.Gelu,
                lambda t, e: gates[:, ds(t, 1), ds(e, 1)].rearrange("p a e -> p (a e)"))


def cross_attention(K, name, H, wq_d, wk_d, wv_d, wo_d, bo_d):
    nc, a, X, XT, CT, bank = K.nc, K.a, K.X, K.XT, K.CT, K.bank
    DH = 64
    HP, G, QT = H // 2, H // 8, S // P
    Q = HP + 2 * G
    R = 2 * G + 1
    sc, tp, ob, pj = bank[0:2], bank[2:4], bank[4:6], bank[6:8]
    with ExitStack() as ctx:
        def sb(n, shape, dt=F32):
            return ctx.enter_context(nc.sbuf_tensor(f"{name}_{n}", shape, dt))
        wq, wk, wv = sb("wq", [P, KD, H * DH]), sb("wk", [P, 2, H * DH]), sb("wv", [P, 2, H * DH])
        wo, bo = sb("wo", [P, HP, D]), sb("bo", [P, D])
        ctb = sb("ctb", [P, 2, S])
        qk = sb("qk", [P, HP, 2 * S])
        v = sb("v", [P, 2, H * DH])
        nmax = sb("nmax", [P, 2, QT])
        pr = sb("pr", [P, 2, QT, S])
        pt = sb("pt", [P, 2, 2 * S])
        sums, rsum = sb("sums", [P, QT, H]), sb("rsum", [P, QT, 8])
        o, oT, tmp = sb("o", [P, QT, H * DH]), sb("oT", [P, QT, HP, P]), sb("tmp", [P, QT, D])
        loaded = K.sem(name + "_loaded")

        def load(sp):
            n = load_rows(sp, wq, wq_d, loaded) + load_rows(sp, wk, wk_d, loaded) + load_rows(sp, wv, wv_d, loaded)
            n += load_rows(sp, wo, wo_d, loaded)
            sp.dma_start(bo[:], bo_d.rearrange("(a n) -> a n", a=1).partition_broadcast(P)).then_inc(loaded, 16)
            sp.wait_ge(loaded, n + 16)
        layernorm(K, name + "_ln", load)

        ctb_ready, pj_done, pj_read = (K.sem(f"{name}_{x}") for x in ("ctb", "pjdone", "pjread"))
        s_done, max_done, exp_done, t_done, pt_ready, pv_done = (
            K.sem(f"{name}_{x}") for x in ("sdone", "maxdone", "expdone", "tdone", "ptready", "pvdone"))
        o_ready = [K.sem(f"{name}_oready{q}") for q in range(QT)]
        o_read = [K.sem(f"{name}_oread{q}") for q in range(QT)]
        rs_done = K.sem(name + "_rsdone")
        EC, RC = 2, G - 1

        def schedule(eng, qkp, vp, main, drain, tail, order=None, per_trip=0):
            qkp(0)
            vp(0)
            with eng.Fori(0, B - 1) as b:
                if order:
                    order.begin(b, per_trip)
                main(b), qkp(b + 1), drain(b), vp(b + 1), tail(b)
                if order:
                    order.end(B - 1)
            main(B - 1), drain(B - 1), tail(B - 1)

        def nothing(b):
            pass

        with nc.Block() as block:
            @block.gpsimd
            def _(pool):
                def copy_context(b):
                    pool.wait_ge(pj_done, Q * b)
                    pool.tensor_copy(ctb[:, 0, :], CT[:, 0, ds(b * S, S)]).then_inc(ctb_ready, 1)
                    pool.tensor_copy(ctb[0:HALF_C, 1, :], CT[0:HALF_C, 1, ds(b * S, S)]).then_inc(ctb_ready, 1)
                with pool.Fori(0, B) as b:
                    copy_context(b)

            @block.tensor
            def _(pe):
                def qk_products(b):
                    pe.wait_ge(ctb_ready, 2 * (b + 1))
                    for p in range(HP):
                        pe.wait_ge(pj_read, b * Q + p)
                        t, w = pj[p % 2], slice(p * P, (p + 1) * P)
                        for k in range(KD):
                            pe.matmul(t[:, 0:S], wq[:, k, w], XT[:, k, ds(b * S, S)], start=k == 0, stop=k == KD - 1)
                        pe.matmul(t[:, S:2 * S], wk[:, 0, w], ctb[:, 0, :], start=True, stop=False)
                        pe.matmul(t[:, S:2 * S], wk[0:HALF_C, 1, w], ctb[0:HALF_C, 1, :], start=False, stop=True).then_inc(pj_done, 1)

                def v_products(b):
                    for u in range(2 * G):
                        kt, g = u % 2, u // 2
                        n = HP + u
                        pe.wait_ge(pj_read, b * Q + n)
                        t, w = pj[n % 2], slice(g * CH, (g + 1) * CH)
                        pe.matmul(t[:], ctb[:, 0, kt * P:(kt + 1) * P], wv[:, 0, w], start=True, stop=False)
                        pe.matmul(t[:], ctb[0:HALF_C, 1, kt * P:(kt + 1) * P], wv[0:HALF_C, 1, w], start=False,
                                  stop=True).then_inc(pj_done, 1)

                def scores(b, h):
                    n = b * H + h
                    pe.wait_ge(pj_read, b * Q + h // 2 + 2)
                    pe.wait_ge(exp_done, 2 * n)
                    r = slice((h % 2) * DH, (h % 2 + 1) * DH)
                    for q in range(QT):
                        last = pe.matmul(sc[h % 2][:, q * S:(q + 1) * S], qk[r, h // 2, q * P:(q + 1) * P],
                                         qk[r, h // 2, S:2 * S], start=True, stop=True)
                    last.then_inc(s_done, 1)

                def turn(b, h):
                    n = b * H + h
                    pe.wait_ge(exp_done, 2 * (n + 1) + EC)
                    pe.wait_ge(pt_ready, n)
                    for kt in range(2):
                        for q in range(QT):
                            c = (kt * QT + q) * P
                            last = pe.transpose(tp[h % 2][:, c:c + P], pr[:, h % 2, q, kt * P:(kt + 1) * P], K.ident[:])
                    last.then_inc(t_done, 1)

                def values(b, h):
                    n = b * H + h
                    g = h // 8
                    pe.wait_ge(pt_ready, n + 2)
                    if h == 0:
                        pe.wait_ge(pj_read, (b + 1) * Q + 1)
                    for q in range(QT):
                        if h % 8 == 0:
                            pe.wait_ge(o_read[q], b * R + g)
                        for kt in range(2):
                            c = (kt * QT + q) * P
                            last = pe.matmul(ob[q][:, (h % 8) * DH:(h % 8 + 1) * DH], pt[:, h % 2, c:c + P],
                                             v[:, kt, h * DH:(h + 1) * DH], start=kt == 0, stop=kt == 1)
                    last.then_inc(pv_done, 1)

                def main(b):
                    for h in range(H):
                        scores(b, h)
                        if h >= 1:
                            turn(b, h - 1)
                        if h >= 2:
                            values(b, h - 2)

                def drain(b):
                    turn(b, H - 1)
                    values(b, H - 2)
                    values(b, H - 1)

                def tail(b):
                    for g in range(G):
                        for q in range(QT):
                            pe.wait_ge(o_read[q], b * R + G + g)
                            for i in range(4):
                                last = pe.transpose(ob[q][:, i * P:(i + 1) * P], o[:, q, (g * 4 + i) * P:(g * 4 + i + 1) * P], K.ident[:])
                            last.then_inc(o_ready[q], 1)
                    for q in range(QT):
                        pe.wait_ge(o_read[q], b * R + 2 * G)
                        for p in range(HP):
                            last = pe.matmul(ob[q][:, 0:D], oT[:, q, p, :], wo[:, p, :], start=p == 0, stop=p == HP - 1)
                        last.then_inc(o_ready[q], 1)
                schedule(pe, qk_products, v_products, main, drain, tail)

            @block.scalar
            def _(act):
                act.sem_inc(pj_read, 1)
                act.sem_inc(exp_done, EC)

                def copy_qk(b):
                    act.wait_ge(s_done, H * b)
                    for p in range(HP):
                        act.wait_ge(pj_done, b * Q + p + 1)
                        act.activation(qk[:, p, 0:S], pj[p % 2][:, 0:S], ACT.Copy, scale=DH ** -0.5)
                        act.activation(qk[:, p, S:2 * S], pj[p % 2][:, S:2 * S], ACT.Copy).then_inc(pj_read, 1)

                def copy_v(b):
                    act.wait_ge(pv_done, H * b + 1)
                    for u in range(2 * G):
                        n = HP + u
                        act.wait_ge(pj_done, b * Q + n + 1)
                        act.activation(v[:, u % 2, (u // 2) * CH:(u // 2 + 1) * CH], pj[n % 2][:], ACT.Copy).then_inc(pj_read, 1)

                def main(b):
                    for h in range(H):
                        n = b * H + h
                        act.wait_ge(max_done, n + 1)
                        act.wait_ge(t_done, n)
                        if h % 8 == 0:
                            act.wait_ge(rs_done, b * G + h // 8)
                        for q in range(QT):
                            act.activation(pr[:, h % 2, q, :], sc[h % 2][:, q * S:(q + 1) * S], ACT.Exp, bias=nmax[:, h % 2, q:q + 1],
                                           accum_out=sums[:, q, h:h + 1]).then_inc(exp_done, 1)
                schedule(act, copy_qk, copy_v, main, nothing, nothing)

            @block.vector
            def _(dve):
                order = K.dve_order
                dve.sem_inc(pt_ready, 1)
                dve.sem_inc(t_done, 1)
                dve.sem_inc(pv_done, 1)
                if RC:
                    dve.sem_inc(rs_done, RC)

                def maximum(b, h):
                    n = b * H + h
                    dve.wait_ge(s_done, n + 1)
                    dve.wait_ge(exp_done, 2 * n)
                    dve.tensor_reduce(nmax[:, h % 2, :], sc[h % 2][:].rearrange("p (q s) -> p q s", q=QT), AX, ALU.max,
                                      negate=True).then_inc(max_done, 1)

                def copy_turned(b, h):
                    n = b * H + h
                    dve.wait_ge(t_done, n + 2)
                    dve.wait_ge(pv_done, n)
                    dve.tensor_copy(pt[:, h % 2, :], tp[h % 2][:]).then_inc(pt_ready, 1)

                def normalise(b, g):
                    dve.wait_ge(pv_done, b * H + 8 * (g + 1) + 1)
                    dve.wait_ge(o_read[QT - 1], b * R + g)
                    dve.reciprocal(rsum[:], sums[:, :, g * 8:(g + 1) * 8]).then_inc(rs_done, 1)
                    dve.wait_ge(rs_done, b * G + g + 1 + RC)
                    for q in range(QT):
                        dve.tensor_tensor(o[:, q, g * CH:(g + 1) * CH].rearrange("p (h d) -> p h d", d=DH),
                                          ob[q][:].rearrange("p (h d) -> p h d", d=DH),
                                          rsum[:, q, :].unsqueeze(2).to_broadcast([P, 8, DH]), ALU.mult).then_inc(o_read[q], 1)

                def main(b):
                    for h in range(H):
                        maximum(b, h)
                        if h >= 1:
                            copy_turned(b, h - 1)
                        if h >= 2 and (h - 2) % 8 == 7:
                            normalise(b, (h - 2) // 8)

                def drain(b):
                    copy_turned(b, H - 1)
                    normalise(b, G - 1)

                def tail(b):
                    for g in range(G):
                        for q in range(QT):
                            dve.wait_ge(o_ready[q], b * (G + 1) + g + 1)
                            dve.tensor_copy(oT[:, q, g * 4:(g + 1) * 4, :], ob[q][:].rearrange("p (i n) -> p i n", i=4)).then_inc(o_read[q], 1)
                    for q in range(QT):
                        dve.wait_ge(o_ready[q], b * (G + 1) + G + 1)
                        dve.tensor_tensor(tmp[:, q, :], ob[q][:, 0:D], bo[:], ALU.add).then_inc(o_read[q], 1)
                    for q in range(QT):
                        dve.wait_ge(o_read[q], (b + 1) * R)
                        xt = X[:, ds(b * QT + q, 1), :]
                        dve.tensor_tensor(xt, xt, tmp[:, q:q + 1, :], ALU.add)
                schedule(dve, nothing, nothing, main, drain, tail)


def l1_xattn(K):
    a = K.a
    cross_attention(K, "l1x", 16, a["L1_xattn_Wq"], a["L1_xattn_Wk"], a["L1_xattn_Wv"], a["L1_xattn_Wo"], a["L1_xattn_bo"])


def l2_xattn(K):
    a = K.a
    cross_attention(K, "l2x", 8, a["L2_xattn_Wq"], a["L2_xattn_Wk"], a["L2_xattn_Wv"], a["L2_xattn_Wo"], a["L2_xattn_bo"])


def ternary(K, name, weights, ones_bank=None):
    nc = K.nc
    with ExitStack() as ctx:
        n_w = len(weights)
        asum = ctx.enter_context(nc.sbuf_tensor(name + "_asum", [P, n_w], F32))
        thr = ctx.enter_context(nc.sbuf_tensor(name + "_thr", [P, 2, n_w], F32))
        below = [ctx.enter_context(nc.sbuf_tensor(f"{name}_below{i}", list(w.shape), BF16)) for i, (w, _, _, _) in enumerate(weights)]
        summed, total, ready = K.sem(name + "_summed"), K.sem(name + "_total"), K.sem(name + "_thr")
        loaded = [K.sem(f"{name}_loaded{i}") for i in range(n_w)]
        with nc.Block() as block:
            @block.sync
            def _(sp):
                for i, (w, src, _, _) in enumerate(weights):
                    load_rows(sp, w, src, loaded[i])

            @block.vector
            def _(dve):
                o = K.dve_order
                o.step(dve, dve.memset(asum[:], 0.0))
                for i, (w, src, _, _) in enumerate(weights):
                    rows = src.shape[0]
                    dve.wait_ge(loaded[i], 16 * (1 + (rows % P > 0)))
                    if rows % P == 0:
                        o.mark(dve.tensor_reduce(asum[:, i:i + 1], w[:].rearrange("p k n -> p (k n)"), AX, ALU.add, apply_absolute_value=True))
                    else:
                        o.step(dve, dve.tensor_reduce(asum[:, i:i + 1], w[:, 0, :], AX, ALU.add, apply_absolute_value=True))
                        o.step(dve, dve.tensor_reduce(thr[0:rows - P, 0, i:i + 1], w[0:rows - P, 1, :], AX, ALU.add, apply_absolute_value=True))
                        o.mark(dve.tensor_tensor(asum[0:rows - P, i:i + 1], asum[0:rows - P, i:i + 1], thr[0:rows - P, 0, i:i + 1], ALU.add))
                o.wait(dve)
                dve.sem_inc(summed, 1)
                dve.wait_ge(total, 1)
                for i, (w, src, _, scale) in enumerate(weights):
                    count = src.shape[0] * src.shape[1]
                    o.mark(dve.tensor_scalar(scale, K.bank[0][:, i:i + 1], 1.0 / count, 1e-5, ALU.mult, ALU.max))
                o.wait(dve)
                for i, (_, _, _, scale) in enumerate(weights):
                    o.mark(dve.tensor_scalar(thr[:, 0, i:i + 1], scale, 0.5, None, ALU.mult))
                    o.mark(dve.tensor_scalar(thr[:, 1, i:i + 1], scale, -0.5, None, ALU.mult))
                o.wait(dve)
                for i, (w, src, q, _) in enumerate(weights):
                    for r, ks in row_parts(src.shape[0]):
                        o.mark(dve.tensor_scalar(below[i][r, ks, :], w[r, ks, :], thr[r, 1, i:i + 1], None, ALU.is_lt))
                o.wait(dve)
                for i, (w, src, q, _) in enumerate(weights):
                    for r, ks in row_parts(src.shape[0]):
                        flat = "p k n -> p (k n)"
                        dve.scalar_tensor_tensor(q[r, ks, :].rearrange(flat), w[r, ks, :].rearrange(flat), thr[r, 0, i:i + 1],
                                                 below[i][r, ks, :].rearrange(flat), ALU.is_gt, ALU.subtract)

            @block.tensor
            def _(pe):
                pe.wait_ge(summed, 1)
                pe.matmul(K.bank[0][:, 0:n_w], K.ones[:], asum[:], start=True, stop=True).then_inc(total, 1)


def row_parts(rows):
    full = rows // P
    parts = [(slice(0, P), slice(0, full))]
    return parts + ([(slice(0, rows % P), slice(full, full + 1))] if rows % P else [])


@stage
def l1_ffn(K):
    nc, a, X, bank = K.nc, K.a, K.X, K.bank
    N = 1024
    KN = N // P
    with ExitStack() as ctx:
        def sb(n, shape, dt=F32):
            return ctx.enter_context(nc.sbuf_tensor("l1f_" + n, shape, dt))
        qg, qu, qd = sb("qg", [P, KD, N], BF16), sb("qu", [P, KD, N], BF16), sb("qd", [P, KN, D], BF16)
        scale = sb("scale", [P, 3])
        XQ, inv = sb("xq_t", [P, KD, T], BF16), sb("inv", [P, NT])
        with ExitStack() as wctx:
            wg, wu, wd = (wctx.enter_context(nc.sbuf_tensor("l1f_" + n, s, F32)) for n, s in
                          (("wg", [P, KD, N]), ("wu", [P, KD, N]), ("wd", [P, KN, D])))
            ternary(K, "l1t", [(wg, a["L1_ffn_w_gateT"], qg, scale[:, 0:1]), (wu, a["L1_ffn_w_upT"], qu, scale[:, 1:2]),
                               (wd, a["L1_ffn_w_downT"], qd, scale[:, 2:3])])
        layernorm(K, "l1f_ln", quant=(XQ, inv))
        sg, su = sb("sg", [P, NT]), sb("su", [P, NT])
        g, h, hq = sb("g", [P, N]), sb("h", [P, N]), sb("hq", [P, N], BF16)
        hT = sb("hT", [P, KN, P], BF16)
        amax, hinv, hscl, down = sb("amax", [P, 1]), sb("hinv", [P, 1]), sb("hscl", [P, 1]), sb("down", [P, 1])
        gate_done, up_done, gate_ok, h_ok, q_ok, turned, hT_ok, y_done, added, scl_ok = (
            K.sem("l1f_" + n) for n in ("gate", "up", "gateok", "hok", "qok", "turned", "htok", "ydone", "added", "sclok"))
        gb, ub, tb, yb = bank[0:2], bank[2:4], bank[4], bank[5]
        with nc.Block() as block:
            @block.tensor
            def _(pe):
                def products(out, q, t):
                    for half in range(2):
                        for k in range(KD):
                            last = pe.matmul(out[half][:], XQ[:, k, ds(t * P, P)], q[:, k, half * CH:(half + 1) * CH],
                                             start=k == 0, stop=k == KD - 1)
                    return last

                def down_product(t):
                    pe.wait_ge(q_ok, t + 1)
                    tbf = tb[:].bitcast(BF16)
                    for i in range(KN):
                        last = pe.transpose(tbf[:, i * P:(i + 1) * P], hq[:, i * P:(i + 1) * P], K.identb[:])
                    last.then_inc(turned, 1)
                    pe.wait_ge(hT_ok, t + 1)
                    pe.wait_ge(added, t)
                    for i in range(KN):
                        last = pe.matmul(yb[:, 0:D], hT[:, i, :], qd[:, i, :], start=i == 0, stop=i == KN - 1)
                    last.then_inc(y_done, 1)
                products(gb, qg, 0).then_inc(gate_done, 1)
                products(ub, qu, 0).then_inc(up_done, 1)
                with pe.Fori(0, NT - 1) as t:
                    pe.wait_ge(gate_ok, t + 1)
                    products(gb, qg, t + 1).then_inc(gate_done, 1)
                    pe.wait_ge(h_ok, t + 1)
                    products(ub, qu, t + 1).then_inc(up_done, 1)
                    down_product(t)
                down_product(NT - 1)

            @block.scalar
            def _(act):
                act.wait_ge(scl_ok, 2)
                with act.Fori(0, NT) as t:
                    act.wait_ge(gate_done, t + 1)
                    act.wait_ge(h_ok, t)
                    act.activation(g[:, 0:CH], gb[0][:], ACT.Silu, scale=sg[:, ds(t, 1)])
                    act.activation(g[:, CH:N], gb[1][:], ACT.Silu, scale=sg[:, ds(t, 1)]).then_inc(gate_ok, 1)
                    act.wait_ge(turned, t + 1)
                    act.wait_ge(y_done, t)
                    act.activation(hT[:].rearrange("p i n -> p (i n)"), tb[:].bitcast(BF16), ACT.Copy).then_inc(hT_ok, 1)

            @block.vector
            def _(dve):
                o = K.dve_order
                dve.tensor_scalar(sg[:], inv[:], scale[:, 0:1], None, ALU.mult).then_inc(scl_ok, 1)
                dve.tensor_scalar(su[:], inv[:], scale[:, 1:2], None, ALU.mult).then_inc(scl_ok, 1)
                dve.wait_ge(scl_ok, 2)
                with dve.Fori(0, NT) as t:
                    o.begin(t, 5)
                    dve.wait_ge(up_done, t + 1)
                    dve.wait_ge(gate_ok, t + 1)
                    for half in range(2):
                        c = slice(half * CH, (half + 1) * CH)
                        ins = dve.scalar_tensor_tensor(h[:, c], ub[half][:], su[:, ds(t, 1)], g[:, c], ALU.mult, ALU.mult)
                    ins.then_inc(h_ok, 1)
                    dve.wait_ge(h_ok, t + 1)
                    o.step(dve, dve.tensor_reduce(amax[:], h[:], AX, ALU.max, apply_absolute_value=True))
                    o.step(dve, dve.tensor_scalar(hinv[:], amax[:], 1e-5, 1.0 / 127.0, ALU.max, ALU.mult))
                    o.mark(dve.tensor_scalar(down[:], hinv[:], scale[:, 2:3], None, ALU.mult))
                    o.step(dve, dve.reciprocal(hscl[:], hinv[:]))
                    o.step(dve, dve.tensor_scalar(h[:], h[:], hscl[:], ROUND, ALU.mult, ALU.add))
                    dve.wait_ge(turned, t)
                    dve.tensor_scalar(hq[:], h[:], ROUND, None, ALU.subtract).then_inc(q_ok, 1)
                    dve.wait_ge(y_done, t + 1)
                    xt = X[:, ds(t, 1), :].rearrange("p a d -> p (a d)")
                    dve.scalar_tensor_tensor(xt, yb[:, 0:D], down[:], xt, ALU.mult, ALU.add).then_inc(added, 1)
                    o.end(NT)


@stage
def l2_ffn(K):
    nc, a, X, XT, bank = K.nc, K.a, K.X, K.XT, K.bank
    E, INNER, PROJ, TOP = 8, 32, 8, 2
    NH = E * INNER
    N1 = E + NH + E * PROJ
    W = E + 8 - TOP
    with ExitStack() as ctx:
        def sb(n, shape, dt=F32):
            return ctx.enter_context(nc.sbuf_tensor("l2f_" + n, shape, dt))
        wv, w1, w2 = sb("wv", [P, KD, D]), sb("w1", [P, KD, N1]), sb("w2", [P, KD, D])
        bv, b1, b2 = sb("bv", [P, KD]), sb("b1", [P, N1]), sb("b2", [E, D])
        gb, alpha = sb("gb", [P, 2, 2, E]), sb("alpha", [P, 1])
        vT, r, pv2 = sb("vT", [P, KD, CH]), sb("r", [P, TPC, N1]), sb("pv2", [P, TPC, E * PROJ])
        css = sb("css", [P, TPC * E])
        z, zc, mean, var = sb("z", [P, 2, TPC, E]), sb("zc", [P, 2, TPC, E]), sb("mean", [P, 2 * TPC]), sb("var", [P, 2 * TPC])
        vals, top, rep = sb("vals", [P, TPC, W]), sb("top", [P, TPC, 8]), sb("rep", [P, TPC, W])
        mask, ex, sm, we = sb("mask", [P, TPC, E]), sb("ex", [P, TPC, E]), sb("sm", [P, TPC, 1]), sb("we", [P, TPC, E])
        hid, hT, weT = sb("hid", [P, TPC, NH]), sb("hT", [P, 2, CH]), sb("weT", [E, CH])
        loaded = K.sem("l2f_loaded")

        def load(sp):
            n = load_rows(sp, wv, a["L2_ffn_WvT"], loaded) + load_rows(sp, w1, a["L2_ffn_W1cat"], loaded)
            n += load_rows(sp, w2, a["L2_ffn_W2cat"], loaded)
            small = [(bv[:], a["L2_ffn_bv"]), (b1[:, 0:E + NH], a["L2_ffn_b1cat"].partition_broadcast(P)), (b2[:], a["L2_ffn_b2"]),
                     (alpha[:], a["L2_ffn_alpha"].partition_broadcast(P)),
                     (gb[:].rearrange("p a b e -> p (a b e)"), a["L2_ffn_gb"].partition_broadcast(P))]
            for dst, src in small:
                sp.dma_start(dst, src).then_inc(loaded, 16)
            sp.wait_ge(loaded, n + 16 * len(small))
        layernorm(K, "l2f_ln", load)

        names = ("vdone", "vok", "sdone", "rok", "css", "cok", "var", "std", "sh", "xp", "silu", "hok", "turned", "tok", "ydone", "added", "alpha", "sig")
        v_done, v_ok, s_done, r_ok, css_ok, c_ok, var_ok, std_ok, sh, xp, silu, h_ok, turned, t_ok, y_done, added, al, sg = (
            K.sem("l2f_" + n) for n in names)
        with nc.Block() as block:
            @block.tensor
            def _(pe):
                with pe.Fori(0, NC) as c:
                    pe.wait_ge(t_ok, 3 * c)
                    for m in range(KD):
                        for k in range(KD):
                            last = pe.matmul(bank[m][:], wv[:, k, m * P:(m + 1) * P], XT[:, k, ds(c * CH, CH)], start=k == 0, stop=k == KD - 1)
                        last.then_inc(v_done, 1)
                    pe.wait_ge(v_ok, KD * (c + 1))
                    pe.wait_ge(added, TPC * c)
                    for j in range(TPC):
                        for k in range(KD):
                            last = pe.matmul(bank[2 + j][:, 0:N1], vT[:, k, j * P:(j + 1) * P], w1[:, k, :], start=k == 0, stop=k == KD - 1)
                        last.then_inc(s_done, 1)
                    pe.wait_ge(h_ok, c + 1)
                    for j in range(TPC):
                        pe.transpose(bank[0][0:E, j * P:(j + 1) * P], we[:, j, :], K.ident[:])
                    for k in range(2):
                        for j in range(TPC):
                            last = pe.transpose(bank[6 + k][:, j * P:(j + 1) * P], hid[:, j, k * P:(k + 1) * P], K.ident[:])
                    last.then_inc(turned, 1)
                    pe.wait_ge(t_ok, 3 * (c + 1))
                    for j in range(TPC):
                        w = slice(j * P, (j + 1) * P)
                        y = bank[2 + j // 2][:, (j % 2) * D:(j % 2 + 1) * D]
                        pe.matmul(y, weT[:, w], b2[:], start=True, stop=False)
                        for k in range(2):
                            pe.matmul(y, hT[:, k, w], w2[:, k, :], start=False, stop=False)
                        for k in range(KD):
                            last = pe.matmul(y[:, k * P:(k + 1) * P], vT[:, k, w], K.ident[:], start=False, stop=k == KD - 1)
                        last.then_inc(y_done, 1)

            @block.scalar
            def _(act):
                act.wait_ge(al, 1)
                act.activation(alpha[:], alpha[:], ACT.Sigmoid).then_inc(sg, 1)
                with act.Fori(0, NC) as c:
                    act.wait_ge(y_done, TPC * c)
                    for m in range(KD):
                        act.wait_ge(v_done, KD * c + m + 1)
                        act.activation(vT[:, m, :], bank[m][:], ACT.Identity, bias=bv[:, m:m + 1]).then_inc(v_ok, 1)
                    act.wait_ge(css_ok, c + 1)
                    act.activation(z[:, 1, :, :].rearrange("p t e -> p (t e)"), css[:], ACT.Sqrt, scale=1.0 / PROJ).then_inc(c_ok, 1)
                    act.wait_ge(var_ok, c + 1)
                    act.activation(var[:], var[:], ACT.Sqrt).then_inc(std_ok, 1)
                    act.wait_ge(sh, c + 1)
                    act.activation(ex[:], ex[:], ACT.Exp).then_inc(xp, 1)
                    act.activation(hid[:], r[:, :, E:E + NH], ACT.Silu).then_inc(silu, 1)
                    act.wait_ge(turned, c + 1)
                    act.activation(weT[:], bank[0][0:E, :], ACT.Copy).then_inc(t_ok, 1)
                    act.activation(hT[:, 0, :], bank[6][:], ACT.Copy).then_inc(t_ok, 1)

            @block.vector
            def _(dve):
                o = K.dve_order
                o.mark(dve.memset(vals[:, :, E:W], NEG))
                o.step(dve, dve.memset(b1[:, E + NH:N1], 0.0))
                dve.sem_inc(al, 1)
                dve.wait_ge(sg, 1)
                bc = [P, 2, TPC, E]
                with dve.Fori(0, NC) as c:
                    o.begin(c, 20 + 2 * TPC)
                    for j in range(TPC):
                        dve.wait_ge(s_done, TPC * c + j + 1)
                        dve.tensor_tensor(r[:, j, :], bank[2 + j][:, 0:N1], b1[:], ALU.add).then_inc(r_ok, 1)
                    dve.wait_ge(r_ok, TPC * (c + 1))
                    pv = r[:, :, E + NH:N1]
                    o.step(dve, dve.tensor_tensor(pv2[:], pv, pv, ALU.mult))
                    dve.tensor_reduce(css[:], pv2[:].rearrange("p t (e q) -> p (t e) q", q=PROJ), AX, ALU.add).then_inc(css_ok, 1)
                    o.step(dve, dve.tensor_copy(z[:, 0, :, :], r[:, :, 0:E]))
                    dve.wait_ge(c_ok, c + 1)
                    zf, zcf = z[:].rearrange("p a t e -> p (a t) e"), zc[:].rearrange("p a t e -> p (a t) e")
                    b8 = [P, 2 * TPC, E]
                    o.step(dve, dve.tensor_reduce(mean[:], zf, AX, ALU.add))
                    o.step(dve, dve.tensor_scalar(mean[:], mean[:], 1.0 / E, None, ALU.mult))
                    o.step(dve, dve.tensor_tensor(zcf, zf, mean[:].unsqueeze(2).to_broadcast(b8), ALU.subtract))
                    o.step(dve, dve.tensor_tensor(zf, zcf, zcf, ALU.mult))
                    o.step(dve, dve.tensor_reduce(var[:], zf, AX, ALU.add))
                    dve.tensor_scalar(var[:], var[:], 1.0 / E, LN_EPS, ALU.mult, ALU.add).then_inc(var_ok, 1)
                    dve.wait_ge(std_ok, c + 1)
                    o.step(dve, dve.reciprocal(var[:], var[:]))
                    o.step(dve, dve.tensor_tensor(zcf, zcf, var[:].unsqueeze(2).to_broadcast(b8), ALU.mult))
                    o.step(dve, dve.tensor_tensor(zc[:], zc[:], gb[:, 0, :, :].unsqueeze(2).to_broadcast(bc), ALU.mult))
                    o.step(dve, dve.tensor_tensor(zc[:], zc[:], gb[:, 1, :, :].unsqueeze(2).to_broadcast(bc), ALU.add))
                    o.step(dve, dve.scalar_tensor_tensor(vals[:, :, 0:E], zc[:, 1, :, :], alpha[:], zc[:, 0, :, :], ALU.mult, ALU.add))
                    select_top(K, dve, o, vals, top, rep, mask[:], E, TOP)
                    dve.tensor_tensor(ex[:], vals[:, :, 0:E], top[:, :, 0:1].to_broadcast([P, TPC, E]), ALU.subtract).then_inc(sh, 1)
                    dve.wait_ge(xp, c + 1)
                    o.step(dve, dve.tensor_tensor(ex[:], ex[:], mask[:], ALU.mult))
                    o.step(dve, dve.tensor_reduce(sm[:], ex[:], AX, ALU.add))
                    o.step(dve, dve.reciprocal(sm[:], sm[:]))
                    o.step(dve, dve.tensor_tensor(we[:], ex[:], sm[:].to_broadcast([P, TPC, E]), ALU.mult))
                    dve.wait_ge(silu, c + 1)
                    hv = hid[:].rearrange("p t (e i) -> p (t e) i", i=INNER)
                    dve.tensor_tensor(hv, hv, we[:].rearrange("p t e -> p (t e)").unsqueeze(2).to_broadcast([P, TPC * E, INNER]), ALU.mult).then_inc(h_ok, 1)
                    dve.wait_ge(turned, c + 1)
                    dve.tensor_copy(hT[:, 1, :], bank[7][:]).then_inc(t_ok, 1)
                    for j in range(TPC):
                        dve.wait_ge(y_done, TPC * c + TPC)
                        xt = X[:, ds(c * TPC + j, 1), :].rearrange("p a d -> p (a d)")
                        dve.tensor_tensor(xt, xt, bank[2 + j // 2][:, (j % 2) * D:(j % 2 + 1) * D], ALU.add).then_inc(added, 1)
                    o.end(NC)


def global_quant(K, name, items):
    nc = K.nc
    n_i = len(items)
    n_p = sum(len(parts) for parts, _ in items)
    with ExitStack() as ctx:
        def sb(n, shape, dt=F32):
            return ctx.enter_context(nc.sbuf_tensor(f"{name}_{n}", shape, dt))
        part_max, item_max = sb("pmax", [P, n_p]), sb("imax", [P, n_i])
        top, inv = sb("top", [n_i, 1]), sb("inv", [P, n_i])
        maxed, turned, topped, spread, inv_ok, scaled = (K.sem(f"{name}_{x}") for x in ("maxed", "turned", "topped", "spread", "inv", "scaled"))
        with nc.Block() as block:
            @block.vector
            def _(dve):
                o = K.dve_order
                o.step(dve, dve.memset(part_max[:], 0.0))
                n = 0
                for parts, _ in items:
                    for x, q in parts:
                        o.mark(dve.tensor_reduce(part_max[0:x.shape[0], n:n + 1], x, AX, ALU.max, apply_absolute_value=True))
                        n += 1
                o.wait(dve)
                n = 0
                for i, (parts, _) in enumerate(items):
                    dve.tensor_reduce(item_max[:, i:i + 1], part_max[:, n:n + len(parts)], AX, ALU.max).then_inc(maxed, 1)
                    n += len(parts)
                dve.wait_ge(turned, 1)
                dve.tensor_reduce(top[:], K.bank[0][0:n_i, 0:P], AX, ALU.max).then_inc(topped, 1)
                dve.wait_ge(spread, 1)
                for i, (_, s) in enumerate(items):
                    o.mark(dve.tensor_scalar(s, K.bank[1][:, i:i + 1], 1e-8, 1.0 / 127.0, ALU.max, ALU.mult))
                o.wait(dve)
                for i, (_, s) in enumerate(items):
                    dve.reciprocal(inv[:, i:i + 1], s).then_inc(inv_ok, 1)
                n = 0
                for parts, _ in items:
                    for x, q in parts:
                        n += 1
                        dve.wait_ge(scaled, n)
                        dve.tensor_scalar(q, x, ROUND, None, ALU.subtract)

            @block.tensor
            def _(pe):
                pe.wait_ge(maxed, n_i)
                pe.transpose(K.bank[0][0:n_i, 0:P], item_max[:], K.ident[:]).then_inc(turned, 1)
                pe.wait_ge(topped, 1)
                pe.matmul(K.bank[1][:, 0:n_i], top[:].to_broadcast([n_i, P]), K.ident[0:n_i, 0:n_i], start=True, stop=True).then_inc(spread, 1)

            @block.scalar
            def _(act):
                act.wait_ge(inv_ok, n_i)
                for i, (parts, _) in enumerate(items):
                    for x, q in parts:
                        p = x.shape[0]
                        act.activation(x, x, ACT.Identity, bias=K.round[0:p, :], scale=inv[0:p, i:i + 1]).then_inc(scaled, 1)


def bit_linear(K, name, jobs, relu=False):
    nc = K.nc
    units = [(j, m) for j, job in enumerate(jobs) for m in range(job[3].shape[1])]
    R = min(4, len(units))
    assert len(units) % R == 0
    with ExitStack() as ctx:
        scale = ctx.enter_context(nc.sbuf_tensor(name + "_scale", [P, len(jobs)], F32))
        scale_ok, done, read = K.sem(name + "_scale"), K.sem(name + "_done"), K.sem(name + "_read")
        with nc.Block() as block:
            @block.vector
            def _(dve):
                for j, job in enumerate(jobs):
                    dve.tensor_tensor(scale[:, j:j + 1], job[4], job[5], ALU.mult).then_inc(scale_ok, 1)

            @block.tensor
            def _(pe):
                with pe.Fori(0, NC) as c:
                    for u, (j, m) in enumerate(units):
                        q, qw, rows = jobs[j][:3]
                        pe.wait_ge(read, c * len(units) + u + 1)
                        kts = -(-rows // P)
                        for k in range(kts):
                            p = min(P, rows - k * P)
                            last = pe.matmul(K.bank[u % R][:], qw[0:p, k, m * P:(m + 1) * P], q[0:p, k, ds(c * CH, CH)], start=k == 0, stop=k == kts - 1)
                        last.then_inc(done, 1)

            @block.scalar
            def _(act):
                act.sem_inc(read, R)
                act.wait_ge(scale_ok, len(jobs))
                with act.Fori(0, NC) as c:
                    for u, (j, m) in enumerate(units):
                        out, bias = jobs[j][3], jobs[j][6]
                        act.wait_ge(done, c * len(units) + u + 1)
                        act.activation(out[:, m, ds(c * CH, CH)], K.bank[u % R][:], ACT.Relu if relu else ACT.Identity,
                                       bias=bias[:, m:m + 1], scale=scale[:, j:j + 1]).then_inc(read, 1)


def shared_key_attention(K, name, F, kv):
    nc, bank = K.nc, K.bank
    NB, QT, A = 2, S // P, len(kv)
    with ExitStack() as ctx:
        def sb(n, shape, dt=F32):
            return ctx.enter_context(nc.sbuf_tensor(f"{name}_{n}", shape, dt))
        fs, kb, kt = sb("fs", [P, NB, S]), sb("kb", [P, NB, S]), sb("kt", [P, NB, 2, P])
        nmax, sums, rs = sb("nmax", [P, NB * QT]), sb("sums", [P, NB * QT]), sb("rs", [P, NB * QT])
        pr, pt = sb("pr", [P, NB, QT, S]), sb("pt", [P, NB, 2 * S])
        kb_ok, fs_ok, s_done, kt_ok, max_ok, exp_ok, pr_ok, t_done, pt_ok, y_done, added = (
            K.sem(f"{name}_{x}") for x in ("kb", "fs", "sdone", "kt", "max", "exp", "pr", "tdone", "pt", "ydone", "added"))
        with nc.Block() as block:
            @block.gpsimd
            def _(pool):
                with pool.Fori(0, B // NB) as g:
                    for i in range(A):
                        n = g * A + i
                        pool.wait_ge(t_done, n)
                        pool.tensor_copy(kb[:].rearrange("p b s -> p (b s)"), kv[i][:, ds(g * NB * S, NB * S)]).then_inc(kb_ok, 1)

            @block.tensor
            def _(pe):
                with pe.Fori(0, B // NB) as g:
                    for i in range(A):
                        n = g * A + i
                        pe.wait_ge(kb_ok, n + 1)
                        pe.wait_ge(fs_ok, n + 1)
                        for b in range(NB):
                            for q in range(QT):
                                last = pe.matmul(bank[b][:, q * S:(q + 1) * S], fs[:, b, q * P:(q + 1) * P], kb[:, b, :], start=True, stop=True)
                            last.then_inc(s_done, 1)
                        for b in range(NB):
                            for k in range(2):
                                last = pe.transpose(bank[2][:, (b * 2 + k) * P:(b * 2 + k + 1) * P], kb[:, b, k * P:(k + 1) * P], K.ident[:])
                        last.then_inc(s_done, 1)
                        for b in range(NB):
                            pe.wait_ge(pr_ok, NB * n + b + 1)
                            for k in range(2):
                                for q in range(QT):
                                    c = (k * QT + q) * P
                                    last = pe.transpose(bank[3 + b][:, c:c + P], pr[:, b, q, k * P:(k + 1) * P], K.ident[:])
                            if b == NB - 1:
                                last.then_inc(t_done, 1)
                            else:
                                last.then_inc(s_done, 1)
                        pe.wait_ge(kt_ok, n + 1)
                        for b in range(NB):
                            pe.wait_ge(pt_ok, NB * n + b + 1)
                            for k in range(2):
                                last = pe.matmul(bank[5][:, b * S:(b + 1) * S], kt[:, b, k, :], pt[:, b, k * S:(k + 1) * S], start=k == 0, stop=k == 1)
                        last.then_inc(y_done, 1)

            @block.scalar
            def _(act):
                with act.Fori(0, B // NB) as g:
                    for i in range(A):
                        n = g * A + i
                        act.wait_ge(t_done, n)
                        for b in range(NB):
                            act.wait_ge(max_ok, NB * n + b + 1)
                            for q in range(QT):
                                x = b * QT + q
                                act.activation(pr[:, b, q, :], bank[b][:, q * S:(q + 1) * S], ACT.Exp, bias=nmax[:, x:x + 1],
                                               scale=D ** -0.5, accum_out=sums[:, x:x + 1]).then_inc(exp_ok, 1)
                        act.wait_ge(s_done, (NB + NB) * n + NB + 1)
                        act.wait_ge(y_done, n)
                        act.activation(kt[:].rearrange("p b k s -> p (b k s)"), bank[2][:], ACT.Copy).then_inc(kt_ok, 1)

            @block.vector
            def _(dve):
                o = K.dve_order
                with dve.Fori(0, B // NB) as g:
                    o.begin(g, A * NB * 3)
                    for i in range(A):
                        n = g * A + i
                        fb = F[:, :, ds(g * NB * S, NB * S)]
                        dve.wait_ge(added, n)
                        dve.tensor_tensor(fs[:].rearrange("p b s -> p (b s)"), fb[:, 0, :], fb[:, 1, :], ALU.add).then_inc(fs_ok, 1)
                        for b in range(NB):
                            dve.wait_ge(s_done, (NB + NB) * n + b + 1)
                            w = slice(b * QT, (b + 1) * QT)
                            o.step(dve, dve.tensor_reduce(nmax[:, w], bank[b][:].rearrange("p (q s) -> p q s", q=QT), AX, ALU.max, negate=True))
                            dve.tensor_scalar(nmax[:, w], nmax[:, w], D ** -0.5, None, ALU.mult).then_inc(max_ok, 1)
                        for b in range(NB):
                            dve.wait_ge(exp_ok, QT * (NB * n + b + 1))
                            w = slice(b * QT, (b + 1) * QT)
                            o.step(dve, dve.reciprocal(rs[:, w], sums[:, w]))
                            for q in range(QT):
                                x = b * QT + q
                                ins = dve.tensor_scalar(pr[:, b, q, :], pr[:, b, q, :], rs[:, x:x + 1], 0.1, ALU.mult, ALU.mult)
                                if q == 0:
                                    o.mark(ins)
                            ins.then_inc(pr_ok, 1)
                        for b in range(NB):
                            if b == NB - 1:
                                dve.wait_ge(t_done, n + 1)
                            else:
                                dve.wait_ge(s_done, (NB + NB) * n + NB + 2 + b)
                            dve.tensor_copy(pt[:, b, :], bank[3 + b][:]).then_inc(pt_ok, 1)
                        dve.wait_ge(y_done, n + 1)
                        dve.tensor_tensor(fb, fb, bank[5][:].unsqueeze(1).to_broadcast([P, KD, NB * S]), ALU.add).then_inc(added, 1)
                    o.end(B // NB)


@stage
def l3_xattn(K):
    nc, a, X, XT, CT, bank = K.nc, K.a, K.X, K.XT, K.CT, K.bank
    N = 1024
    KN = N // P
    with ExitStack() as ctx:
        def sb(n, shape, dt=F32, c=ctx):
            return c.enter_context(nc.sbuf_tensor("l3x_" + n, shape, dt))
        ws = [("d2v", DC, D), ("img", D, D), ("txt", D, D), ("att0", D, P), ("att1", D, P), ("f1", 2 * D, N), ("f2", N, D)]
        q, scale, bias = {}, sb("wscale", [P, len(ws)]), {}
        for n, rows, cols in ws:
            q[n] = sb("q_" + n, [P, -(-rows // P), cols], BF16)
            bias[n] = sb("b_" + n, [P, D if n == "f2" else cols // P])
        wsc = {n: scale[:, i:i + 1] for i, (n, _, _) in enumerate(ws)}
        loaded = K.sem("l3x_loaded")
        with ExitStack() as wctx:
            ternary(K, "l3t", [(sb("w_" + n, [P, -(-rows // P), cols], F32, wctx), a[f"L3_xattn_W_{n}T"], q[n], wsc[n]) for n, rows, cols in ws])

        def load(sp):
            for n, rows, cols in ws:
                src = a[f"L3_xattn_b_{n}"]
                sp.dma_start(bias[n][:], src.partition_broadcast(P) if n == "f2" else src).then_inc(loaded, 16)
            sp.wait_ge(loaded, 16 * len(ws))
        layernorm(K, "l3x_ln", load)

        s = sb("s", [P, 6])
        hctx = ExitStack()
        hid = sb("hid", [P, KN, T], F32, hctx)
        with ExitStack() as c1:
            qa = sb("qa", [P, 4, T], BF16, c1)
            kv = sb("kv", [P, 2, T], F32, c1)
            avg = sb("avg", [P, KD, B], F32, c1)
            avg_q = sb("avgq", [P, KD, B], BF16, c1)
            global_quant(K, "l3q0", [([(CT[:, 0, :], qa[:, 0, :]), (CT[0:HALF_C, 1, :], qa[0:HALF_C, 1, :])], s[:, 0:1]),
                                     ([(XT[:, k, :], qa[:, 2 + k, :]) for k in range(KD)], s[:, 1:2])])
            VIS, FUSED = CT, XT
            bit_linear(K, "l3l0", [(qa[:, 0:2, :], q["d2v"], DC, VIS, s[:, 0:1], wsc["d2v"], bias["d2v"]),
                                   (qa[:, 2:4, :], q["txt"], D, FUSED, s[:, 1:2], wsc["txt"], bias["txt"])])
            global_quant(K, "l3q1", [([(VIS[:, k, :], qa[:, k, :]) for k in range(KD)], s[:, 2:3])])
            IMG = VIS
            bit_linear(K, "l3l1", [(qa[:, 0:2, :], q["img"], D, IMG, s[:, 2:3], wsc["img"], bias["img"])])
            with nc.Block() as block:
                @block.vector
                def _(dve):
                    for k in range(KD):
                        K.dve_order.step(dve, dve.tensor_reduce(avg[:, k, :], IMG[:, k, :].rearrange("p (b s) -> p b s", s=S), AX, ALU.add))
                    dve.tensor_scalar(avg[:], avg[:], 1.0 / S, None, ALU.mult)
            global_quant(K, "l3q2", [([(IMG[:, k, :], qa[:, k, :]) for k in range(KD)], s[:, 3:4])])
            bit_linear(K, "l3l2", [(qa[:, 0:2, :], q["att%d" % i], D, kv[:, i:i + 1, :], s[:, 3:4], wsc["att%d" % i], bias["att%d" % i])
                                   for i in range(2)])
            shared_key_attention(K, "l3a", FUSED, [kv[:, i, :] for i in range(2)])
            flat = "p k b -> p (k b)"
            global_quant(K, "l3q3", [([(FUSED[:, k, :], qa[:, k, :]) for k in range(KD)]
                                      + [(avg[:].rearrange(flat), avg_q[:].rearrange(flat))], s[:, 4:5])])
            with nc.Block() as block:
                @block.vector
                def _(dve):
                    for k in range(KD):
                        dve.tensor_copy(qa[:, 2 + k, :].rearrange("p (b s) -> p b s", s=S), avg_q[:, k, :].unsqueeze(2).to_broadcast([P, B, S]))
            bit_linear(K, "l3l3", [(qa, q["f1"], 2 * D, hid, s[:, 4:5], wsc["f1"], bias["f1"])], relu=True)
        qh, out_scale = sb("qh", [P, KN, T], BF16, hctx), sb("oscale", [P, 1], F32, hctx)
        tmp = sb("tmp", [P, 2, D], F32, hctx)
        global_quant(K, "l3q4", [([(hid[:, k, :], qh[:, k, :]) for k in range(KN)], s[:, 5:6])])
        y_done, y_read = K.sem("l3x_ydone"), K.sem("l3x_yread")
        with nc.Block() as block:
            @block.tensor
            def _(pe):
                with pe.Fori(0, NT // 2) as g:
                    for i in range(2):
                        pe.wait_ge(y_read, 2 * g + i + 1)
                        for k in range(KN):
                            last = pe.matmul(bank[i][:, 0:D], qh[:, k, ds((g * 2 + i) * P, P)], q["f2"][:, k, :], start=k == 0, stop=k == KN - 1)
                        last.then_inc(y_done, 1)

            @block.vector
            def _(dve):
                o = K.dve_order
                dve.sem_inc(y_read, 2)
                o.step(dve, dve.tensor_tensor(out_scale[:], s[:, 5:6], wsc["f2"], ALU.mult))
                with dve.Fori(0, NT // 2) as g:
                    o.begin(g, 2)
                    for i in range(2):
                        dve.wait_ge(y_done, 2 * g + i + 1)
                        dve.scalar_tensor_tensor(tmp[:, i, :], bank[i][:, 0:D], out_scale[:], bias["f2"][:], ALU.mult, ALU.add).then_inc(y_read, 1)
                        dve.wait_ge(y_read, 2 * g + i + 3)
                        xt = X[:, ds(g * 2 + i, 1), :]
                        o.mark(dve.tensor_tensor(xt, xt, tmp[:, i:i + 1, :], ALU.add))
                    o.wait(dve)
                    o.end(NT // 2)
        hctx.close()


@stage
def l3_ffn(K):
    nc, a, X, bank = K.nc, K.a, K.X, K.bank
    E, N = 8, 1024
    with ExitStack() as ctx:
        def sb(n, shape, dt=F32):
            return ctx.enter_context(nc.sbuf_tensor("l3f_" + n, shape, dt))
        w, br, b1, b2 = sb("wr", [P, KD, E]), sb("br", [E, 1]), sb("b1", [P, E, N // P]), sb("b2", [E, D])
        gates, gT = sb("gates", [P, NT, E]), sb("gT", [E, T])
        loaded = K.sem("l3f_loaded")

        def load(sp):
            load_rows(sp, w, a["L3_ffn_Wr"], loaded)
            sp.dma_start(br[:], a["L3_ffn_br"].rearrange("(e a) -> e a", a=1)).then_inc(loaded, 16)
            sp.dma_start(b1[:], a["L3_ffn_b1p"]).then_inc(loaded, 16)
            sp.dma_start(b2[:], a["L3_ffn_b2"]).then_inc(loaded, 16)
            sp.wait_ge(loaded, 64)
        layernorm(K, "l3f_ln", load)
        router(K, "l3r", E, 2, w, br[:], gates[:], False)
        turned, copied, biased = (K.sem("l3f_" + n) for n in ("turned", "copied", "biased"))
        with nc.Block() as block:
            @block.tensor
            def _(pe):
                for c in range(NC):
                    for j in range(TPC):
                        last = pe.transpose(bank[c][0:E, j * P:(j + 1) * P], gates[:, c * TPC + j, :], K.ident[:])
                    last.then_inc(turned, 1)
                for c in range(NC):
                    pe.wait_ge(copied, c + 1)
                    if c >= 2:
                        pe.wait_ge(copied, NC)
                    for j in range(TPC):
                        t = c * TPC + j
                        bk = bank[4 + (t // 2) % 4] if c < 2 else bank[(t // 2) % 4]
                        last = pe.matmul(bk[:, (t % 2) * D:(t % 2 + 1) * D], gT[:, t * P:(t + 1) * P], b2[:], start=True, stop=True)
                        last.then_inc(biased, 1)

            @block.scalar
            def _(act):
                for c in range(NC):
                    act.wait_ge(turned, c + 1)
                    act.activation(gT[:, c * CH:(c + 1) * CH], bank[c][0:E, :], ACT.Copy).then_inc(copied, 1)

            @block.vector
            def _(dve):
                for t in range(NT):
                    dve.wait_ge(biased, t - t % 2 + 2)
                    bk = bank[4 + (t // 2) % 4] if t < 2 * TPC else bank[(t // 2) % 4]
                    dve.tensor_tensor(X[:, t, :], X[:, t, :], bk[:, (t % 2) * D:(t % 2 + 1) * D], ALU.add)
        experts(K, "l3e", E, N // P, a["L3_ffn_W1"], a["L3_ffn_W2"],
                lambda m, e: b1[:, ds(e, 1), m], ACT.Relu, lambda t, e: gates[:, ds(t, 1), ds(e, 1)].rearrange("p a e -> p (a e)"))


def build(nc, a, first=0, last=7):
    with ExitStack() as ctx:
        K = Shared()
        K.nc, K.a = nc, a
        K.sem = lambda n: ctx.enter_context(nc.semaphore(n))

        def sb(n, shape, dt=F32):
            return ctx.enter_context(nc.sbuf_tensor(n, shape, dt))
        K.X, K.XT, K.CT = sb("X", [P, NT, D]), sb("XT", [P, KD, T]), sb("CT", [P, 2, T])
        K.ident, K.identb, K.ones = sb("ident", [P, P]), sb("identb", [P, P], BF16), sb("ones", [P, P])
        K.round, K.carry = sb("round", [P, 1]), sb("carry", [P, 1])
        K.bank = [ctx.enter_context(nc.psum_tensor(f"bank{i}", [P, CH], F32)) for i in range(8)]
        K.dve_order, K.act_order, K.pool_order = (Order(K.sem(n)) for n in ("dve_order", "act_order", "pool_order"))
        stages = [l0_cosine, l0_ffn, l1_xattn, l1_ffn, l2_xattn, l2_ffn, l3_xattn, l3_ffn]
        start(K)
        for sublayer in stages[first:last + 1]:
            sublayer(K)
        finish(K)


def _t(w):
    import numpy as np
    return np.ascontiguousarray(np.swapaxes(w, -1, -2))


def arrays(inputs):
    import numpy as np
    i = {k: np.asarray(v) for k, v in inputs.items()}
    r = {"x": i["x"], "ctxT": _t(i["ctx_768"].reshape(T, DC))}
    r["L0_xattn_WvT"], r["L0_xattn_WtT"] = _t(i["L0_xattn_Wv"]), _t(i["L0_xattn_Wt"])
    r["L0_xattn_bv"], r["L0_xattn_bt"] = i["L0_xattn_bv"], i["L0_xattn_bt"]
    r["L0_ffn_router_wT"] = _t(i["L0_ffn_router_w"])
    r["L0_ffn_upT"] = _t(np.concatenate([i["L0_ffn_shared_up"], i["L0_ffn_routed_up"]]))
    r["L0_ffn_downT"] = _t(np.concatenate([i["L0_ffn_shared_down"], i["L0_ffn_routed_down"]]))
    for n in ("L1_xattn", "L2_xattn"):
        for w in ("Wq", "Wk", "Wv", "Wo", "bo"):
            r[f"{n}_{w}"] = i[f"{n}_{w}"]
    for w in ("w_gate", "w_up", "w_down"):
        r[f"L1_ffn_{w}T"] = _t(i[f"L1_ffn_{w}"])
    def feature_columns(b):
        return np.moveaxis(b.reshape(b.shape[:-1] + (-1, P)), -1, 0)
    n = "L2_ffn_"
    r[n + "WvT"], r[n + "bv"], r[n + "b2"] = _t(i[n + "Wv"]), feature_columns(i[n + "bv"]), i[n + "b2"]
    r[n + "W1cat"] = np.concatenate([_t(i[n + "Wg"]), _t(i[n + "W1"].reshape(-1, D)), _t(i[n + "Wp"].reshape(-1, D))], axis=1)
    r[n + "b1cat"] = np.concatenate([i[n + "bg"], i[n + "b1"].reshape(-1)])[None]
    r[n + "W2cat"] = _t(i[n + "W2"]).reshape(-1, D)
    r[n + "alpha"] = i[n + "alpha"].reshape(1, 1)
    r[n + "gb"] = np.concatenate([i[n + "g_r"], i[n + "g_c"], i[n + "b_r"], i[n + "b_c"]])[None]
    for w in ("d2v", "img", "txt", "att0", "att1", "f1", "f2"):
        r[f"L3_xattn_W_{w}T"] = _t(i["L3_xattn_W_" + w])
        b = i["L3_xattn_b_" + w]
        r["L3_xattn_b_" + w] = b[None] if w == "f2" else feature_columns(b)
    n = "L3_ffn_"
    for w in ("Wr", "br", "W1", "W2", "b2"):
        r[n + w] = i[n + w]
    r[n + "b1p"] = feature_columns(i[n + "b1"])
    return {k: np.ascontiguousarray(v) for k, v in r.items()}


def kernel(**inputs):
    import concourse.bacc as bacc
    from concourse.bass_utils import run_bass_kernel_spmd
    nc = bacc.Bacc("TRN2", target_bir_lowering=False, num_devices=1)
    data = arrays(inputs)
    aps = {n: nc.dram_tensor("in_" + n, v.shape, mybir.dt.from_np(v.dtype), kind="ExternalInput").ap() for n, v in data.items()}
    aps["out"] = nc.dram_tensor("out_x", (B, S, D), F32, kind="ExternalOutput").ap()
    build(nc, aps)
    r = run_bass_kernel_spmd(nc, [{"in_" + n: v for n, v in data.items()}], core_ids=[0])
    return r.results[0]["out_x"]
```

```python
import concourse.bass as bass
from concourse import mybir
from concourse.alu_op_type import AluOpType as ALU
from contextlib import ExitStack

F32 = mybir.dt.float32
BF16 = mybir.dt.bfloat16
F32R = mybir.dt.float32r
I32 = mybir.dt.int32
ACT = mybir.ActivationFunctionType
AX = mybir.AxisListType.X
ds = bass.ds

P = 128
D = 256
KD = D // P
DC = 192
B, S = 8, 256
T = B * S
NT = T // P
CH = 512
NC = T // CH
TPC = CH // P
HALF_C = DC - P
EXPERTS3, TOP3 = 8, 2
SLOT_TILES = (T * TOP3 + EXPERTS3 * (P - 1)) // P
LN_EPS = 1e-5
COS_EPS = 1e-8
ROUND = 12582912.0
NEG = -1.0e30


class Shared:
    pass


class Order:

    def __init__(self, sem):
        self.sem, self.n, self.loop = sem, 0, None

    def begin(self, index, per_trip):
        self.loop = (index, per_trip, self.n)

    def end(self, trips):
        index, per_trip, base = self.loop
        assert self.n - base == per_trip, (self.n - base, per_trip)
        self.n, self.loop = base + trips * per_trip, None

    def mark(self, ins):
        self.n += 1
        return ins.then_inc(self.sem, 1)

    def wait(self, eng):
        eng.wait_ge(self.sem, self.n if self.loop is None else self.loop[0] * self.loop[1] + self.n)

    def step(self, eng, ins):
        self.mark(ins)
        self.wait(eng)


def stage(emit):
    def scoped(K):
        taken = []

        def take(name):
            taken.append(K.nc.alloc_semaphore(name=name))
            return taken[-1]
        outer, K.sem = K.sem, take
        emit(K)
        K.sem = outer
        K.nc.clear_and_free_semaphores(taken)
        K.nc.all_engine_barrier()
    return scoped


def load_rows(eng, dst, src, sem):
    rows = src.shape[0]
    full = rows // P
    eng.dma_start(dst[:, 0:full, :], src[0:full * P, :].rearrange("(k p) n -> p k n", p=P)).then_inc(sem, 16)
    if rows % P:
        eng.dma_start(dst[0:rows % P, full, :], src[full * P:rows, :]).then_inc(sem, 16)
        return 32
    return 16


def start(K):
    nc, a = K.nc, K.a
    loaded, id0, zero_ok = K.sem("start_loaded"), K.sem("start_ident"), K.sem("start_zero")
    with nc.Block() as block:
        @block.sync
        def _(sp):
            sp.dma_start(K.X[:], a["x"].rearrange("b (h p) d -> p (b h) d", p=P)).then_inc(loaded, 16)
            n = 16 + load_rows(sp, K.CT, a["ctxT"], loaded)
            sp.wait_ge(loaded, n)

            sp.wait_ge(zero_ok, 1)
            sp.dma_start(K.slots.rearrange("(i p) d -> p i d", p=P),
                         K.zero[:].unsqueeze(1).to_broadcast([P, SLOT_TILES, D])).then_inc(K.slots_zeroed, 16)

        @block.vector
        def _(dve):
            dve.memset(K.zero[:], 0.0).then_inc(zero_ok, 1)
            dve.memset(K.CT[HALF_C:P, 1, :], 0.0)

        @block.gpsimd
        def _(pool):
            pool.memset(K.ident[:], 0.0).then_inc(id0, 1)
            pool.memset(K.ones[:], 1.0)
            pool.memset(K.round[:], ROUND)
            pool.wait_ge(id0, 1)
            pool.affine_select(out=K.ident[:], in_=K.ident[:], compare_op=ALU.not_equal, fill=1.0, base=0,
                               pattern=[[-1, P]], channel_multiplier=1).then_inc(id0, 1)
            pool.wait_ge(id0, 2)
            pool.tensor_copy(K.identb[:], K.ident[:])


def finish(K):
    stored = K.sem("stored")
    with K.nc.Block() as block:
        @block.sync
        def _(sp):
            sp.dma_start(K.a["out"].rearrange("b (h p) d -> p (b h) d", p=P), K.X[:]).then_inc(stored, 16)
            sp.wait_ge(stored, 16)


def layernorm(K, name, load=None, quant=None, keep=None):
    nc, X, XT = K.nc, K.X, K.XT
    with ExitStack() as ctx:
        def sb(n, shape, dt=F32):
            return ctx.enter_context(nc.sbuf_tensor(f"{name}_{n}", shape, dt))
        G = TPC
        st = sb("st", [P, NT, 6])
        small = sb("small", [P, 6, NT])
        mean2, dif, var, std, rstd, nmr = (small[:, i, :] for i in range(6))
        xn = sb("xn", [P, G, D])
        if quant:
            XQT, inv127 = quant
            xr = sb("xr", [P, G, D])
            xq = sb("xq", [P, G, D], BF16)
            amax = sb("amax", [P, G])
            scl = sb("scl", [P, G])
            big = sb("big", [P, 1])
        stats, std_ok, coef_ok = K.sem(name + "_stats"), K.sem(name + "_std"), K.sem(name + "_coef")
        xn_ready, t_done, t_read = K.sem(name + "_xn"), K.sem(name + "_tdone"), K.sem(name + "_tread")
        q_ready = K.sem(name + "_q") if quant else None
        kept = None if keep is None else K.sem(name + "_kept")
        with nc.Block() as block:
            if load:
                @block.sync
                def _(sp):
                    load(sp)

            if keep is not None:
                @block.gpsimd
                def _(pool):
                    with pool.Fori(0, NT // G) as g:
                        pool.wait_ge(xn_ready, G * (g + 1))
                        pool.tensor_copy(keep[:, ds(g * G, G), :], xn[:]).then_inc(kept, 1)

            @block.vector
            def _(dve):
                o = K.dve_order
                with dve.Fori(0, NT // G) as g:
                    for j in range(G):
                        dve.bn_stats(st[:, ds(g * G + j, 1), :], X[:, ds(g * G + j, 1), :]).then_inc(stats, 1)
                dve.wait_ge(stats, NT)
                me, mo, ve, vo = st[:, :, 1], st[:, :, 4], st[:, :, 2], st[:, :, 5]
                o.mark(dve.tensor_tensor(mean2, me, mo, ALU.add))
                o.mark(dve.tensor_tensor(dif, me, mo, ALU.subtract))
                o.step(dve, dve.tensor_tensor(var, ve, vo, ALU.add))
                o.mark(dve.tensor_scalar(var, var, 1.0 / D, LN_EPS, ALU.mult, ALU.add))
                o.step(dve, dve.scalar_tensor_tensor(dif, dif, 0.25, dif, ALU.mult, ALU.mult))
                dve.tensor_tensor(var, var, dif, ALU.add).then_inc(coef_ok, 1)
                dve.wait_ge(std_ok, 1)
                o.step(dve, dve.reciprocal(rstd, std))
                dve.scalar_tensor_tensor(nmr, mean2, -0.5, rstd, ALU.mult, ALU.mult).then_inc(coef_ok, 1)
                with dve.Fori(0, NT // G) as g:
                    if quant:
                        o.begin(g, 8)
                        dve.wait_ge(xn_ready, G * (g + 1))
                        o.step(dve, dve.tensor_reduce(amax[:], xn[:], AX, ALU.max, apply_absolute_value=True))
                        o.step(dve, dve.tensor_scalar(amax[:], amax[:], 1e-5, 1.0 / 127.0, ALU.max, ALU.mult))
                        o.mark(dve.tensor_copy(inv127[:, ds(g * G, G)], amax[:]))
                        o.step(dve, dve.reciprocal(scl[:], amax[:]))
                        for j in range(G):
                            o.mark(dve.tensor_scalar(xr[:, j, :], xn[:, j, :], scl[:, j:j + 1], ROUND, ALU.mult, ALU.add))
                        o.wait(dve)
                        dve.wait_ge(t_done, KD * g)
                        dve.tensor_scalar(xq[:], xr[:], ROUND, None, ALU.subtract).then_inc(q_ready, 1)
                        o.end(NT // G)
                    else:
                        for k in range(KD):
                            dve.wait_ge(t_done, KD * g + k + 1)
                            dve.tensor_copy(XT[:, k, ds(g * CH, CH)], K.bank[k][:]).then_inc(t_read, 1)

            @block.scalar
            def _(act):
                act.wait_ge(coef_ok, 1)
                act.activation(std, var, ACT.Sqrt).then_inc(std_ok, 1)
                act.wait_ge(coef_ok, 2)
                with act.Fori(0, NT // G) as g:
                    act.wait_ge(q_ready, g) if quant else act.wait_ge(t_done, KD * g)
                    if keep is not None:
                        act.wait_ge(kept, g)
                    for j in range(G):
                        act.activation(xn[:, j, :], X[:, ds(g * G + j, 1), :], ACT.Identity,
                                       bias=nmr[:, ds(g * G + j, 1)], scale=rstd[:, ds(g * G + j, 1)]).then_inc(xn_ready, 1)
                    if quant:
                        for k in range(KD):
                            act.wait_ge(t_done, KD * g + k + 1)
                            act.activation(XQT[:, k, ds(g * CH, CH)], K.bank[k][:, 0:CH // 2].bitcast(BF16), ACT.Copy).then_inc(t_read, 1)

            @block.tensor
            def _(pe):
                src, ident = (xq, K.identb) if quant else (xn, K.ident)
                with pe.Fori(0, NT // G) as g:
                    if quant:
                        pe.wait_ge(q_ready, g + 1)
                    else:
                        pe.wait_ge(xn_ready, G * (g + 1))
                    pe.wait_ge(t_read, KD * g)
                    for k in range(KD):
                        out = K.bank[k][:, 0:CH // 2].bitcast(BF16) if quant else K.bank[k][:]
                        for j in range(G):
                            last = pe.transpose(out[:, j * P:(j + 1) * P], src[:, j, k * P:(k + 1) * P], ident[:])
                        last.then_inc(t_done, 1)


@stage
def l0_cosine(K):
    nc, a, X, XT, CT, bank = K.nc, K.a, K.X, K.XT, K.CT, K.bank
    HV = 128
    with ExitStack() as ctx:
        def sb(n, shape, dt=F32):
            return ctx.enter_context(nc.sbuf_tensor("l0x_" + n, shape, dt))
        wv, wt, bv, bt = sb("wv", [P, KD, HV]), sb("wt", [P, 2, HV]), sb("bv", [P, 1]), sb("bt", [P, 1])
        vT, tT, sq = sb("vT", [P, CH]), sb("tT", [P, CH]), sb("sq", [P, 2, CH])
        norm, rn, lim, cos = sb("norm", [P, 2 * TPC]), sb("rn", [P, 2 * TPC]), sb("lim", [P, TPC, S]), sb("cos", [P, TPC, S])
        loaded = K.sem("l0x_loaded")

        def load(sp):
            load_rows(sp, wv, a["L0_xattn_WvT"], loaded)
            load_rows(sp, wt, a["L0_xattn_WtT"], loaded)
            sp.dma_start(bv[:], a["L0_xattn_bv"].rearrange("(p a) -> p a", a=1)).then_inc(loaded, 16)
            sp.dma_start(bt[:], a["L0_xattn_bt"].rearrange("(p a) -> p a", a=1)).then_inc(loaded, 16)
            sp.wait_ge(loaded, 80)
        layernorm(K, "ln0x", load)

        proj, sides, norms, roots, recips, dots, added = (
            K.sem("l0x_" + n) for n in ("proj", "sides", "norms", "roots", "recips", "dots", "added"))
        with nc.Block() as block:
            @block.tensor
            def _(pe):
                with pe.Fori(0, NC) as c:
                    pe.wait_ge(sides, 4 * c)
                    for k in range(KD):
                        pe.matmul(bank[0][:], wv[:, k, :], XT[:, k, ds(c * CH, CH)], start=k == 0, stop=k == 1)
                    pe.matmul(bank[1][:], wt[:, 0, :], CT[:, 0, ds(c * CH, CH)], start=True, stop=False)
                    pe.matmul(bank[1][:], wt[0:HALF_C, 1, :], CT[0:HALF_C, 1, ds(c * CH, CH)], start=False,
                              stop=True).then_inc(proj, 1)
                    pe.wait_ge(sides, 4 * c + 4)
                    for s in range(2):
                        for j in range(TPC):
                            n = s * TPC + j
                            last = pe.matmul(bank[2][:, n:n + 1], sq[:, s, j * P:(j + 1) * P], K.ones[:, 0:1], start=True, stop=True)
                    last.then_inc(norms, 1)
                    pe.wait_ge(recips, c + 1)
                    pe.wait_ge(added, TPC * c)
                    for j in range(TPC):
                        pe.matmul(bank[3][:, j * P:(j + 1) * P], rn[:, TPC + j:TPC + j + 1].to_broadcast([P, P]),
                                  K.ident[:], start=True, stop=True)
                    for j in range(TPC):
                        b, i = j // 2, j % 2
                        last = pe.matmul(bank[4 + b][:, i * S:(i + 1) * S], vT[:, j * P:(j + 1) * P],
                                         tT[:, b * S:(b + 1) * S], start=True, stop=True)
                    last.then_inc(dots, 1)

            @block.scalar
            def _(act):
                with act.Fori(0, NC) as c:
                    act.wait_ge(proj, c + 1)
                    act.wait_ge(dots, c)
                    act.activation(sq[:, 0, :], bank[0][:], ACT.Square, bias=bv[:]).then_inc(sides, 1)
                    act.activation(sq[:, 1, :], bank[1][:], ACT.Square, bias=bt[:]).then_inc(sides, 1)
                    act.activation(vT[:], bank[0][:], ACT.Identity, bias=bv[:]).then_inc(sides, 1)
                    act.activation(tT[:], bank[1][:], ACT.Identity, bias=bt[:]).then_inc(sides, 1)
                    act.wait_ge(norms, c + 1)
                    act.activation(norm[:], bank[2][:, 0:2 * TPC], ACT.Sqrt).then_inc(roots, 1)

            @block.vector
            def _(dve):
                o = K.dve_order
                with dve.Fori(0, NC) as c:
                    o.begin(c, 2 * TPC)
                    dve.wait_ge(roots, c + 1)
                    dve.reciprocal(rn[:], norm[:]).then_inc(recips, 1)
                    dve.wait_ge(dots, c + 1)
                    for j in range(TPC):
                        b = j // 2
                        o.mark(dve.tensor_scalar(lim[:, j, :], bank[3][:, b * S:(b + 1) * S], rn[:, j:j + 1],
                                                 1.0 / COS_EPS, ALU.mult, ALU.min))
                    o.wait(dve)
                    for j in range(TPC):
                        b, i = j // 2, j % 2
                        o.mark(dve.tensor_tensor(cos[:, j, :], bank[4 + b][:, i * S:(i + 1) * S], lim[:, j, :], ALU.mult))
                    o.wait(dve)
                    for j in range(TPC):
                        xt = X[:, ds(c * TPC + j, 1), :]
                        dve.tensor_tensor(xt, xt, cos[:, j:j + 1, :], ALU.add).then_inc(added, 1)
                    o.end(NC)


def select_top(K, dve, o, vals, top, rep, mask, E, k):
    n = vals.shape[1]
    o.mark(dve.memset(K.carry[:], 0.0))
    for t in range(n):
        o.mark(dve.max(top[:, t, :], vals[:, t, :]))
    o.wait(dve)
    o.step(dve, dve.memset(top[:, :, k:8], NEG))
    o.mark(dve.memset(K.carry[:], 0.0))
    for t in range(n):
        o.mark(dve.match_replace(out=rep[:, t, :], in_to_replace=top[:, t, :], in_values=vals[:, t, :], imm_value=2 * NEG))
    o.wait(dve)
    o.step(dve, dve.tensor_tensor(mask, vals[:, :, 0:E], rep[:, :, 0:E], ALU.is_gt))


def router(K, name, E, k, w, bias, gates, mask, over_all, split=None):
    nc, XT, bank = K.nc, K.XT, K.bank
    with ExitStack() as ctx:
        def sb(n, shape, dt=F32):
            return ctx.enter_context(nc.sbuf_tensor(f"{name}_{n}", shape, dt))
        W = E + 8 - k
        lg, vals, top, rep = sb("lg", [P, NT, E]), sb("vals", [P, NT, W]), sb("top", [P, NT, 8]), sb("rep", [P, NT, W])
        ex, mx, sm = sb("ex", [P, NT, E]), sb("mx", [P, NT, 1]), sb("sm", [P, NT, 1])
        if mask is None:
            mask = sb("mask", [P, NT, E])[:]
        logits, sh, xp, hi = (K.sem(f"{name}_{n}") for n in ("logits", "shifted", "exp", "hi"))
        with nc.Block() as block:
            @block.tensor
            def _(pe):
                for t in range(NT):
                    for kk in range(KD):
                        last = pe.matmul(bank[0][:, t * E:(t + 1) * E], XT[:, kk, t * P:(t + 1) * P], w[:, kk, :], start=kk == 0, stop=kk == 1)
                last.then_inc(logits, 1)

            @block.scalar
            def _(act):
                if split:
                    for kk in range(KD):
                        act.activation(split[0][:, kk, :], XT[:, kk, :], ACT.Copy).then_inc(hi, 1)
                act.wait_ge(sh, 1)
                act.activation(ex[:], ex[:], ACT.Exp).then_inc(xp, 1)

            if split:
                @block.gpsimd
                def _(pool):
                    for kk in range(KD):
                        pool.wait_ge(hi, kk + 1)
                        pool.tensor_tensor(split[1][:, kk, :], XT[:, kk, :], split[0][:, kk, :].bitcast(F32), ALU.subtract)

            @block.vector
            def _(dve):
                o = K.dve_order
                every = [P, NT, E]
                o.mark(dve.memset(vals[:, :, E:W], NEG))
                dve.wait_ge(logits, 1)
                raw = bank[0][:, 0:NT * E].rearrange("p (t e) -> p t e", e=E)
                if bias is None:
                    o.step(dve, dve.tensor_copy(lg[:], raw))
                else:
                    o.step(dve, dve.tensor_tensor(lg[:], raw, bias.unsqueeze(1).to_broadcast(every), ALU.add))
                o.step(dve, dve.tensor_reduce(mx[:], lg[:], AX, ALU.max))
                dve.tensor_tensor(ex[:], lg[:], mx[:].to_broadcast(every), ALU.subtract).then_inc(sh, 1)
                if over_all:
                    dve.wait_ge(xp, 1)
                    o.step(dve, dve.tensor_reduce(sm[:], ex[:], AX, ALU.add))
                    o.step(dve, dve.reciprocal(sm[:], sm[:]))
                    o.step(dve, dve.tensor_tensor(vals[:, :, 0:E], ex[:], sm[:].to_broadcast(every), ALU.mult))
                    select_top(K, dve, o, vals, top, rep, mask, E, k)
                    dve.tensor_tensor(gates, vals[:, :, 0:E], mask, ALU.mult)
                else:
                    o.step(dve, dve.tensor_copy(vals[:, :, 0:E], lg[:]))
                    select_top(K, dve, o, vals, top, rep, mask, E, k)
                    dve.wait_ge(xp, 1)
                    o.step(dve, dve.tensor_tensor(ex[:], ex[:], mask, ALU.mult))
                    o.step(dve, dve.tensor_reduce(sm[:], ex[:], AX, ALU.add))
                    o.step(dve, dve.reciprocal(sm[:], sm[:]))
                    dve.tensor_tensor(gates, ex[:], sm[:].to_broadcast(every), ALU.mult)


def small_experts(K, name, E, XH, XL, up, down, gates):
    nc, X, bank = K.nc, K.X, K.bank
    YB = bank[4:8]
    with ExitStack() as ctx:
        def sb(n, shape, dt=F32):
            return ctx.enter_context(nc.sbuf_tensor(f"{name}_{n}", shape, dt))
        wu, wd = [sb(f"wu{s}", [P, D]) for s in range(2)], [sb(f"wd{s}", [P, D]) for s in range(2)]
        wu_r = [[sb(f"wu{part}{s}", [P, D], F32R) for part in ("hi", "lo")] for s in range(2)]
        wd_r = [[sb(f"wd{part}{s}", [P, D], F32R) for part in ("hi", "lo")] for s in range(2)]
        h, h_hi, h_lo = sb("h", [P, 2, CH]), sb("hhi", [P, 2, CH], F32R), sb("hlo", [P, 2, CH], F32R)
        up_done, gelu_done, hi_done, lo_done, y_done, added, w_hi, w_ok = (
            K.sem(f"{name}_{n}") for n in ("updone", "gelu", "hi", "lo", "ydone", "added", "whi", "wok"))
        loaded = [K.sem(f"{name}_loaded{s}") for s in range(2)]

        def units(eng, body, lead=None):
            if lead:
                lead(0, 0, 0, 0)

            def pair_of(pair, last):
                for i in range(2 * NC):
                    s, c = divmod(i, NC)
                    if lead and not (last and i == 2 * NC - 1):
                        s1, c1 = divmod((i + 1) % (2 * NC), NC)
                        lead(pair + (i + 1) // (2 * NC), s1, c1, pair * (2 * NC) + i + 1)
                    body(pair, s, c, pair * (2 * NC) + i)
            with eng.Fori(0, E // 2 - 1) as pair:
                pair_of(pair, False)
            pair_of(E // 2 - 1, True)

        with nc.Block() as block:
            @block.sync
            def _(sp):
                def load(e, s):
                    sp.dma_start(wu[s][:].rearrange("p (k n) -> p k n", k=KD), up[ds(e, 1), :, :].rearrange("e (k p) n -> p (e k) n", p=P)).then_inc(loaded[s], 16)
                    sp.dma_start(wd[s][:], down[ds(e, 1), :, :].rearrange("e p n -> p (e n)")).then_inc(loaded[s], 16)
                for s in range(2):
                    load(s, s)
                with sp.Fori(0, E // 2 - 1) as pair:
                    for s in range(2):
                        sp.wait_ge(w_ok, 2 * (pair * 2 + s + 1))
                        load(pair * 2 + 2 + s, s)

            @block.gpsimd
            def _(pool):
                pool.sem_inc(y_done, 2)

                def split(pair, s):
                    e = pair * 2 + s
                    pool.wait_ge(loaded[s], 32 * (pair + 1))
                    if not isinstance(pair, int) or pair > 0:
                        pool.wait_ge(y_done, NC * (e - 1) + 2)
                    pool.tensor_tensor(wu_r[s][0][:], wu[s][:], K.zero[:], ALU.add).then_inc(w_hi, 1)
                    pool.tensor_tensor(wd_r[s][0][:], wd[s][:], K.zero[:], ALU.add).then_inc(w_hi, 1)
                    pool.wait_ge(w_hi, 2 * (e + 1))
                    pool.tensor_tensor(wu_r[s][1][:], wu[s][:], wu_r[s][0][:].bitcast(F32), ALU.subtract).then_inc(w_ok, 1)
                    pool.tensor_tensor(wd_r[s][1][:], wd[s][:], wd_r[s][0][:].bitcast(F32), ALU.subtract).then_inc(w_ok, 1)
                for s in range(2):
                    split(0, s)
                with pool.Fori(1, E // 2) as pair:
                    for s in range(2):
                        split(pair, s)

            @block.tensor
            def _(pe):
                def hidden(pair, s, c, n):
                    if c == 0:
                        pe.wait_ge(w_ok, 2 * (pair * 2 + s + 1))
                    pe.wait_ge(gelu_done, n + 1)
                    terms = [(w, x, k) for w, x in ((0, XH), (1, XH), (0, XL)) for k in range(KD)]
                    for i, (w, x, k) in enumerate(terms):
                        last = pe.matmul(bank[c % 2][:], wu_r[s][w][:, k * P:(k + 1) * P], x[:, k, c * CH:(c + 1) * CH],
                                         start=i == 0, stop=i == len(terms) - 1)
                    last.then_inc(up_done, 1)

                def outputs(pair, s, c, n):
                    pe.wait_ge(added, TPC * (n + 1))
                    pe.wait_ge(hi_done, n + 1)
                    pe.wait_ge(lo_done, n + 3)
                    for j in range(TPC):
                        y = YB[c % 2 * 2 + j // 2][:, j % 2 * D:(j % 2 + 1) * D]
                        w = slice(j * P, (j + 1) * P)
                        pe.matmul(y, h_hi[:, c % 2, w], wd_r[s][0][:], start=True, stop=False)
                        pe.matmul(y, h_hi[:, c % 2, w], wd_r[s][1][:], start=False, stop=False)
                        last = pe.matmul(y, h_lo[:, c % 2, w], wd_r[s][0][:], start=False, stop=True)
                    last.then_inc(y_done, 1)
                units(pe, outputs, hidden)

            @block.scalar
            def _(act):
                act.sem_inc(gelu_done, 2)

                def body(pair, s, c, n):
                    act.wait_ge(up_done, n + 1)
                    act.wait_ge(lo_done, n + 1)
                    act.activation(h[:, c % 2, :], bank[c % 2][:], ACT.Gelu).then_inc(gelu_done, 1)
                    act.wait_ge(gelu_done, n + 3)
                    act.wait_ge(y_done, n + 1)
                    act.activation(h_hi[:, c % 2, :], h[:, c % 2, :], ACT.Copy).then_inc(hi_done, 1)
                units(act, body)

            @block.vector
            def _(dve):
                dve.sem_inc(added, 2 * TPC)
                dve.sem_inc(lo_done, 2)

                def rest(pair, s, c, n):
                    dve.wait_ge(hi_done, n + 1)
                    dve.wait_ge(y_done, n + 1)
                    dve.tensor_tensor(h_lo[:, c % 2, :], h[:, c % 2, :], h_hi[:, c % 2, :].bitcast(F32), ALU.subtract).then_inc(lo_done, 1)

                def add(pair, s, c, n):
                    dve.wait_ge(y_done, n + 3)
                    dve.wait_ge(added, TPC * (n + 1))
                    for j in range(TPC):
                        t = c * TPC + j
                        dve.scalar_tensor_tensor(X[:, t, :], YB[c % 2 * 2 + j // 2][:, j % 2 * D:(j % 2 + 1) * D], gates(t, pair * 2 + s), X[:, t, :],
                                                 ALU.mult, ALU.add).then_inc(added, 1)
                units(dve, add, rest)


@stage
def l0_ffn(K):
    nc, a = K.nc, K.a
    E, NS = 16, 2
    with ExitStack() as ctx:
        w = ctx.enter_context(nc.sbuf_tensor("l0f_wr", [P, KD, E], F32))
        gates = ctx.enter_context(nc.sbuf_tensor("l0f_gates", [P, NT, NS + E], F32))
        XH, XL = (ctx.enter_context(nc.sbuf_tensor("l0f_" + n, [P, KD, T], F32R)) for n in ("xh", "xl"))
        loaded = K.sem("l0f_loaded")

        def load(sp):
            load_rows(sp, w, a["L0_ffn_router_wT"], loaded)
            sp.wait_ge(loaded, 16)
        layernorm(K, "ln0f", load)
        with nc.Block() as block:
            @block.gpsimd
            def _(pool):
                pool.memset(gates[:, :, 0:NS], 1.0)
        router(K, "l0r", E, 4, w, None, gates[:, :, NS:NS + E], None, True, split=(XH, XL))
        small_experts(K, "l0e", NS + E, XH, XL, a["L0_ffn_upT"], a["L0_ffn_downT"],
                      lambda t, e: gates[:, t, ds(e, 1)])


def cross_attention(K, name, H, wq_d, wk_d, wv_d, wo_d, bo_d):
    nc, a, X, XT, CT, bank = K.nc, K.a, K.X, K.XT, K.CT, K.bank
    DH = 64
    HP, G, QT = H // 2, H // 8, S // P
    Q = HP + 2 * G
    R = 2 * G + 1
    sc, tp, ob, pj = bank[0:2], bank[2:4], bank[4:6], bank[6:8]
    with ExitStack() as ctx:
        def sb(n, shape, dt=F32):
            return ctx.enter_context(nc.sbuf_tensor(f"{name}_{n}", shape, dt))
        wq, wk, wv = sb("wq", [P, KD, H * DH]), sb("wk", [P, 2, H * DH]), sb("wv", [P, 2, H * DH])
        wo, bo = sb("wo", [P, HP, D]), sb("bo", [P, D])
        ctb = sb("ctb", [P, 2, S])
        qk = sb("qk", [P, HP, 3 * S])
        v = sb("v", [P, 2, H * DH])
        nmax = sb("nmax", [P, 2, QT])
        pr = sb("pr", [P, 2, QT, S])
        pt = sb("pt", [P, 2, 2 * S])
        sums, rsum = sb("sums", [P, QT, H]), sb("rsum", [P, QT, 8])
        o, oT, tmp = sb("o", [P, QT, H * DH]), sb("oT", [P, QT, HP, P]), sb("tmp", [P, QT, D])
        loaded = K.sem(name + "_loaded")

        def load(sp):
            n = load_rows(sp, wq, wq_d, loaded) + load_rows(sp, wk, wk_d, loaded) + load_rows(sp, wv, wv_d, loaded)
            n += load_rows(sp, wo, wo_d, loaded)
            sp.dma_start(bo[:], bo_d.rearrange("(a n) -> a n", a=1).partition_broadcast(P)).then_inc(loaded, 16)
            sp.wait_ge(loaded, n + 16)
        layernorm(K, name + "_ln", load)

        ctb_ready, pj_done, pj_read = (K.sem(f"{name}_{x}") for x in ("ctb", "pjdone", "pjread"))
        s_done, max_done, exp_done, t_done, pt_ready, pv_done = (
            K.sem(f"{name}_{x}") for x in ("sdone", "maxdone", "expdone", "tdone", "ptready", "pvdone"))
        o_ready = [K.sem(f"{name}_oready{q}") for q in range(QT)]
        o_read = [K.sem(f"{name}_oread{q}") for q in range(QT)]
        rs_done, zeroed = K.sem(name + "_rsdone"), K.sem(name + "_zeroed")
        EC, RC = 2, G - 1

        def schedule(eng, qkp, vp, main, drain, tail, order=None, per_trip=0):
            qkp(0)
            vp(0)
            with eng.Fori(0, B - 1) as b:
                if order:
                    order.begin(b, per_trip)
                main(b), qkp(b + 1), drain(b), vp(b + 1), tail(b)
                if order:
                    order.end(B - 1)
            main(B - 1), drain(B - 1), tail(B - 1)

        def nothing(b):
            pass

        with nc.Block() as block:
            @block.gpsimd
            def _(pool):
                def copy_context(b):
                    pool.wait_ge(pj_done, Q * b)
                    pool.tensor_copy(ctb[:], CT[:, :, ds(b * S, S)]).then_inc(ctb_ready, 1)
                with pool.Fori(0, B) as b:
                    copy_context(b)

            @block.tensor
            def _(pe):
                def qk_products(b):
                    pe.wait_ge(ctb_ready, b + 1)
                    for p in range(HP):
                        pe.wait_ge(pj_read, b * Q + p)
                        t, w = pj[p % 2], slice(p * P, (p + 1) * P)
                        for k in range(KD):
                            pe.matmul(t[:, 0:S], wq[:, k, w], XT[:, k, ds(b * S, S)], start=k == 0, stop=k == KD - 1)
                        pe.matmul(t[:, S:2 * S], wk[:, 0, w], ctb[:, 0, :], start=True, stop=False)
                        pe.matmul(t[:, S:2 * S], wk[:, 1, w], ctb[:, 1, :], start=False, stop=True).then_inc(pj_done, 1)

                def v_products(b):
                    for u in range(2 * G):
                        kt, g = u % 2, u // 2
                        n = HP + u
                        pe.wait_ge(pj_read, b * Q + n)
                        t, w = pj[n % 2], slice(g * CH, (g + 1) * CH)
                        pe.matmul(t[:], ctb[:, 0, kt * P:(kt + 1) * P], wv[:, 0, w], start=True, stop=False)
                        pe.matmul(t[:], ctb[:, 1, kt * P:(kt + 1) * P], wv[:, 1, w], start=False,
                                  stop=True).then_inc(pj_done, 1)

                def scores(b, h):
                    n = b * H + h
                    pe.wait_ge(pj_read, b * Q + h // 2 + 2)
                    pe.wait_ge(exp_done, 2 * n)
                    for q in range(QT):
                        last = pe.matmul(sc[h % 2][:, q * S:(q + 1) * S], qk[:, h // 2, (h % 2) * S + q * P:(h % 2) * S + (q + 1) * P],
                                         qk[:, h // 2, 2 * S:3 * S], start=True, stop=True)
                    last.then_inc(s_done, 1)

                def turn(b, h):
                    n = b * H + h
                    pe.wait_ge(exp_done, 2 * (n + 1) + EC)
                    pe.wait_ge(pt_ready, n)
                    for kt in range(2):
                        for q in range(QT):
                            c = (kt * QT + q) * P
                            last = pe.transpose(tp[h % 2][:, c:c + P], pr[:, h % 2, q, kt * P:(kt + 1) * P], K.ident[:])
                    last.then_inc(t_done, 1)

                def values(b, h):
                    n = b * H + h
                    g = h // 8
                    pe.wait_ge(pt_ready, n + 2)
                    if h == 0:
                        pe.wait_ge(pj_read, (b + 1) * Q + 1)
                    for q in range(QT):
                        if h % 8 == 0:
                            pe.wait_ge(o_read[q], b * R + g)
                        for kt in range(2):
                            c = (kt * QT + q) * P
                            last = pe.matmul(ob[q][:, (h % 8) * DH:(h % 8 + 1) * DH], pt[:, h % 2, c:c + P],
                                             v[:, kt, h * DH:(h + 1) * DH], start=kt == 0, stop=kt == 1)
                    last.then_inc(pv_done, 1)

                def main(b):
                    for h in range(H):
                        scores(b, h)
                        if h >= 1:
                            turn(b, h - 1)
                        if h >= 2:
                            values(b, h - 2)

                def drain(b):
                    turn(b, H - 1)
                    values(b, H - 2)
                    values(b, H - 1)

                def tail(b):
                    for g in range(G):
                        for q in range(QT):
                            pe.wait_ge(o_read[q], b * R + G + g)
                            for i in range(4):
                                last = pe.transpose(ob[q][:, i * P:(i + 1) * P], o[:, q, (g * 4 + i) * P:(g * 4 + i + 1) * P], K.ident[:])
                            last.then_inc(o_ready[q], 1)
                    for q in range(QT):
                        pe.wait_ge(o_read[q], b * R + 2 * G)
                        for p in range(HP):
                            last = pe.matmul(ob[q][:, 0:D], oT[:, q, p, :], wo[:, p, :], start=p == 0, stop=p == HP - 1)
                        last.then_inc(o_ready[q], 1)
                pe.wait_ge(zeroed, 4)
                schedule(pe, qk_products, v_products, main, drain, tail)

            @block.scalar
            def _(act):
                act.sem_inc(pj_read, 1)
                act.sem_inc(exp_done, EC)

                def copy_qk(b):
                    act.wait_ge(s_done, H * b)
                    for p in range(HP):
                        act.wait_ge(pj_done, b * Q + p + 1)
                        for i in range(2):
                            r = slice(i * DH, (i + 1) * DH)
                            act.activation(qk[r, p, i * S:(i + 1) * S], pj[p % 2][r, 0:S], ACT.Copy, scale=DH ** -0.5)
                        act.activation(qk[:, p, 2 * S:3 * S], pj[p % 2][:, S:2 * S], ACT.Copy).then_inc(pj_read, 1)

                def copy_v(b):
                    act.wait_ge(pv_done, H * b + 1)
                    for u in range(2 * G):
                        n = HP + u
                        act.wait_ge(pj_done, b * Q + n + 1)
                        act.activation(v[:, u % 2, (u // 2) * CH:(u // 2 + 1) * CH], pj[n % 2][:], ACT.Copy).then_inc(pj_read, 1)

                def main(b):
                    for h in range(H):
                        n = b * H + h
                        act.wait_ge(max_done, n + 1)
                        act.wait_ge(t_done, n)
                        if h % 8 == 0:
                            act.wait_ge(rs_done, b * G + h // 8)
                        for q in range(QT):
                            act.activation(pr[:, h % 2, q, :], sc[h % 2][:, q * S:(q + 1) * S], ACT.Exp, bias=nmax[:, h % 2, q:q + 1],
                                           accum_out=sums[:, q, h:h + 1]).then_inc(exp_done, 1)
                schedule(act, copy_qk, copy_v, main, nothing, nothing)

            @block.vector
            def _(dve):
                order = K.dve_order
                dve.memset(wk[HALF_C:P, 1, :], 0.0).then_inc(zeroed, 1)
                dve.memset(wv[HALF_C:P, 1, :], 0.0).then_inc(zeroed, 1)
                for i in range(2):
                    other = slice((1 - i) * DH, (2 - i) * DH)
                    dve.memset(qk[other, :, i * S:(i + 1) * S], 0.0).then_inc(zeroed, 1)
                dve.sem_inc(pt_ready, 1)
                dve.sem_inc(t_done, 1)
                dve.sem_inc(pv_done, 1)
                if RC:
                    dve.sem_inc(rs_done, RC)

                def maximum(b, h):
                    n = b * H + h
                    dve.wait_ge(s_done, n + 1)
                    dve.wait_ge(exp_done, 2 * n)
                    dve.tensor_reduce(nmax[:, h % 2, :], sc[h % 2][:].rearrange("p (q s) -> p q s", q=QT), AX, ALU.max,
                                      negate=True).then_inc(max_done, 1)

                def copy_turned(b, h):
                    n = b * H + h
                    dve.wait_ge(t_done, n + 2)
                    dve.wait_ge(pv_done, n)
                    dve.tensor_copy(pt[:, h % 2, :], tp[h % 2][:]).then_inc(pt_ready, 1)

                def normalise(b, g):
                    dve.wait_ge(pv_done, b * H + 8 * (g + 1) + 1)
                    dve.wait_ge(o_read[QT - 1], b * R + g)
                    dve.reciprocal(rsum[:], sums[:, :, g * 8:(g + 1) * 8]).then_inc(rs_done, 1)
                    dve.wait_ge(rs_done, b * G + g + 1 + RC)
                    for q in range(QT):
                        dve.tensor_tensor(o[:, q, g * CH:(g + 1) * CH].rearrange("p (h d) -> p h d", d=DH),
                                          ob[q][:].rearrange("p (h d) -> p h d", d=DH),
                                          rsum[:, q, :].unsqueeze(2).to_broadcast([P, 8, DH]), ALU.mult).then_inc(o_read[q], 1)

                def main(b):
                    for h in range(H):
                        maximum(b, h)
                        if h >= 1:
                            copy_turned(b, h - 1)
                        if h >= 2 and (h - 2) % 8 == 7:
                            normalise(b, (h - 2) // 8)

                def drain(b):
                    copy_turned(b, H - 1)
                    normalise(b, G - 1)

                def tail(b):
                    for g in range(G):
                        for q in range(QT):
                            dve.wait_ge(o_ready[q], b * (G + 1) + g + 1)
                            dve.tensor_copy(oT[:, q, g * 4:(g + 1) * 4, :], ob[q][:].rearrange("p (i n) -> p i n", i=4)).then_inc(o_read[q], 1)
                    for q in range(QT):
                        dve.wait_ge(o_ready[q], b * (G + 1) + G + 1)
                        dve.tensor_tensor(tmp[:, q, :], ob[q][:, 0:D], bo[:], ALU.add).then_inc(o_read[q], 1)
                    for q in range(QT):
                        dve.wait_ge(o_read[q], (b + 1) * R)
                        xt = X[:, ds(b * QT + q, 1), :]
                        dve.tensor_tensor(xt, xt, tmp[:, q:q + 1, :], ALU.add)
                schedule(dve, nothing, nothing, main, drain, tail)


def l1_xattn(K):
    a = K.a
    cross_attention(K, "l1x", 16, a["L1_xattn_Wq"], a["L1_xattn_Wk"], a["L1_xattn_Wv"], a["L1_xattn_Wo"], a["L1_xattn_bo"])


def l2_xattn(K):
    a = K.a
    cross_attention(K, "l2x", 8, a["L2_xattn_Wq"], a["L2_xattn_Wk"], a["L2_xattn_Wv"], a["L2_xattn_Wo"], a["L2_xattn_bo"])


def ternary(K, name, weights, ones_bank=None):
    nc = K.nc
    with ExitStack() as ctx:
        n_w = len(weights)
        asum = ctx.enter_context(nc.sbuf_tensor(name + "_asum", [P, n_w], F32))
        thr = ctx.enter_context(nc.sbuf_tensor(name + "_thr", [P, 2, n_w], F32))
        below = [ctx.enter_context(nc.sbuf_tensor(f"{name}_below{i}", list(w.shape), BF16)) for i, (w, _, _, _) in enumerate(weights)]
        summed, total, ready = K.sem(name + "_summed"), K.sem(name + "_total"), K.sem(name + "_thr")
        loaded = [K.sem(f"{name}_loaded{i}") for i in range(n_w)]
        with nc.Block() as block:
            @block.sync
            def _(sp):
                for i, (w, src, _, _) in enumerate(weights):
                    load_rows(sp, w, src, loaded[i])

            @block.vector
            def _(dve):
                o = K.dve_order
                o.step(dve, dve.memset(asum[:], 0.0))
                for i, (w, src, _, _) in enumerate(weights):
                    rows = src.shape[0]
                    dve.wait_ge(loaded[i], 16 * (1 + (rows % P > 0)))
                    if rows % P == 0:
                        o.mark(dve.tensor_reduce(asum[:, i:i + 1], w[:].rearrange("p k n -> p (k n)"), AX, ALU.add, apply_absolute_value=True))
                    else:
                        o.step(dve, dve.tensor_reduce(asum[:, i:i + 1], w[:, 0, :], AX, ALU.add, apply_absolute_value=True))
                        o.step(dve, dve.tensor_reduce(thr[0:rows - P, 0, i:i + 1], w[0:rows - P, 1, :], AX, ALU.add, apply_absolute_value=True))
                        o.mark(dve.tensor_tensor(asum[0:rows - P, i:i + 1], asum[0:rows - P, i:i + 1], thr[0:rows - P, 0, i:i + 1], ALU.add))
                o.wait(dve)
                dve.sem_inc(summed, 1)
                dve.wait_ge(total, 1)
                for i, (w, src, _, scale) in enumerate(weights):
                    count = src.shape[0] * src.shape[1]
                    o.mark(dve.tensor_scalar(scale, K.bank[0][:, i:i + 1], 1.0 / count, 1e-5, ALU.mult, ALU.max))
                o.wait(dve)
                for i, (_, _, _, scale) in enumerate(weights):
                    o.mark(dve.tensor_scalar(thr[:, 0, i:i + 1], scale, 0.5, None, ALU.mult))
                    o.mark(dve.tensor_scalar(thr[:, 1, i:i + 1], scale, -0.5, None, ALU.mult))
                o.wait(dve)
                for i, (w, src, q, _) in enumerate(weights):
                    for r, ks in row_parts(src.shape[0]):
                        o.mark(dve.tensor_scalar(below[i][r, ks, :], w[r, ks, :], thr[r, 1, i:i + 1], None, ALU.is_lt))
                o.wait(dve)
                for i, (w, src, q, _) in enumerate(weights):
                    for r, ks in row_parts(src.shape[0]):
                        flat = "p k n -> p (k n)"
                        dve.scalar_tensor_tensor(q[r, ks, :].rearrange(flat), w[r, ks, :].rearrange(flat), thr[r, 0, i:i + 1],
                                                 below[i][r, ks, :].rearrange(flat), ALU.is_gt, ALU.subtract)

            @block.tensor
            def _(pe):
                pe.wait_ge(summed, 1)
                pe.matmul(K.bank[0][:, 0:n_w], K.ones[:], asum[:], start=True, stop=True).then_inc(total, 1)


def row_parts(rows):
    full = rows // P
    parts = [(slice(0, P), slice(0, full))]
    return parts + ([(slice(0, rows % P), slice(full, full + 1))] if rows % P else [])


@stage
def l1_ffn(K):
    nc, a, X, bank = K.nc, K.a, K.X, K.bank
    N = 1024
    KN = N // P
    with ExitStack() as ctx:
        def sb(n, shape, dt=F32):
            return ctx.enter_context(nc.sbuf_tensor("l1f_" + n, shape, dt))
        qg, qu, qd = sb("qg", [P, KD, N], BF16), sb("qu", [P, KD, N], BF16), sb("qd", [P, KN, D], BF16)
        scale = sb("scale", [P, 3])
        XQ, inv = sb("xq_t", [P, KD, T], BF16), sb("inv", [P, NT])
        with ExitStack() as wctx:
            wg, wu, wd = (wctx.enter_context(nc.sbuf_tensor("l1f_" + n, s, F32)) for n, s in
                          (("wg", [P, KD, N]), ("wu", [P, KD, N]), ("wd", [P, KN, D])))
            ternary(K, "l1t", [(wg, a["L1_ffn_w_gateT"], qg, scale[:, 0:1]), (wu, a["L1_ffn_w_upT"], qu, scale[:, 1:2]),
                               (wd, a["L1_ffn_w_downT"], qd, scale[:, 2:3])])
        layernorm(K, "l1f_ln", quant=(XQ, inv))
        sg, su = sb("sg", [P, NT]), sb("su", [P, NT])
        g, h, hq = sb("g", [P, N]), sb("h", [P, N]), sb("hq", [P, N], BF16)
        hT = sb("hT", [P, KN, P], BF16)
        amax, hinv, hscl, down = sb("amax", [P, 1]), sb("hinv", [P, 1]), sb("hscl", [P, 1]), sb("down", [P, 1])
        gate_done, up_done, gate_ok, h_ok, q_ok, turned, hT_ok, y_done, added, scl_ok, hscl_ok, rounded = (
            K.sem("l1f_" + n) for n in ("gate", "up", "gateok", "hok", "qok", "turned", "htok", "ydone", "added", "sclok", "hsclok", "rounded"))
        gb, ub, tb, yb = bank[0:2], bank[2:4], bank[4], bank[5]
        with nc.Block() as block:
            @block.tensor
            def _(pe):
                def products(out, q, t):
                    for half in range(2):
                        for k in range(KD):
                            last = pe.matmul(out[half][:], XQ[:, k, ds(t * P, P)], q[:, k, half * CH:(half + 1) * CH],
                                             start=k == 0, stop=k == KD - 1)
                    return last

                def down_product(t):
                    pe.wait_ge(q_ok, t + 1)
                    tbf = tb[:].bitcast(BF16)
                    for i in range(KN):
                        last = pe.transpose(tbf[:, i * P:(i + 1) * P], hq[:, i * P:(i + 1) * P], K.identb[:])
                    last.then_inc(turned, 1)
                    pe.wait_ge(hT_ok, t + 1)
                    pe.wait_ge(added, t)
                    for i in range(KN):
                        last = pe.matmul(yb[:, 0:D], hT[:, i, :], qd[:, i, :], start=i == 0, stop=i == KN - 1)
                    last.then_inc(y_done, 1)
                products(gb, qg, 0).then_inc(gate_done, 1)
                products(ub, qu, 0).then_inc(up_done, 1)
                with pe.Fori(0, NT - 1) as t:
                    pe.wait_ge(gate_ok, t + 1)
                    products(gb, qg, t + 1).then_inc(gate_done, 1)
                    pe.wait_ge(h_ok, t + 1)
                    products(ub, qu, t + 1).then_inc(up_done, 1)
                    down_product(t)
                down_product(NT - 1)

            @block.scalar
            def _(act):
                act.wait_ge(scl_ok, 2)

                def gate(t):
                    act.wait_ge(gate_done, t + 1)
                    act.wait_ge(h_ok, t)
                    act.activation(g[:, 0:CH], gb[0][:], ACT.Silu, scale=sg[:, ds(t, 1)])
                    act.activation(g[:, CH:N], gb[1][:], ACT.Silu, scale=sg[:, ds(t, 1)]).then_inc(gate_ok, 1)

                def scale_hidden(t):
                    act.wait_ge(hscl_ok, t + 1)
                    act.activation(h[:], h[:], ACT.Identity, bias=K.round[:], scale=hscl[:]).then_inc(rounded, 1)

                def copy_turned(t):
                    act.wait_ge(turned, t + 1)
                    act.wait_ge(y_done, t)
                    act.activation(hT[:].rearrange("p i n -> p (i n)"), tb[:].bitcast(BF16), ACT.Copy).then_inc(hT_ok, 1)
                gate(0)
                with act.Fori(0, NT - 1) as t:
                    scale_hidden(t)
                    gate(t + 1)
                    copy_turned(t)
                scale_hidden(NT - 1)
                copy_turned(NT - 1)

            @block.vector
            def _(dve):
                o = K.dve_order
                dve.tensor_scalar(sg[:], inv[:], scale[:, 0:1], None, ALU.mult).then_inc(scl_ok, 1)
                dve.tensor_scalar(su[:], inv[:], scale[:, 1:2], None, ALU.mult).then_inc(scl_ok, 1)
                dve.wait_ge(scl_ok, 2)

                def hidden(t):
                    dve.wait_ge(up_done, t + 1)
                    dve.wait_ge(gate_ok, t + 1)
                    for half in range(2):
                        c = slice(half * CH, (half + 1) * CH)
                        ins = dve.scalar_tensor_tensor(h[:, c], ub[half][:], su[:, ds(t, 1)], g[:, c], ALU.mult, ALU.mult)
                    ins.then_inc(h_ok, 1)
                    dve.wait_ge(h_ok, t + 1)
                    o.step(dve, dve.tensor_reduce(amax[:], h[:], AX, ALU.max, apply_absolute_value=True))
                    o.step(dve, dve.tensor_scalar(hinv[:], amax[:], 1e-5, 1.0 / 127.0, ALU.max, ALU.mult))
                    dve.reciprocal(hscl[:], hinv[:]).then_inc(hscl_ok, 1)

                def add_output(t):
                    dve.wait_ge(y_done, t + 1)
                    xt = X[:, ds(t, 1), :].rearrange("p a d -> p (a d)")
                    dve.scalar_tensor_tensor(xt, yb[:, 0:D], down[:], xt, ALU.mult, ALU.add).then_inc(added, 1)

                def quantised(t):
                    dve.wait_ge(rounded, t + 1)
                    dve.wait_ge(turned, t)
                    dve.tensor_scalar(hq[:], h[:], ROUND, None, ALU.subtract).then_inc(q_ok, 1)
                hidden(0)
                dve.tensor_scalar(down[:], hinv[:], scale[:, 2:3], None, ALU.mult)
                quantised(0)
                dve.wait_ge(q_ok, 1)
                with dve.Fori(0, NT - 1) as t:
                    o.begin(t, 2)
                    hidden(t + 1)
                    add_output(t)
                    dve.wait_ge(added, t + 1)
                    dve.tensor_scalar(down[:], hinv[:], scale[:, 2:3], None, ALU.mult)
                    quantised(t + 1)
                    dve.wait_ge(q_ok, t + 2)
                    o.end(NT - 1)
                add_output(NT - 1)


@stage
def l2_ffn(K):
    nc, a, X, XT, bank = K.nc, K.a, K.X, K.XT, K.bank
    E, INNER, PROJ, TOP = 8, 32, 8, 2
    NH = E * INNER
    N1 = E + NH + E * PROJ
    W = E + 8 - TOP
    with ExitStack() as ctx:
        def sb(n, shape, dt=F32):
            return ctx.enter_context(nc.sbuf_tensor("l2f_" + n, shape, dt))
        wv, w1, w2 = sb("wv", [P, KD, D]), sb("w1", [P, KD, N1]), sb("w2", [P, KD, D])
        bv, b1, b2 = sb("bv", [P, KD]), sb("b1", [P, N1]), sb("b2", [E, D])
        gb, alpha = sb("gb", [P, 2, 2, E]), sb("alpha", [P, 1])
        vT, r, pv2 = sb("vT", [P, KD, CH]), sb("r", [P, TPC, N1]), sb("pv2", [P, TPC, E * PROJ])
        css = sb("css", [P, TPC * E])
        z, zc, mean, var = sb("z", [P, 2, TPC, E]), sb("zc", [P, 2, TPC, E]), sb("mean", [P, 2 * TPC]), sb("var", [P, 2 * TPC])
        vals, top, rep = sb("vals", [P, TPC, W]), sb("top", [P, TPC, 8]), sb("rep", [P, TPC, W])
        mask, ex, sm, we = sb("mask", [P, TPC, E]), sb("ex", [P, TPC, E]), sb("sm", [P, TPC, 1]), sb("we", [P, TPC, E])
        hid, hT, weT = sb("hid", [P, TPC, NH]), sb("hT", [P, 2, CH]), sb("weT", [E, CH])
        loaded = K.sem("l2f_loaded")

        def load(sp):
            n = load_rows(sp, wv, a["L2_ffn_WvT"], loaded) + load_rows(sp, w1, a["L2_ffn_W1cat"], loaded)
            n += load_rows(sp, w2, a["L2_ffn_W2cat"], loaded)
            small = [(bv[:], a["L2_ffn_bv"]), (b1[:, 0:E + NH], a["L2_ffn_b1cat"].partition_broadcast(P)), (b2[:], a["L2_ffn_b2"]),
                     (alpha[:], a["L2_ffn_alpha"].partition_broadcast(P)),
                     (gb[:].rearrange("p a b e -> p (a b e)"), a["L2_ffn_gb"].partition_broadcast(P))]
            for dst, src in small:
                sp.dma_start(dst, src).then_inc(loaded, 16)
            sp.wait_ge(loaded, n + 16 * len(small))
        layernorm(K, "l2f_ln", load)

        names = ("vdone", "vok", "sdone", "rok", "css", "cok", "var", "std", "sh", "xp", "silu", "hok", "turned", "tok", "ydone", "added", "alpha", "sig")
        v_done, v_ok, s_done, r_ok, css_ok, c_ok, var_ok, std_ok, sh, xp, silu, h_ok, turned, t_ok, y_done, added, al, sg = (
            K.sem("l2f_" + n) for n in names)
        with nc.Block() as block:
            @block.tensor
            def _(pe):
                with pe.Fori(0, NC) as c:
                    pe.wait_ge(t_ok, 3 * c)
                    for m in range(KD):
                        for k in range(KD):
                            last = pe.matmul(bank[m][:], wv[:, k, m * P:(m + 1) * P], XT[:, k, ds(c * CH, CH)], start=k == 0, stop=k == KD - 1)
                        last.then_inc(v_done, 1)
                    pe.wait_ge(v_ok, KD * (c + 1))
                    pe.wait_ge(added, TPC * c)
                    for j in range(TPC):
                        for k in range(KD):
                            last = pe.matmul(bank[2 + j][:, 0:N1], vT[:, k, j * P:(j + 1) * P], w1[:, k, :], start=k == 0, stop=k == KD - 1)
                        last.then_inc(s_done, 1)
                    pe.wait_ge(h_ok, c + 1)
                    for j in range(TPC):
                        pe.transpose(bank[0][0:E, j * P:(j + 1) * P], we[:, j, :], K.ident[:])
                    for k in range(2):
                        for j in range(TPC):
                            last = pe.transpose(bank[6 + k][:, j * P:(j + 1) * P], hid[:, j, k * P:(k + 1) * P], K.ident[:])
                    last.then_inc(turned, 1)
                    pe.wait_ge(t_ok, 3 * (c + 1))
                    for j in range(TPC):
                        w = slice(j * P, (j + 1) * P)
                        y = bank[2 + j // 2][:, (j % 2) * D:(j % 2 + 1) * D]
                        pe.matmul(y, weT[:, w], b2[:], start=True, stop=False)
                        for k in range(2):
                            pe.matmul(y, hT[:, k, w], w2[:, k, :], start=False, stop=False)
                        for k in range(KD):
                            last = pe.matmul(y[:, k * P:(k + 1) * P], vT[:, k, w], K.ident[:], start=False, stop=k == KD - 1)
                        last.then_inc(y_done, 1)

            @block.scalar
            def _(act):
                act.wait_ge(al, 1)
                act.activation(alpha[:], alpha[:], ACT.Sigmoid).then_inc(sg, 1)
                with act.Fori(0, NC) as c:
                    act.wait_ge(y_done, TPC * c)
                    for m in range(KD):
                        act.wait_ge(v_done, KD * c + m + 1)
                        act.activation(vT[:, m, :], bank[m][:], ACT.Identity, bias=bv[:, m:m + 1]).then_inc(v_ok, 1)
                    act.wait_ge(css_ok, c + 1)
                    act.activation(z[:, 1, :, :].rearrange("p t e -> p (t e)"), css[:], ACT.Sqrt, scale=1.0 / PROJ).then_inc(c_ok, 1)
                    act.wait_ge(var_ok, c + 1)
                    act.activation(var[:], var[:], ACT.Sqrt).then_inc(std_ok, 1)
                    act.wait_ge(sh, c + 1)
                    act.activation(ex[:], ex[:], ACT.Exp).then_inc(xp, 1)
                    act.activation(hid[:], r[:, :, E:E + NH], ACT.Silu).then_inc(silu, 1)
                    act.wait_ge(turned, c + 1)
                    act.activation(weT[:], bank[0][0:E, :], ACT.Copy).then_inc(t_ok, 1)
                    act.activation(hT[:, 0, :], bank[6][:], ACT.Copy).then_inc(t_ok, 1)

            @block.vector
            def _(dve):
                o = K.dve_order
                o.mark(dve.memset(vals[:, :, E:W], NEG))
                o.step(dve, dve.memset(b1[:, E + NH:N1], 0.0))
                dve.sem_inc(al, 1)
                dve.wait_ge(sg, 1)
                bc = [P, 2, TPC, E]
                with dve.Fori(0, NC) as c:
                    o.begin(c, 20 + 2 * TPC)
                    for j in range(TPC):
                        dve.wait_ge(s_done, TPC * c + j + 1)
                        dve.tensor_tensor(r[:, j, :], bank[2 + j][:, 0:N1], b1[:], ALU.add).then_inc(r_ok, 1)
                    dve.wait_ge(r_ok, TPC * (c + 1))
                    pv = r[:, :, E + NH:N1]
                    o.step(dve, dve.tensor_tensor(pv2[:], pv, pv, ALU.mult))
                    dve.tensor_reduce(css[:], pv2[:].rearrange("p t (e q) -> p (t e) q", q=PROJ), AX, ALU.add).then_inc(css_ok, 1)
                    o.step(dve, dve.tensor_copy(z[:, 0, :, :], r[:, :, 0:E]))
                    dve.wait_ge(c_ok, c + 1)
                    zf, zcf = z[:].rearrange("p a t e -> p (a t) e"), zc[:].rearrange("p a t e -> p (a t) e")
                    b8 = [P, 2 * TPC, E]
                    o.step(dve, dve.tensor_reduce(mean[:], zf, AX, ALU.add))
                    o.step(dve, dve.tensor_scalar(mean[:], mean[:], 1.0 / E, None, ALU.mult))
                    o.step(dve, dve.tensor_tensor(zcf, zf, mean[:].unsqueeze(2).to_broadcast(b8), ALU.subtract))
                    o.step(dve, dve.tensor_tensor(zf, zcf, zcf, ALU.mult))
                    o.step(dve, dve.tensor_reduce(var[:], zf, AX, ALU.add))
                    dve.tensor_scalar(var[:], var[:], 1.0 / E, LN_EPS, ALU.mult, ALU.add).then_inc(var_ok, 1)
                    dve.wait_ge(std_ok, c + 1)
                    o.step(dve, dve.reciprocal(var[:], var[:]))
                    o.step(dve, dve.tensor_tensor(zcf, zcf, var[:].unsqueeze(2).to_broadcast(b8), ALU.mult))
                    o.step(dve, dve.tensor_tensor(zc[:], zc[:], gb[:, 0, :, :].unsqueeze(2).to_broadcast(bc), ALU.mult))
                    o.step(dve, dve.tensor_tensor(zc[:], zc[:], gb[:, 1, :, :].unsqueeze(2).to_broadcast(bc), ALU.add))
                    o.step(dve, dve.scalar_tensor_tensor(vals[:, :, 0:E], zc[:, 1, :, :], alpha[:], zc[:, 0, :, :], ALU.mult, ALU.add))
                    select_top(K, dve, o, vals, top, rep, mask[:], E, TOP)
                    dve.tensor_tensor(ex[:], vals[:, :, 0:E], top[:, :, 0:1].to_broadcast([P, TPC, E]), ALU.subtract).then_inc(sh, 1)
                    dve.wait_ge(xp, c + 1)
                    o.step(dve, dve.tensor_tensor(ex[:], ex[:], mask[:], ALU.mult))
                    o.step(dve, dve.tensor_reduce(sm[:], ex[:], AX, ALU.add))
                    o.step(dve, dve.reciprocal(sm[:], sm[:]))
                    o.step(dve, dve.tensor_tensor(we[:], ex[:], sm[:].to_broadcast([P, TPC, E]), ALU.mult))
                    dve.wait_ge(silu, c + 1)
                    hv = hid[:].rearrange("p t (e i) -> p (t e) i", i=INNER)
                    dve.tensor_tensor(hv, hv, we[:].rearrange("p t e -> p (t e)").unsqueeze(2).to_broadcast([P, TPC * E, INNER]), ALU.mult).then_inc(h_ok, 1)
                    dve.wait_ge(turned, c + 1)
                    dve.tensor_copy(hT[:, 1, :], bank[7][:]).then_inc(t_ok, 1)
                    for j in range(TPC):
                        dve.wait_ge(y_done, TPC * c + TPC)
                        xt = X[:, ds(c * TPC + j, 1), :].rearrange("p a d -> p (a d)")
                        dve.tensor_tensor(xt, xt, bank[2 + j // 2][:, (j % 2) * D:(j % 2 + 1) * D], ALU.add).then_inc(added, 1)
                    o.end(NC)


def global_quant(K, name, items):
    nc = K.nc
    n_i = len(items)
    n_p = sum(len(parts) for parts, _ in items)
    with ExitStack() as ctx:
        def sb(n, shape, dt=F32):
            return ctx.enter_context(nc.sbuf_tensor(f"{name}_{n}", shape, dt))
        part_max, item_max = sb("pmax", [P, n_p]), sb("imax", [P, n_i])
        top, inv = sb("top", [n_i, 1]), sb("inv", [P, n_i])
        maxed, turned, topped, spread, inv_ok, scaled = (K.sem(f"{name}_{x}") for x in ("maxed", "turned", "topped", "spread", "inv", "scaled"))
        with nc.Block() as block:
            @block.vector
            def _(dve):
                o = K.dve_order
                o.step(dve, dve.memset(part_max[:], 0.0))
                n = 0
                for parts, _ in items:
                    for x, q in parts:
                        o.mark(dve.tensor_reduce(part_max[0:x.shape[0], n:n + 1], x, AX, ALU.max, apply_absolute_value=True))
                        n += 1
                o.wait(dve)
                n = 0
                for i, (parts, _) in enumerate(items):
                    dve.tensor_reduce(item_max[:, i:i + 1], part_max[:, n:n + len(parts)], AX, ALU.max).then_inc(maxed, 1)
                    n += len(parts)
                dve.wait_ge(turned, 1)
                dve.tensor_reduce(top[:], K.bank[0][0:n_i, 0:P], AX, ALU.max).then_inc(topped, 1)
                dve.wait_ge(spread, 1)
                for i, (_, s) in enumerate(items):
                    o.mark(dve.tensor_scalar(s, K.bank[1][:, i:i + 1], 1e-8, 1.0 / 127.0, ALU.max, ALU.mult))
                o.wait(dve)
                for i, (_, s) in enumerate(items):
                    dve.reciprocal(inv[:, i:i + 1], s).then_inc(inv_ok, 1)
                n = 0
                for parts, _ in items:
                    for x, q in parts:
                        n += 1
                        dve.wait_ge(scaled, n)
                        dve.tensor_scalar(q, x, ROUND, None, ALU.subtract)

            @block.tensor
            def _(pe):
                pe.wait_ge(maxed, n_i)
                pe.transpose(K.bank[0][0:n_i, 0:P], item_max[:], K.ident[:]).then_inc(turned, 1)
                pe.wait_ge(topped, 1)
                pe.matmul(K.bank[1][:, 0:n_i], top[:].to_broadcast([n_i, P]), K.ident[0:n_i, 0:n_i], start=True, stop=True).then_inc(spread, 1)

            @block.scalar
            def _(act):
                act.wait_ge(inv_ok, n_i)
                for i, (parts, _) in enumerate(items):
                    for x, q in parts:
                        p = x.shape[0]
                        act.activation(x, x, ACT.Identity, bias=K.round[0:p, :], scale=inv[0:p, i:i + 1]).then_inc(scaled, 1)


def bit_linear(K, name, jobs, relu=False):
    nc = K.nc
    units = [(j, m) for j, job in enumerate(jobs) for m in range(job[3].shape[1])]
    R = min(4, len(units))
    assert len(units) % R == 0
    with ExitStack() as ctx:
        scale = ctx.enter_context(nc.sbuf_tensor(name + "_scale", [P, len(jobs)], F32))
        scale_ok, done, read = K.sem(name + "_scale"), K.sem(name + "_done"), K.sem(name + "_read")
        with nc.Block() as block:
            @block.vector
            def _(dve):
                for j, job in enumerate(jobs):
                    dve.tensor_tensor(scale[:, j:j + 1], job[4], job[5], ALU.mult).then_inc(scale_ok, 1)

            @block.tensor
            def _(pe):
                with pe.Fori(0, NC) as c:
                    for u, (j, m) in enumerate(units):
                        q, qw, rows = jobs[j][:3]
                        pe.wait_ge(read, c * len(units) + u + 1)
                        kts = -(-rows // P)
                        for k in range(kts):
                            p = min(P, rows - k * P)
                            last = pe.matmul(K.bank[u % R][:], qw[0:p, k, m * P:(m + 1) * P], q[0:p, k, ds(c * CH, CH)], start=k == 0, stop=k == kts - 1)
                        last.then_inc(done, 1)

            @block.scalar
            def _(act):
                act.sem_inc(read, R)
                act.wait_ge(scale_ok, len(jobs))
                with act.Fori(0, NC) as c:
                    for u, (j, m) in enumerate(units):
                        out, bias = jobs[j][3], jobs[j][6]
                        act.wait_ge(done, c * len(units) + u + 1)
                        act.activation(out[:, m, ds(c * CH, CH)], K.bank[u % R][:], ACT.Relu if relu else ACT.Identity,
                                       bias=bias[:, m:m + 1], scale=scale[:, j:j + 1]).then_inc(read, 1)


def shared_key_attention(K, name, F, kv):
    nc, bank = K.nc, K.bank
    NB, QT, A = 2, S // P, len(kv)
    with ExitStack() as ctx:
        def sb(n, shape, dt=F32):
            return ctx.enter_context(nc.sbuf_tensor(f"{name}_{n}", shape, dt))
        fs, kb, kt = sb("fs", [P, NB, S]), sb("kb", [P, NB, S]), sb("kt", [P, NB, 2, P])
        nmax, sums, rs = sb("nmax", [P, NB * QT]), sb("sums", [P, NB * QT]), sb("rs", [P, NB * QT])
        pr, pt = sb("pr", [P, NB, QT, S]), sb("pt", [P, NB, 2 * S])
        kb_ok, fs_ok, s_done, kt_ok, max_ok, exp_ok, pr_ok, t_done, pt_ok, y_done, added = (
            K.sem(f"{name}_{x}") for x in ("kb", "fs", "sdone", "kt", "max", "exp", "pr", "tdone", "pt", "ydone", "added"))
        with nc.Block() as block:
            @block.gpsimd
            def _(pool):
                with pool.Fori(0, B // NB) as g:
                    for i in range(A):
                        n = g * A + i
                        pool.wait_ge(t_done, n)
                        pool.tensor_copy(kb[:].rearrange("p b s -> p (b s)"), kv[i][:, ds(g * NB * S, NB * S)]).then_inc(kb_ok, 1)

            @block.tensor
            def _(pe):
                with pe.Fori(0, B // NB) as g:
                    for i in range(A):
                        n = g * A + i
                        pe.wait_ge(kb_ok, n + 1)
                        pe.wait_ge(fs_ok, n + 1)
                        for b in range(NB):
                            for q in range(QT):
                                last = pe.matmul(bank[b][:, q * S:(q + 1) * S], fs[:, b, q * P:(q + 1) * P], kb[:, b, :], start=True, stop=True)
                            last.then_inc(s_done, 1)
                        for b in range(NB):
                            for k in range(2):
                                last = pe.transpose(bank[2][:, (b * 2 + k) * P:(b * 2 + k + 1) * P], kb[:, b, k * P:(k + 1) * P], K.ident[:])
                        last.then_inc(s_done, 1)
                        for b in range(NB):
                            pe.wait_ge(pr_ok, NB * n + b + 1)
                            for k in range(2):
                                for q in range(QT):
                                    c = (k * QT + q) * P
                                    last = pe.transpose(bank[3 + b][:, c:c + P], pr[:, b, q, k * P:(k + 1) * P], K.ident[:])
                            if b == NB - 1:
                                last.then_inc(t_done, 1)
                            else:
                                last.then_inc(s_done, 1)
                        pe.wait_ge(kt_ok, n + 1)
                        for b in range(NB):
                            pe.wait_ge(pt_ok, NB * n + b + 1)
                            for k in range(2):
                                last = pe.matmul(bank[5][:, b * S:(b + 1) * S], kt[:, b, k, :], pt[:, b, k * S:(k + 1) * S], start=k == 0, stop=k == 1)
                        last.then_inc(y_done, 1)

            @block.scalar
            def _(act):
                with act.Fori(0, B // NB) as g:
                    for i in range(A):
                        n = g * A + i
                        act.wait_ge(t_done, n)
                        for b in range(NB):
                            act.wait_ge(max_ok, NB * n + b + 1)
                            for q in range(QT):
                                x = b * QT + q
                                act.activation(pr[:, b, q, :], bank[b][:, q * S:(q + 1) * S], ACT.Exp, bias=nmax[:, x:x + 1],
                                               scale=D ** -0.5, accum_out=sums[:, x:x + 1]).then_inc(exp_ok, 1)
                        act.wait_ge(s_done, (NB + NB) * n + NB + 1)
                        act.wait_ge(y_done, n)
                        act.activation(kt[:].rearrange("p b k s -> p (b k s)"), bank[2][:], ACT.Copy).then_inc(kt_ok, 1)

            @block.vector
            def _(dve):
                o = K.dve_order
                with dve.Fori(0, B // NB) as g:
                    o.begin(g, A * NB * 3)
                    for i in range(A):
                        n = g * A + i
                        fb = F[:, :, ds(g * NB * S, NB * S)]
                        dve.wait_ge(added, n)
                        dve.tensor_tensor(fs[:].rearrange("p b s -> p (b s)"), fb[:, 0, :], fb[:, 1, :], ALU.add).then_inc(fs_ok, 1)
                        for b in range(NB):
                            dve.wait_ge(s_done, (NB + NB) * n + b + 1)
                            w = slice(b * QT, (b + 1) * QT)
                            o.step(dve, dve.tensor_reduce(nmax[:, w], bank[b][:].rearrange("p (q s) -> p q s", q=QT), AX, ALU.max, negate=True))
                            dve.tensor_scalar(nmax[:, w], nmax[:, w], D ** -0.5, None, ALU.mult).then_inc(max_ok, 1)
                        for b in range(NB):
                            dve.wait_ge(exp_ok, QT * (NB * n + b + 1))
                            w = slice(b * QT, (b + 1) * QT)
                            o.step(dve, dve.reciprocal(rs[:, w], sums[:, w]))
                            for q in range(QT):
                                x = b * QT + q
                                ins = dve.tensor_scalar(pr[:, b, q, :], pr[:, b, q, :], rs[:, x:x + 1], 0.1, ALU.mult, ALU.mult)
                                if q == 0:
                                    o.mark(ins)
                            ins.then_inc(pr_ok, 1)
                        for b in range(NB):
                            if b == NB - 1:
                                dve.wait_ge(t_done, n + 1)
                            else:
                                dve.wait_ge(s_done, (NB + NB) * n + NB + 2 + b)
                            dve.tensor_copy(pt[:, b, :], bank[3 + b][:]).then_inc(pt_ok, 1)
                        dve.wait_ge(y_done, n + 1)
                        dve.tensor_tensor(fb, fb, bank[5][:].unsqueeze(1).to_broadcast([P, KD, NB * S]), ALU.add).then_inc(added, 1)
                    o.end(B // NB)


@stage
def l3_xattn(K):
    nc, a, X, XT, CT, bank = K.nc, K.a, K.X, K.XT, K.CT, K.bank
    N = 1024
    KN = N // P
    with ExitStack() as ctx:
        def sb(n, shape, dt=F32, c=ctx):
            return c.enter_context(nc.sbuf_tensor("l3x_" + n, shape, dt))
        ws = [("d2v", DC, D), ("img", D, D), ("txt", D, D), ("att0", D, P), ("att1", D, P), ("f1", 2 * D, N), ("f2", N, D)]
        q, scale, bias = {}, sb("wscale", [P, len(ws)]), {}
        for n, rows, cols in ws:
            q[n] = sb("q_" + n, [P, -(-rows // P), cols], BF16)
            bias[n] = sb("b_" + n, [P, D if n == "f2" else cols // P])
        wsc = {n: scale[:, i:i + 1] for i, (n, _, _) in enumerate(ws)}
        loaded = K.sem("l3x_loaded")
        with ExitStack() as wctx:
            ternary(K, "l3t", [(sb("w_" + n, [P, -(-rows // P), cols], F32, wctx), a[f"L3_xattn_W_{n}T"], q[n], wsc[n]) for n, rows, cols in ws])

        def load(sp):
            for n, rows, cols in ws:
                src = a[f"L3_xattn_b_{n}"]
                sp.dma_start(bias[n][:], src.partition_broadcast(P) if n == "f2" else src).then_inc(loaded, 16)
            sp.wait_ge(loaded, 16 * len(ws))
        layernorm(K, "l3x_ln", load)

        s = sb("s", [P, 6])
        hctx = ExitStack()
        hid = sb("hid", [P, KN, T], F32, hctx)
        with ExitStack() as c1:
            qa = sb("qa", [P, 4, T], BF16, c1)
            kv = sb("kv", [P, 2, T], F32, c1)
            avg = sb("avg", [P, KD, B], F32, c1)
            avg_q = sb("avgq", [P, KD, B], BF16, c1)
            global_quant(K, "l3q0", [([(CT[:, 0, :], qa[:, 0, :]), (CT[0:HALF_C, 1, :], qa[0:HALF_C, 1, :])], s[:, 0:1]),
                                     ([(XT[:, k, :], qa[:, 2 + k, :]) for k in range(KD)], s[:, 1:2])])
            VIS, FUSED = CT, XT
            bit_linear(K, "l3l0", [(qa[:, 0:2, :], q["d2v"], DC, VIS, s[:, 0:1], wsc["d2v"], bias["d2v"]),
                                   (qa[:, 2:4, :], q["txt"], D, FUSED, s[:, 1:2], wsc["txt"], bias["txt"])])
            global_quant(K, "l3q1", [([(VIS[:, k, :], qa[:, k, :]) for k in range(KD)], s[:, 2:3])])
            IMG = VIS
            bit_linear(K, "l3l1", [(qa[:, 0:2, :], q["img"], D, IMG, s[:, 2:3], wsc["img"], bias["img"])])
            with nc.Block() as block:
                @block.vector
                def _(dve):
                    for k in range(KD):
                        K.dve_order.step(dve, dve.tensor_reduce(avg[:, k, :], IMG[:, k, :].rearrange("p (b s) -> p b s", s=S), AX, ALU.add))
                    dve.tensor_scalar(avg[:], avg[:], 1.0 / S, None, ALU.mult)
            global_quant(K, "l3q2", [([(IMG[:, k, :], qa[:, k, :]) for k in range(KD)], s[:, 3:4])])
            bit_linear(K, "l3l2", [(qa[:, 0:2, :], q["att%d" % i], D, kv[:, i:i + 1, :], s[:, 3:4], wsc["att%d" % i], bias["att%d" % i])
                                   for i in range(2)])
            shared_key_attention(K, "l3a", FUSED, [kv[:, i, :] for i in range(2)])
            flat = "p k b -> p (k b)"
            global_quant(K, "l3q3", [([(FUSED[:, k, :], qa[:, k, :]) for k in range(KD)]
                                      + [(avg[:].rearrange(flat), avg_q[:].rearrange(flat))], s[:, 4:5])])
            with nc.Block() as block:
                @block.vector
                def _(dve):
                    for k in range(KD):
                        dve.tensor_copy(qa[:, 2 + k, :].rearrange("p (b s) -> p b s", s=S), avg_q[:, k, :].unsqueeze(2).to_broadcast([P, B, S]))
            bit_linear(K, "l3l3", [(qa, q["f1"], 2 * D, hid, s[:, 4:5], wsc["f1"], bias["f1"])], relu=True)
        qh, out_scale = sb("qh", [P, KN, T], BF16, hctx), sb("oscale", [P, 1], F32, hctx)
        tmp = sb("tmp", [P, 2, D], F32, hctx)
        global_quant(K, "l3q4", [([(hid[:, k, :], qh[:, k, :]) for k in range(KN)], s[:, 5:6])])
        y_done, y_read = K.sem("l3x_ydone"), K.sem("l3x_yread")
        with nc.Block() as block:
            @block.tensor
            def _(pe):
                with pe.Fori(0, NT // 2) as g:
                    for i in range(2):
                        pe.wait_ge(y_read, 2 * g + i + 1)
                        for k in range(KN):
                            last = pe.matmul(bank[i][:, 0:D], qh[:, k, ds((g * 2 + i) * P, P)], q["f2"][:, k, :], start=k == 0, stop=k == KN - 1)
                        last.then_inc(y_done, 1)

            @block.vector
            def _(dve):
                o = K.dve_order
                dve.sem_inc(y_read, 2)
                o.step(dve, dve.tensor_tensor(out_scale[:], s[:, 5:6], wsc["f2"], ALU.mult))
                with dve.Fori(0, NT // 2) as g:
                    o.begin(g, 2)
                    for i in range(2):
                        dve.wait_ge(y_done, 2 * g + i + 1)
                        dve.scalar_tensor_tensor(tmp[:, i, :], bank[i][:, 0:D], out_scale[:], bias["f2"][:], ALU.mult, ALU.add).then_inc(y_read, 1)
                        dve.wait_ge(y_read, 2 * g + i + 3)
                        xt = X[:, ds(g * 2 + i, 1), :]
                        o.mark(dve.tensor_tensor(xt, xt, tmp[:, i:i + 1, :], ALU.add))
                    o.wait(dve)
                    o.end(NT // 2)
        hctx.close()


def place_tokens(K, name, mask, gates, slot, gate, tile_expert):
    nc, bank = K.nc, K.bank
    E = EXPERTS3
    FAR = 2.0 * SLOT_TILES * P
    with ExitStack() as ctx:
        def sb(n, shape, dt=F32):
            return ctx.enter_context(nc.sbuf_tensor(f"{name}_{n}", shape, dt))
        before, ones, chosen = sb("before", [P, P], BF16), sb("ones", [P, P], BF16), sb("chosen", [P, NT, E], BF16)
        pos, hit, pick, edge = sb("pos", [P, NT, E]), sb("hit", [P, NT, E]), sb("pick", [P, NT, E]), sb("edge", [P, NT, 1])
        ends, shifted = sb("ends", [P, E]), sb("shifted", [P, E])
        passed, te = sb("passed", [1, SLOT_TILES, E]), sb("te", [1, SLOT_TILES])
        tri, counted, chosen_ok = K.sem(name + "_tri"), K.sem(name + "_counted"), K.sem(name + "_chosen")
        with nc.Block() as block:
            @block.gpsimd
            def _(pool):
                pool.memset(ones[:], 1.0).then_inc(tri, 1)
                pool.wait_ge(tri, 1)
                pool.affine_select(out=before[:], in_=ones[:], compare_op=ALU.is_gt, fill=0.0, base=0,
                                   pattern=[[1, P]], channel_multiplier=-1).then_inc(tri, 1)

            @block.tensor
            def _(pe):
                pe.wait_ge(chosen_ok, 1)
                pe.wait_ge(tri, 2)
                for t in range(NT):
                    pe.matmul(bank[0][:, 0:E], ones[:], chosen[:, t, :], start=t == 0, stop=t == NT - 1)
                pe.matmul(bank[1][:, 0:NT * E], before[:], chosen[:].rearrange("p t e -> p (t e)"), start=True, stop=False)
                for u in range(1, NT):
                    pe.matmul(bank[1][:, u * E:NT * E], ones[:], chosen[:, 0:NT - u, :].rearrange("p t e -> p (t e)"),
                              start=False, stop=u == NT - 1)
                pe.matmul(bank[2][:, 0:P], ones[:], before[:], start=True, stop=True).then_inc(counted, 1)

            @block.vector
            def _(dve):
                o = K.dve_order
                dve.tensor_copy(chosen[:], mask).then_inc(chosen_ok, 1)
                dve.wait_ge(counted, 1)
                o.step(dve, dve.tensor_scalar(ends[:], bank[0][:, 0:E], 1.0 / P, 0.5 - 0.5 / P, ALU.mult, ALU.add))
                o.step(dve, dve.tensor_scalar(ends[:], ends[:], ROUND, None, ALU.add))
                o.step(dve, dve.tensor_scalar(ends[:], ends[:], ROUND, None, ALU.subtract))
                n = 1
                while n < E:
                    o.step(dve, dve.tensor_copy(shifted[:], ends[:]))
                    o.step(dve, dve.tensor_tensor(ends[:, n:E], ends[:, n:E], shifted[:, 0:E - n], ALU.add))
                    n *= 2
                o.mark(dve.memset(shifted[:, 0:1], 0.0))
                o.step(dve, dve.tensor_scalar(shifted[:, 1:E], ends[:, 0:E - 1], float(P), None, ALU.mult))
                every = [P, NT, E]
                o.mark(dve.tensor_tensor(pos[:], bank[1][:, 0:NT * E].rearrange("p (t e) -> p t e", e=E),
                                         shifted[:].unsqueeze(1).to_broadcast(every), ALU.add))
                o.mark(dve.tensor_tensor(passed[:], ends[0:1, :].unsqueeze(1).to_broadcast([1, SLOT_TILES, E]),
                                         bank[2][0:1, 0:SLOT_TILES].unsqueeze(2).to_broadcast([1, SLOT_TILES, E]), ALU.is_le))
                o.wait(dve)
                o.step(dve, dve.tensor_reduce(te[:], passed[:], AX, ALU.add))
                o.mark(dve.tensor_scalar(tile_expert, te[:], E - 1.0, None, ALU.min))
                for i, sign in enumerate((-1.0, 1.0)):
                    o.step(dve, dve.scalar_tensor_tensor(hit[:], mask, sign * FAR, pos[:], ALU.mult, ALU.add))
                    o.step(dve, dve.tensor_reduce(edge[:], hit[:], AX, ALU.min if i == 0 else ALU.max))
                    o.step(dve, dve.tensor_tensor(pick[:], hit[:], edge[:].to_broadcast(every), ALU.is_equal))
                    o.step(dve, dve.tensor_tensor(pick[:], pick[:], gates, ALU.mult))
                    o.mark(dve.tensor_reduce(gate[i], pick[:], AX, ALU.add))
                    o.step(dve, dve.tensor_scalar(slot[i], edge[:].rearrange("p t a -> p (t a)"), -sign * FAR, None, ALU.add))


def routed_tiles(K, name, E, N, wu, wd, b1, b2_src, tile_expert, weights, weights_n):
    nc, bank = K.nc, K.bank
    HT, U = N // P, 3
    assert SLOT_TILES % U == 0
    up_b, turn_b, x_b, y_b = bank[0:2], bank[2:4], bank[4], bank[5]
    area = K.XT[:].rearrange("p k t -> p (k t)")

    def part(at, n, k):
        return area[:, at:at + n * k].rearrange("p (k n) -> p k n", k=k)
    xs, ys, xT = part(0, D, U), part(U * D, D, U), part(2 * U * D, P, KD)
    h, hT = area[:, 7 * D:7 * D + N], part(7 * D + N, P, HT)
    b2 = K.CT[:].rearrange("p k t -> p (k t)")[:, 0:E * D].rearrange("p (e d) -> p e d", e=E)
    x_in = [K.sem(f"{name}_xin{u}") for u in range(U)]
    y_out = [K.sem(f"{name}_yout{u}") for u in range(U)]
    b2_in, x_turned, xT_ok, up_done, h_act, h_dve, turned, hT_act, hT_dve, y_done, y_ok = (
        K.sem(f"{name}_{n}") for n in ("b2in", "xturned", "xtok", "updone", "hact", "hdve", "turned", "htact", "htdve", "ydone", "yok"))
    G = SLOT_TILES // U

    def tiles(eng, body):
        for u in range(U):
            body(u, u, u == 0, False)
        with eng.Fori(1, G - 1) as g:
            for u in range(U):
                body(g * U + u, u, False, False)
        for u in range(U):
            body((G - 1) * U + u, u, False, u == U - 1)

    def expert(eng, i):
        at = tile_expert[:, i:i + 1] if isinstance(i, int) else tile_expert[:, ds(i, 1)]
        return eng.value_load(at, min_val=0, max_val=E - 1)

    with nc.Block() as block:
        @block.sync
        def _(sp):
            sp.dma_start(b2.rearrange("p e d -> p (e d)"), b2_src.partition_broadcast(P)).then_inc(b2_in, 16)

            def load(i, u):
                sp.dma_start(xs[:, u, :], K.slots[ds(i * P, P), :]).then_inc(x_in[u], 16)

            def store(i, u):
                sp.wait_ge(y_ok, i + 1)
                sp.dma_start(K.slot_out[ds(i * P, P), :], ys[:, u, :]).then_inc(y_out[u], 16)
            for u in range(U):
                load(u, u)
            with sp.Fori(0, G - 1) as g:
                for u in range(U):
                    i = g * U + u
                    sp.wait_ge(x_turned, i + 1)
                    load(i + U, u)
                    store(i, u)
            for u in range(U):
                store((G - 1) * U + u, u)
            for u in range(U):
                sp.wait_ge(y_out[u], 16 * G)

        @block.tensor
        def _(pe):
            def turn_input(i, u, n):
                pe.wait_ge(x_in[u], 16 * n)
                for k in range(KD):
                    last = pe.transpose(x_b[:, k * P:(k + 1) * P], xs[:, u, k * P:(k + 1) * P], K.ident[:])
                last.then_inc(x_turned, 1)

            def up(i):
                e = expert(pe, i)
                pe.wait_ge(xT_ok, i + 1)
                for half in range(2):
                    for k in range(KD):
                        last = pe.matmul(up_b[half][:], xT[:, k, :], wu[:, ds(e * KD + k, 1), half * CH:(half + 1) * CH].rearrange("p a n -> p (a n)"),
                                         start=k == 0, stop=k == KD - 1)
                    last.then_inc(up_done, 1)

            def down(i):
                e = expert(pe, i)
                pe.wait_ge(hT_act, i + 1)
                pe.wait_ge(hT_dve, i + 1)
                for m in range(HT):
                    last = pe.matmul(y_b[:, 0:D], hT[:, m, :], wd[:, ds(e * HT + m, 1), :].rearrange("p a n -> p (a n)"),
                                     start=m == 0, stop=m == HT - 1)
                last.then_inc(y_done, 1)

            def turn_hidden(i):
                for half in range(2):
                    pe.wait_ge(h_act if half == 0 else h_dve, i + 1)
                    for j in range(HT // 2):
                        m = half * (HT // 2) + j
                        last = pe.transpose(turn_b[half][:, j * P:(j + 1) * P], h[:, m * P:(m + 1) * P], K.ident[:])
                    last.then_inc(turned, 1)
            pe.wait_ge(weights, weights_n)
            turn_input(0, 0, 1)

            def body(i, u, n, first, last):
                up(i)
                if not last:
                    turn_input(i + 1, (u + 1) % U, n + (u + 1) // U)
                if not first:
                    down(i - 1)
                turn_hidden(i)
            for u in range(U):
                body(u, u, 1, u == 0, False)
            with pe.Fori(1, G - 1) as g:
                for u in range(U):
                    body(g * U + u, u, g + 1, False, False)
            for u in range(U):
                body((G - 1) * U + u, u, G, False, u == U - 1)
            down(SLOT_TILES - 1)

        @block.scalar
        def _(act):
            act.wait_ge(x_turned, 1)
            act.activation(xT.rearrange("p k n -> p (k n)"), x_b[:, 0:D], ACT.Copy).then_inc(xT_ok, 1)

            def body(i, u, first, last):
                e = expert(act, i)
                act.wait_ge(up_done, 2 * i + 1)
                act.activation(h[:, 0:CH], up_b[0][:], ACT.Copy).then_inc(h_act, 1)
                if not last:
                    act.wait_ge(x_turned, i + 2)
                    act.activation(xT.rearrange("p k n -> p (k n)"), x_b[:, 0:D], ACT.Copy).then_inc(xT_ok, 1)
                act.wait_ge(turned, 2 * i + 1)
                for m in range(HT // 2):
                    last_one = act.activation(hT[:, m, :], turn_b[0][:, m * P:(m + 1) * P], ACT.Relu, bias=b1[:, ds(e * HT + m, 1)])
                last_one.then_inc(hT_act, 1)
            tiles(act, body)

        @block.vector
        def _(dve):
            def output(i, u, n):
                e = expert(dve, i)
                dve.wait_ge(y_done, i + 1)
                if not isinstance(n, int) or n > 0:
                    dve.wait_ge(y_out[u], 16 * n)
                dve.tensor_tensor(ys[:, u, :], y_b[:, 0:D], b2[:, ds(e, 1), :].rearrange("p a n -> p (a n)"), ALU.add).then_inc(y_ok, 1)

            def body(i, u, n, first, last):
                e = expert(dve, i)
                dve.wait_ge(up_done, 2 * i + 2)
                dve.tensor_copy(h[:, CH:N], up_b[1][:]).then_inc(h_dve, 1)
                if not first:
                    output(i - 1, (u - 1) % U, n if u else n - 1)
                dve.wait_ge(turned, 2 * i + 2)
                for j in range(HT // 2):
                    m = HT // 2 + j
                    last_one = dve.tensor_scalar(hT[:, m, :], turn_b[1][:, j * P:(j + 1) * P], b1[:, ds(e * HT + m, 1)], 0.0, ALU.add, ALU.max)
                last_one.then_inc(hT_dve, 1)
            dve.wait_ge(b2_in, 16)
            for u in range(U):
                body(u, u, 0, u == 0, False)
            with dve.Fori(1, G - 1) as g:
                for u in range(U):
                    body(g * U + u, u, g, False, False)
            for u in range(U):
                body((G - 1) * U + u, u, G - 1, False, u == U - 1)
            output(SLOT_TILES - 1, U - 1, G - 1)


@stage
def l3_ffn(K):
    nc, a, X = K.nc, K.a, K.X
    E, N = EXPERTS3, 1024
    HT = N // P
    with ExitStack() as ctx:
        def sb(n, shape, dt=F32):
            return ctx.enter_context(nc.sbuf_tensor("l3f_" + n, shape, dt))
        wu, wd = sb("wu", [P, E * KD, N]), sb("wd", [P, E * HT, D])
        w, br, b1 = sb("wr", [P, KD, E]), sb("br", [P, E]), sb("b1", [P, E * HT])
        tile_expert = sb("tile_expert", [1, SLOT_TILES], I32)
        slot = [sb(f"slot{i}", [P, NT], I32) for i in range(TOP3)]
        gate = [sb(f"gate{i}", [P, NT]) for i in range(TOP3)]
        loaded, weights, scattered = K.sem("l3f_loaded"), K.sem("l3f_weights"), K.sem("l3f_scattered")
        gathered = [K.sem(f"l3f_gathered{i}") for i in range(NT)]
        XN = K.CT[:].rearrange("p k t -> p (k t)").rearrange("p (t d) -> p t d", d=D)

        def load(sp):
            load_rows(sp, w, a["L3_ffn_Wr"], loaded)
            sp.dma_start(br[:], a["L3_ffn_br"].partition_broadcast(P)).then_inc(loaded, 16)
            sp.dma_start(b1[:], a["L3_ffn_b1p"].rearrange("p e m -> p (e m)")).then_inc(loaded, 16)
            for e in range(E):
                sp.dma_start(wu[:, e * KD:(e + 1) * KD, :], a["L3_ffn_W1"][e].rearrange("(k p) n -> p k n", p=P)).then_inc(weights, 16)
                sp.dma_start(wd[:, e * HT:(e + 1) * HT, :], a["L3_ffn_W2"][e].rearrange("(k p) n -> p k n", p=P)).then_inc(weights, 16)
            sp.wait_ge(loaded, 48)
        layernorm(K, "l3f_ln", load, keep=XN)
        with ExitStack() as c1:
            gates, mask = (c1.enter_context(nc.sbuf_tensor("l3f_" + n, [P, NT, E], F32)) for n in ("gates", "mask"))
            router(K, "l3r", E, TOP3, w, br[:], gates[:], mask[:], False)
            place_tokens(K, "l3p", mask[:], gates[:], [s[:] for s in slot], [g[:] for g in gate], tile_expert[:])
        with nc.Block() as block:
            @block.gpsimd
            def _(pool):
                pool.wait_ge(K.slots_zeroed, 16)
                for t in range(NT):
                    for i in range(TOP3):
                        pool.indirect_dma_start(K.slots, bass.IndirectOffsetOnAxis(ap=slot[i][:, t:t + 1], axis=0),
                                                XN[:, t, :], None).then_inc(scattered, 16)
                pool.wait_ge(scattered, 16 * NT * TOP3)
        routed_tiles(K, "l3t", E, N, wu, wd, b1, a["L3_ffn_b2"], tile_expert, weights, 32 * E)
        YS = [XN, K.XT[:].rearrange("p k t -> p (k t)").rearrange("p (t d) -> p t d", d=D)]
        first = K.sem("l3f_first")
        with nc.Block() as block:
            @block.gpsimd
            def _(pool):
                for t in range(NT):
                    for i in range(TOP3):
                        pool.indirect_dma_start(YS[i][:, t, :], None, K.slot_out,
                                                bass.IndirectOffsetOnAxis(ap=slot[i][:, t:t + 1], axis=0)).then_inc(gathered[t], 16)

            @block.vector
            def _(dve):
                for t in range(NT):
                    dve.wait_ge(gathered[t], 16 * TOP3)
                    for i in range(TOP3):
                        dve.scalar_tensor_tensor(X[:, t, :], YS[i][:, t, :], gate[i][:, t:t + 1], X[:, t, :], ALU.mult, ALU.add).then_inc(first, 1)
                        dve.wait_ge(first, TOP3 * t + i + 1)


def build(nc, a, first=0, last=7):
    with ExitStack() as ctx:
        K = Shared()
        K.nc, K.a = nc, a
        K.sem = lambda n: ctx.enter_context(nc.semaphore(n))

        def sb(n, shape, dt=F32):
            return ctx.enter_context(nc.sbuf_tensor(n, shape, dt))
        K.X, K.XT, K.CT = sb("X", [P, NT, D]), sb("XT", [P, KD, T]), sb("CT", [P, 2, T])
        K.ident, K.identb, K.ones = sb("ident", [P, P]), sb("identb", [P, P], BF16), sb("ones", [P, P])
        K.zero, K.slots_zeroed = sb("zero", [P, D]), K.sem("slots_zeroed")
        K.slots, K.slot_out = (nc.dram_tensor(n, (SLOT_TILES * P, D), F32, kind="Internal").ap() for n in ("slots", "slot_out"))
        K.round, K.carry = sb("round", [P, 1]), sb("carry", [P, 1])
        K.bank = [ctx.enter_context(nc.psum_tensor(f"bank{i}", [P, CH], F32)) for i in range(8)]
        K.dve_order, K.act_order, K.pool_order = (Order(K.sem(n)) for n in ("dve_order", "act_order", "pool_order"))
        stages = [l0_cosine, l0_ffn, l1_xattn, l1_ffn, l2_xattn, l2_ffn, l3_xattn, l3_ffn]
        start(K)
        for sublayer in stages[first:last + 1]:
            sublayer(K)
        finish(K)


def _t(w):
    import numpy as np
    return np.ascontiguousarray(np.swapaxes(w, -1, -2))


def arrays(inputs):
    import numpy as np
    i = {k: np.asarray(v) for k, v in inputs.items()}
    r = {"x": i["x"], "ctxT": _t(i["ctx_768"].reshape(T, DC))}
    r["L0_xattn_WvT"], r["L0_xattn_WtT"] = _t(i["L0_xattn_Wv"]), _t(i["L0_xattn_Wt"])
    r["L0_xattn_bv"], r["L0_xattn_bt"] = i["L0_xattn_bv"], i["L0_xattn_bt"]
    r["L0_ffn_router_wT"] = _t(i["L0_ffn_router_w"])
    r["L0_ffn_upT"] = _t(np.concatenate([i["L0_ffn_shared_up"], i["L0_ffn_routed_up"]]))
    r["L0_ffn_downT"] = _t(np.concatenate([i["L0_ffn_shared_down"], i["L0_ffn_routed_down"]]))
    for n in ("L1_xattn", "L2_xattn"):
        for w in ("Wq", "Wk", "Wv", "Wo", "bo"):
            r[f"{n}_{w}"] = i[f"{n}_{w}"]
    for w in ("w_gate", "w_up", "w_down"):
        r[f"L1_ffn_{w}T"] = _t(i[f"L1_ffn_{w}"])
    def feature_columns(b):
        return np.moveaxis(b.reshape(b.shape[:-1] + (-1, P)), -1, 0)
    n = "L2_ffn_"
    r[n + "WvT"], r[n + "bv"], r[n + "b2"] = _t(i[n + "Wv"]), feature_columns(i[n + "bv"]), i[n + "b2"]
    r[n + "W1cat"] = np.concatenate([_t(i[n + "Wg"]), _t(i[n + "W1"].reshape(-1, D)), _t(i[n + "Wp"].reshape(-1, D))], axis=1)
    r[n + "b1cat"] = np.concatenate([i[n + "bg"], i[n + "b1"].reshape(-1)])[None]
    r[n + "W2cat"] = _t(i[n + "W2"]).reshape(-1, D)
    r[n + "alpha"] = i[n + "alpha"].reshape(1, 1)
    r[n + "gb"] = np.concatenate([i[n + "g_r"], i[n + "g_c"], i[n + "b_r"], i[n + "b_c"]])[None]
    for w in ("d2v", "img", "txt", "att0", "att1", "f1", "f2"):
        r[f"L3_xattn_W_{w}T"] = _t(i["L3_xattn_W_" + w])
        b = i["L3_xattn_b_" + w]
        r["L3_xattn_b_" + w] = b[None] if w == "f2" else feature_columns(b)
    n = "L3_ffn_"
    for w in ("Wr", "br", "W1", "W2", "b2"):
        r[n + w] = i[n + w]
    r[n + "br"], r[n + "b2"] = i[n + "br"][None], i[n + "b2"].reshape(1, -1)
    r[n + "b1p"] = feature_columns(i[n + "b1"])
    return {k: np.ascontiguousarray(v) for k, v in r.items()}


def kernel(**inputs):
    import concourse.bacc as bacc
    from concourse.bass_utils import run_bass_kernel_spmd
    nc = bacc.Bacc("TRN2", target_bir_lowering=False, num_devices=1)
    data = arrays(inputs)
    aps = {n: nc.dram_tensor("in_" + n, v.shape, mybir.dt.from_np(v.dtype), kind="ExternalInput").ap() for n, v in data.items()}
    aps["out"] = nc.dram_tensor("out_x", (B, S, D), F32, kind="ExternalOutput").ap()
    build(nc, aps)
    r = run_bass_kernel_spmd(nc, [{"in_" + n: v for n, v in data.items()}], core_ids=[0])
    return r.results[0]["out_x"]
```

```python
import concourse.bass as bass
from concourse import mybir
from concourse.alu_op_type import AluOpType as ALU
from contextlib import ExitStack

F32 = mybir.dt.float32
BF16 = mybir.dt.bfloat16
F32R = mybir.dt.float32r
I32 = mybir.dt.int32
ACT = mybir.ActivationFunctionType
AX = mybir.AxisListType.X
ds = bass.ds

P = 128
D = 256
KD = D // P
DC = 192
B, S = 8, 256
T = B * S
NT = T // P
CH = 512
NC = T // CH
TPC = CH // P
HALF_C = DC - P
EXPERTS3, TOP3 = 8, 2
SLOT_TILES = (T * TOP3 + EXPERTS3 * (P - 1)) // P
LN_EPS = 1e-5
COS_EPS = 1e-8
ROUND = 12582912.0
NEG = -1.0e30


class Shared:
    pass


class Order:

    def __init__(self, sem):
        self.sem, self.n, self.loop = sem, 0, None

    def begin(self, index, per_trip):
        self.loop = (index, per_trip, self.n)

    def end(self, trips):
        index, per_trip, base = self.loop
        assert self.n - base == per_trip, (self.n - base, per_trip)
        self.n, self.loop = base + trips * per_trip, None

    def mark(self, ins):
        self.n += 1
        return ins.then_inc(self.sem, 1)

    def wait(self, eng):
        eng.wait_ge(self.sem, self.n if self.loop is None else self.loop[0] * self.loop[1] + self.n)

    def step(self, eng, ins):
        self.mark(ins)
        self.wait(eng)


def stage(emit):
    def scoped(K):
        taken = []

        def take(name):
            taken.append(K.nc.alloc_semaphore(name=name))
            return taken[-1]
        outer, K.sem = K.sem, take
        emit(K)
        K.sem = outer
        K.nc.clear_and_free_semaphores(taken)
        K.nc.all_engine_barrier()
    return scoped


def load_rows(eng, dst, src, sem):
    rows = src.shape[0]
    full = rows // P
    eng.dma_start(dst[:, 0:full, :], src[0:full * P, :].rearrange("(k p) n -> p k n", p=P)).then_inc(sem, 16)
    if rows % P:
        eng.dma_start(dst[0:rows % P, full, :], src[full * P:rows, :]).then_inc(sem, 16)
        return 32
    return 16


def start(K):
    nc, a = K.nc, K.a
    loaded, id0, zero_ok = K.sem("start_loaded"), K.sem("start_ident"), K.sem("start_zero")
    with nc.Block() as block:
        @block.sync
        def _(sp):
            sp.dma_start(K.X[:], a["x"].rearrange("b (h p) d -> p (b h) d", p=P)).then_inc(loaded, 16)
            load_rows(sp, K.CT, a["ctxT"], K.ctx_loaded)
            sp.dma_start(K.CT[HALF_C:P, 1, :], a["ctxT"][P:DC, :]).then_inc(K.ctx_loaded, 16)

            sp.wait_ge(zero_ok, 1)
            sp.dma_start(K.slots.rearrange("(i p) d -> p i d", p=P),
                         K.zero[:].unsqueeze(1).to_broadcast([P, SLOT_TILES, D])).then_inc(K.slots_zeroed, 16)
            sp.wait_ge(loaded, 16)

        @block.vector
        def _(dve):
            dve.memset(K.zero[:], 0.0).then_inc(zero_ok, 1)

        @block.gpsimd
        def _(pool):
            pool.memset(K.ident[:], 0.0).then_inc(id0, 1)
            pool.memset(K.ones[:], 1.0)
            pool.memset(K.round[:], ROUND)
            pool.wait_ge(id0, 1)
            pool.affine_select(out=K.ident[:], in_=K.ident[:], compare_op=ALU.not_equal, fill=1.0, base=0,
                               pattern=[[-1, P]], channel_multiplier=1).then_inc(id0, 1)
            pool.wait_ge(id0, 2)
            pool.tensor_copy(K.identb[:], K.ident[:])


def finish(K):
    stored = K.sem("stored")
    with K.nc.Block() as block:
        @block.sync
        def _(sp):
            sp.dma_start(K.a["out"].rearrange("b (h p) d -> p (b h) d", p=P), K.X[:]).then_inc(stored, 16)
            sp.wait_ge(stored, 16)


def token_stats(K, eng, t):
    return eng.bn_stats(K.stats[:, ds(t, 1), :], K.X[:, ds(t, 1), :])


class Normaliser:

    def __init__(self, K, name, ctx):
        self.K = K
        small = ctx.enter_context(K.nc.sbuf_tensor(f"{name}_small", [P, 6, NT], F32))
        self.mean2, self.dif, self.var, self.std, self.rstd, self.nmr = (small[:, i, :] for i in range(6))
        self.counted, self.coef_ok, self.std_ok = (K.sem(f"{name}_{x}") for x in ("stats", "coef", "std"))

    def vector(self, dve, have_stats):
        K, o = self.K, self.K.dve_order
        if not have_stats:
            with dve.Fori(0, NT // TPC) as g:
                for j in range(TPC):
                    token_stats(K, dve, g * TPC + j).then_inc(self.counted, 1)
            dve.wait_ge(self.counted, NT)
        me, mo, ve, vo = (K.stats[:, :, i] for i in (1, 4, 2, 5))
        o.mark(dve.tensor_tensor(self.mean2, me, mo, ALU.add))
        o.mark(dve.tensor_tensor(self.dif, me, mo, ALU.subtract))
        o.step(dve, dve.tensor_tensor(self.var, ve, vo, ALU.add))
        o.mark(dve.tensor_scalar(self.var, self.var, 1.0 / D, LN_EPS, ALU.mult, ALU.add))
        o.step(dve, dve.scalar_tensor_tensor(self.dif, self.dif, 0.25, self.dif, ALU.mult, ALU.mult))
        dve.tensor_tensor(self.var, self.var, self.dif, ALU.add).then_inc(self.coef_ok, 1)
        dve.wait_ge(self.std_ok, 1)
        o.step(dve, dve.reciprocal(self.rstd, self.std))
        dve.scalar_tensor_tensor(self.nmr, self.mean2, -0.5, self.rstd, ALU.mult, ALU.mult).then_inc(self.coef_ok, 1)

    def scalar(self, act):
        act.wait_ge(self.coef_ok, 1)
        act.activation(self.std, self.var, ACT.Sqrt).then_inc(self.std_ok, 1)

    def factors(self, t):
        return self.rstd[:, ds(t, 1)], self.nmr[:, ds(t, 1)]


def layernorm(K, name, load=None, keep=None, have_stats=False):
    nc, X, XT, bank = K.nc, K.X, K.XT, K.bank
    G = TPC
    U = 1 if keep is not None else 2
    with ExitStack() as ctx:
        norm = Normaliser(K, name, ctx)
        xn = ctx.enter_context(nc.sbuf_tensor(name + "_xn", [P, U, G, D], F32))
        xn_ready, t_done, t_read, kept = (K.sem(f"{name}_{x}") for x in ("xn", "tdone", "tread", "kept"))

        def groups(eng, body):
            with eng.Fori(0, NT // G // U) as trip:
                for u in range(U):
                    body(trip * U + u, u)

        with nc.Block() as block:
            if load:
                @block.sync
                def _(sp):
                    load(sp)

            if keep is not None:
                @block.gpsimd
                def _(pool):
                    def body(g, u):
                        pool.wait_ge(xn_ready, G * (g + 1))
                        pool.tensor_copy(keep[:, ds(g * G, G), :], xn[:, u, :, :]).then_inc(kept, 1)
                    groups(pool, body)

            @block.vector
            def _(dve):
                norm.vector(dve, have_stats)
                dve.wait_ge(norm.coef_ok, 2)

                def body(g, u):
                    dve.wait_ge(t_done, KD * g)
                    if keep is not None:
                        dve.wait_ge(kept, g)
                    for j in range(G):
                        rstd, nmr = norm.factors(g * G + j)
                        dve.tensor_scalar(xn[:, u, j, :], X[:, ds(g * G + j, 1), :].rearrange("p a d -> p (a d)"), rstd, nmr,
                                          ALU.mult, ALU.add).then_inc(xn_ready, 1)
                groups(dve, body)

            @block.scalar
            def _(act):
                if U > 1:
                    act.sem_inc(t_done, KD * (U - 1))
                    act.sem_inc(t_read, KD * (U - 1))
                norm.scalar(act)

                def body(g, u):
                    for k in range(KD):
                        act.wait_ge(t_done, KD * (g + U - 1) + k + 1)
                        act.activation(XT[:, k, ds(g * CH, CH)], bank[u * KD + k][:], ACT.Copy).then_inc(t_read, 1)
                groups(act, body)

            @block.tensor
            def _(pe):
                def body(g, u):
                    pe.wait_ge(xn_ready, G * (g + 1))
                    pe.wait_ge(t_read, KD * g)
                    for k in range(KD):
                        for j in range(G):
                            last = pe.transpose(bank[u * KD + k][:, j * P:(j + 1) * P], xn[:, u, j, k * P:(k + 1) * P], K.ident[:])
                        last.then_inc(t_done, 1)
                groups(pe, body)


def layernorm_quant(K, name, XQT, inv127, load=None, have_stats=False):
    nc, X = K.nc, K.X
    G = TPC
    with ExitStack() as ctx:
        def sb(n, shape, dt=F32):
            return ctx.enter_context(nc.sbuf_tensor(f"{name}_{n}", shape, dt))
        norm = Normaliser(K, name, ctx)
        xn, xr, xq = sb("xn", [P, 2, G, D]), sb("xr", [P, G, D]), sb("xq", [P, G, D], BF16)
        amax, scl = sb("amax", [P, G]), sb("scl", [P, G])
        xn_ready, q_ready, t_done, t_read = (K.sem(f"{name}_{x}") for x in ("xn", "q", "tdone", "tread"))
        with nc.Block() as block:
            @block.sync
            def _(sp):
                load(sp)

            @block.vector
            def _(dve):
                o = K.dve_order
                norm.vector(dve, have_stats)
                with dve.Fori(0, NT // G // 2) as trip:
                    o.begin(trip, 2 * 8)
                    for u in range(2):
                        g = trip * 2 + u
                        dve.wait_ge(xn_ready, G * (g + 1))
                        o.step(dve, dve.tensor_reduce(amax[:], xn[:, u, :, :], AX, ALU.max, apply_absolute_value=True))
                        o.step(dve, dve.tensor_scalar(amax[:], amax[:], 1e-5, 1.0 / 127.0, ALU.max, ALU.mult))
                        o.mark(dve.tensor_copy(inv127[:, ds(g * G, G)], amax[:]))
                        o.step(dve, dve.reciprocal(scl[:], amax[:]))
                        for j in range(G):
                            o.mark(dve.tensor_scalar(xr[:, j, :], xn[:, u, j, :], scl[:, j:j + 1], ROUND, ALU.mult, ALU.add))
                        o.wait(dve)
                        dve.wait_ge(t_done, KD * g)
                        dve.tensor_scalar(xq[:], xr[:], ROUND, None, ALU.subtract).then_inc(q_ready, 1)
                        dve.wait_ge(q_ready, g + 2)
                    o.end(NT // G // 2)

            @block.scalar
            def _(act):
                act.sem_inc(q_ready, 1)
                norm.scalar(act)
                act.wait_ge(norm.coef_ok, 2)

                def normalise(g, u):
                    act.wait_ge(q_ready, g)
                    for j in range(G):
                        rstd, nmr = norm.factors(g * G + j)
                        act.activation(xn[:, u, j, :], X[:, ds(g * G + j, 1), :], ACT.Identity, bias=nmr, scale=rstd).then_inc(xn_ready, 1)

                def copy_turned(g):
                    for k in range(KD):
                        act.wait_ge(t_done, KD * g + k + 1)
                        act.activation(XQT[:, k, ds(g * CH, CH)], K.bank[k][:, 0:CH // 2].bitcast(BF16), ACT.Copy).then_inc(t_read, 1)
                normalise(0, 0)
                for g in range(1, NT // G):
                    normalise(g, g % 2)
                    copy_turned(g - 1)
                copy_turned(NT // G - 1)

            @block.tensor
            def _(pe):
                with pe.Fori(0, NT // G) as g:
                    pe.wait_ge(q_ready, g + 2)
                    pe.wait_ge(t_read, KD * g)
                    for k in range(KD):
                        out = K.bank[k][:, 0:CH // 2].bitcast(BF16)
                        for j in range(G):
                            last = pe.transpose(out[:, j * P:(j + 1) * P], xq[:, j, k * P:(k + 1) * P], K.identb[:])
                        last.then_inc(t_done, 1)


TERNARY = [("L1_ffn_w_gateT", D, 1024), ("L1_ffn_w_upT", D, 1024), ("L1_ffn_w_downT", 1024, D),
           ("L3_xattn_W_d2vT", DC, D), ("L3_xattn_W_imgT", D, D), ("L3_xattn_W_txtT", D, D),
           ("L3_xattn_W_att0T", D, P), ("L3_xattn_W_att1T", D, P), ("L3_xattn_W_f1T", 2 * D, 1024), ("L3_xattn_W_f2T", 1024, D)]
TERNARY_AT = [sum(-(-rows // P) * cols for _, rows, cols in TERNARY[:i]) for i in range(len(TERNARY) + 1)]


class TernaryWeights:
    GROUPS = [(0, 2), (2, 8), (8, 10)]
    OWN = 8

    def __init__(self, K, ctx):
        nc, n = K.nc, TERNARY_AT[-1]
        self.K = K
        self.w = ctx.enter_context(nc.sbuf_tensor("tern_w", [P, n], F32))
        self.below, self.q = (ctx.enter_context(nc.sbuf_tensor("tern_" + x, [P, n], BF16)) for x in ("below", "q"))
        self.sums, self.thr = (ctx.enter_context(nc.sbuf_tensor("tern_" + x, [P, w], F32)) for x, w in (("sums", len(TERNARY)), ("thr", 2 * len(TERNARY))))
        self.loaded = [K.sem(f"tern_loaded{i}") for i in range(len(TERNARY))]
        self.zeroed, self.summed, self.total, self.thr_ok, self.below_ok, self.q_ok, self.stored = (
            K.sem("tern_" + x) for x in ("zeroed", "summed", "total", "thr", "below", "q", "stored"))

    def part(self, t, i):
        return t[:, TERNARY_AT[i]:TERNARY_AT[i + 1]]

    def zero_missing_rows(self, dve):
        for i, (_, rows, cols) in enumerate(TERNARY):
            if rows % P:
                dve.memset(self.w[rows % P:P, TERNARY_AT[i + 1] - cols:TERNARY_AT[i + 1]], 0.0).then_inc(self.zeroed, 1)

    def load(self, sp):
        for i, (name, rows, cols) in enumerate(TERNARY):
            load_rows(sp, self.part(self.w, i).rearrange("p (k n) -> p k n", n=cols), self.K.a[name], self.loaded[i])

    def sum(self, act, g):
        for i in range(*self.GROUPS[g]):
            rows = TERNARY[i][1]
            act.wait_ge(self.loaded[i], 16 * (1 + (rows % P > 0)))
            if rows % P:
                act.wait_ge(self.zeroed, 1)
            act.activation(self.part(self.below, i), self.part(self.w, i), ACT.Abs, accum_out=self.sums[:, i:i + 1]).then_inc(self.summed, 1)

    def spread(self, pe, g):
        a, b = self.GROUPS[g]
        pe.wait_ge(self.summed, b)
        pe.matmul(self.K.bank[6][:, a:b], self.K.ones[:], self.sums[:, a:b], start=True, stop=True).then_inc(self.total, 1)

    def scales(self, dve, g):
        K, o = self.K, self.K.dve_order
        dve.wait_ge(self.total, g + 1)
        span = range(*self.GROUPS[g])
        for i in span:
            count = TERNARY[i][1] * TERNARY[i][2]
            o.mark(dve.tensor_scalar(K.wscale[:, i:i + 1], K.bank[6][:, i:i + 1], 1.0 / count, 1e-5, ALU.mult, ALU.max))
        o.wait(dve)
        a, b = self.GROUPS[g]
        n = len(TERNARY)
        dve.tensor_scalar(self.thr[:, a:b], K.wscale[:, a:b], 0.5, None, ALU.mult).then_inc(self.thr_ok, 1)
        dve.tensor_scalar(self.thr[:, n + a:n + b], K.wscale[:, a:b], -0.5, None, ALU.mult).then_inc(self.thr_ok, 1)

    def compare_low(self, eng, i, g):
        eng.wait_ge(self.thr_ok, 2 * (g + 1))
        n = len(TERNARY)
        return eng.tensor_scalar(self.part(self.below, i), self.part(self.w, i), self.thr[:, n + i:n + i + 1], None, ALU.is_lt)

    def low(self, pool, g):
        for i in range(*self.GROUPS[g]):
            if i != self.OWN:
                self.compare_low(pool, i, g).then_inc(self.below_ok, 1)

    def high(self, dve, g):
        o = self.K.dve_order
        for i in range(*self.GROUPS[g]):
            if i == self.OWN:
                o.step(dve, self.compare_low(dve, i, g))
            else:
                dve.wait_ge(self.below_ok, i + 1 - (i > self.OWN))
            dve.scalar_tensor_tensor(self.part(self.q, i), self.part(self.w, i), self.thr[:, i:i + 1], self.part(self.below, i),
                                     ALU.is_gt, ALU.subtract).then_inc(self.q_ok, 1)

    def store(self, sp):
        pieces = [(0, 2), (2, 8), (8, 9), (9, 10)]
        for a, b in pieces:
            sp.wait_ge(self.q_ok, b)
            w = slice(TERNARY_AT[a], TERNARY_AT[b])
            sp.dma_start(self.K.qweights[:, w], self.q[:, w]).then_inc(self.stored, 16)
        sp.wait_ge(self.stored, 16 * len(pieces))


@stage
def l0_cosine(K):
    nc, a, X, XT, CT, bank = K.nc, K.a, K.X, K.XT, K.CT, K.bank
    HV = 128
    with ExitStack() as ctx:
        def sb(n, shape, dt=F32):
            return ctx.enter_context(nc.sbuf_tensor("l0x_" + n, shape, dt))
        wv, wt, bv, bt = sb("wv", [P, KD, HV]), sb("wt", [P, 2, HV]), sb("bv", [P, 1]), sb("bt", [P, 1])
        vT, tT, sq = sb("vT", [P, CH]), sb("tT", [P, CH]), sb("sq", [P, 2, CH])
        norm, rn, lim, cos = sb("norm", [P, 2 * TPC]), sb("rn", [P, 2 * TPC]), sb("lim", [P, TPC, S]), sb("cos", [P, TPC, S])
        loaded = K.sem("l0x_loaded")

        def load(sp):
            load_rows(sp, wv, a["L0_xattn_WvT"], loaded)
            load_rows(sp, wt, a["L0_xattn_WtT"], loaded)
            sp.dma_start(bv[:], a["L0_xattn_bv"].rearrange("(p a) -> p a", a=1)).then_inc(loaded, 16)
            sp.dma_start(bt[:], a["L0_xattn_bt"].rearrange("(p a) -> p a", a=1)).then_inc(loaded, 16)
            ternary.load(sp)
            sp.wait_ge(loaded, 80)
            sp.wait_ge(K.ctx_loaded, 48)
        ternary = TernaryWeights(K, ctx)
        with nc.Block() as block:
            @block.vector
            def _(dve):
                ternary.zero_missing_rows(dve)
        layernorm(K, "ln0x", load)

        proj, sides, norms, roots, recips, dots, added = (
            K.sem("l0x_" + n) for n in ("proj", "sides", "norms", "roots", "recips", "dots", "added"))
        assert len(ternary.GROUPS) == NC - 1
        with nc.Block() as block:
            @block.tensor
            def _(pe):
                for c in range(NC):
                    if c:
                        pe.wait_ge(sides, 4 * c)
                    for k in range(KD):
                        pe.matmul(bank[0][:], wv[:, k, :], XT[:, k, ds(c * CH, CH)], start=k == 0, stop=k == 1)
                    pe.matmul(bank[1][:], wt[:, 0, :], CT[:, 0, ds(c * CH, CH)], start=True, stop=False)
                    pe.matmul(bank[1][:], wt[0:HALF_C, 1, :], CT[0:HALF_C, 1, ds(c * CH, CH)], start=False,
                              stop=True).then_inc(proj, 1)
                    pe.wait_ge(sides, 4 * c + 4)
                    for s in range(2):
                        for j in range(TPC):
                            n = s * TPC + j
                            last = pe.matmul(bank[2][:, n:n + 1], sq[:, s, j * P:(j + 1) * P], K.ones[:, 0:1], start=True, stop=True)
                    last.then_inc(norms, 1)
                    pe.wait_ge(recips, c + 1)
                    if c:
                        pe.wait_ge(added, TPC * c)
                    for j in range(TPC):
                        pe.matmul(bank[3][:, j * P:(j + 1) * P], rn[:, TPC + j:TPC + j + 1].to_broadcast([P, P]),
                                  K.ident[:], start=True, stop=True)
                    for j in range(TPC):
                        b, i = j // 2, j % 2
                        last = pe.matmul(bank[4 + b][:, i * S:(i + 1) * S], vT[:, j * P:(j + 1) * P],
                                         tT[:, b * S:(b + 1) * S], start=True, stop=True)
                    last.then_inc(dots, 1)
                    if c < NC - 1:
                        ternary.spread(pe, c)

            @block.scalar
            def _(act):
                ternary.sum(act, 0)
                for c in range(NC):
                    act.wait_ge(proj, c + 1)
                    if c:
                        act.wait_ge(dots, c)
                    act.activation(sq[:, 0, :], bank[0][:], ACT.Square, bias=bv[:]).then_inc(sides, 1)
                    act.activation(sq[:, 1, :], bank[1][:], ACT.Square, bias=bt[:]).then_inc(sides, 1)
                    act.activation(vT[:], bank[0][:], ACT.Identity, bias=bv[:]).then_inc(sides, 1)
                    act.activation(tT[:], bank[1][:], ACT.Identity, bias=bt[:]).then_inc(sides, 1)
                    act.wait_ge(norms, c + 1)
                    act.activation(norm[:], bank[2][:, 0:2 * TPC], ACT.Sqrt).then_inc(roots, 1)
                    if c < NC - 2:
                        ternary.sum(act, c + 1)

            @block.vector
            def _(dve):
                o = K.dve_order
                for c in range(NC):
                    dve.wait_ge(roots, c + 1)
                    dve.reciprocal(rn[:], norm[:]).then_inc(recips, 1)
                    if c:
                        ternary.high(dve, c - 1)
                    dve.wait_ge(dots, c + 1)
                    for j in range(TPC):
                        b = j // 2
                        o.mark(dve.tensor_scalar(lim[:, j, :], bank[3][:, b * S:(b + 1) * S], rn[:, j:j + 1],
                                                 1.0 / COS_EPS, ALU.mult, ALU.min))
                    o.wait(dve)
                    for j in range(TPC):
                        b, i = j // 2, j % 2
                        o.mark(dve.tensor_tensor(cos[:, j, :], bank[4 + b][:, i * S:(i + 1) * S], lim[:, j, :], ALU.mult))
                    o.wait(dve)
                    for j in range(TPC):
                        xt = X[:, ds(c * TPC + j, 1), :]
                        dve.tensor_tensor(xt, xt, cos[:, j:j + 1, :], ALU.add).then_inc(added, 1)
                    for j in range(TPC):
                        dve.wait_ge(added, c * TPC + j + 1)
                        token_stats(K, dve, c * TPC + j)
                    if c < NC - 1:
                        ternary.scales(dve, c)

            @block.gpsimd
            def _(pool):
                for g in range(NC - 1):
                    ternary.low(pool, g)

            @block.sync
            def _(sp):
                ternary.store(sp)


def select_top(K, dve, o, vals, top, rep, mask, E, k):
    n = vals.shape[1]
    o.mark(dve.memset(K.carry[:], 0.0))
    for t in range(n):
        o.mark(dve.max(top[:, t, :], vals[:, t, :]))
    o.wait(dve)
    o.step(dve, dve.memset(top[:, :, k:8], NEG))
    o.mark(dve.memset(K.carry[:], 0.0))
    for t in range(n):
        o.mark(dve.match_replace(out=rep[:, t, :], in_to_replace=top[:, t, :], in_values=vals[:, t, :], imm_value=2 * NEG))
    o.wait(dve)
    o.step(dve, dve.tensor_tensor(mask, vals[:, :, 0:E], rep[:, :, 0:E], ALU.is_gt))


def router(K, name, E, k, w, bias, gates, mask, over_all, split=None):
    nc, XT, bank = K.nc, K.XT, K.bank
    with ExitStack() as ctx:
        def sb(n, shape, dt=F32):
            return ctx.enter_context(nc.sbuf_tensor(f"{name}_{n}", shape, dt))
        W = E + 8 - k
        lg, vals, top, rep = sb("lg", [P, NT, E]), sb("vals", [P, NT, W]), sb("top", [P, NT, 8]), sb("rep", [P, NT, W])
        ex, mx, sm = sb("ex", [P, NT, E]), sb("mx", [P, NT, 1]), sb("sm", [P, NT, 1])
        if mask is None:
            mask = sb("mask", [P, NT, E])[:]
        logits, sh, xp, hi = (K.sem(f"{name}_{n}") for n in ("logits", "shifted", "exp", "hi"))
        with nc.Block() as block:
            @block.tensor
            def _(pe):
                for t in range(NT):
                    for kk in range(KD):
                        last = pe.matmul(bank[0][:, t * E:(t + 1) * E], XT[:, kk, t * P:(t + 1) * P], w[:, kk, :], start=kk == 0, stop=kk == 1)
                last.then_inc(logits, 1)

            @block.scalar
            def _(act):
                if split:
                    for kk in range(KD):
                        act.activation(split[0][:, kk, :], XT[:, kk, :], ACT.Copy).then_inc(hi, 1)
                act.wait_ge(sh, 1)
                act.activation(ex[:], ex[:], ACT.Exp).then_inc(xp, 1)

            if split:
                @block.gpsimd
                def _(pool):
                    for kk in range(KD):
                        pool.wait_ge(hi, kk + 1)
                        pool.tensor_tensor(split[1][:, kk, :], XT[:, kk, :], split[0][:, kk, :].bitcast(F32), ALU.subtract)

            @block.vector
            def _(dve):
                o = K.dve_order
                every = [P, NT, E]
                o.mark(dve.memset(vals[:, :, E:W], NEG))
                dve.wait_ge(logits, 1)
                raw = bank[0][:, 0:NT * E].rearrange("p (t e) -> p t e", e=E)
                if bias is None:
                    o.step(dve, dve.tensor_copy(lg[:], raw))
                else:
                    o.step(dve, dve.tensor_tensor(lg[:], raw, bias.unsqueeze(1).to_broadcast(every), ALU.add))
                o.step(dve, dve.tensor_reduce(mx[:], lg[:], AX, ALU.max))
                dve.tensor_tensor(ex[:], lg[:], mx[:].to_broadcast(every), ALU.subtract).then_inc(sh, 1)
                if over_all:
                    dve.wait_ge(xp, 1)
                    o.step(dve, dve.tensor_reduce(sm[:], ex[:], AX, ALU.add))
                    o.step(dve, dve.reciprocal(sm[:], sm[:]))
                    o.step(dve, dve.tensor_tensor(vals[:, :, 0:E], ex[:], sm[:].to_broadcast(every), ALU.mult))
                    select_top(K, dve, o, vals, top, rep, mask, E, k)
                    dve.tensor_tensor(gates, vals[:, :, 0:E], mask, ALU.mult)
                else:
                    o.step(dve, dve.tensor_copy(vals[:, :, 0:E], lg[:]))
                    select_top(K, dve, o, vals, top, rep, mask, E, k)
                    dve.wait_ge(xp, 1)
                    o.step(dve, dve.tensor_tensor(ex[:], ex[:], mask, ALU.mult))
                    o.step(dve, dve.tensor_reduce(sm[:], ex[:], AX, ALU.add))
                    o.step(dve, dve.reciprocal(sm[:], sm[:]))
                    dve.tensor_tensor(gates, ex[:], sm[:].to_broadcast(every), ALU.mult)


def small_experts(K, name, E, XH, XL, up, down, gates):
    nc, X, bank = K.nc, K.X, K.bank
    YB = bank[4:8]
    with ExitStack() as ctx:
        def sb(n, shape, dt=F32):
            return ctx.enter_context(nc.sbuf_tensor(f"{name}_{n}", shape, dt))
        wu, wd = [sb(f"wu{s}", [P, D]) for s in range(2)], [sb(f"wd{s}", [P, D]) for s in range(2)]
        wu_r = [[sb(f"wu{part}{s}", [P, D], F32R) for part in ("hi", "lo")] for s in range(2)]
        wd_r = [[sb(f"wd{part}{s}", [P, D], F32R) for part in ("hi", "lo")] for s in range(2)]
        h, h_hi, h_lo = sb("h", [P, 2, CH]), sb("hhi", [P, 2, CH], F32R), sb("hlo", [P, 2, CH], F32R)
        up_done, gelu_done, hi_done, lo_done, y_done, added, w_hi, w_ok = (
            K.sem(f"{name}_{n}") for n in ("updone", "gelu", "hi", "lo", "ydone", "added", "whi", "wok"))
        loaded = [K.sem(f"{name}_loaded{s}") for s in range(2)]

        def units(eng, body, lead=None):
            if lead:
                lead(0, 0, 0, 0)

            def pair_of(pair, last):
                for i in range(2 * NC):
                    s, c = divmod(i, NC)
                    if lead and not (last and i == 2 * NC - 1):
                        s1, c1 = divmod((i + 1) % (2 * NC), NC)
                        lead(pair + (i + 1) // (2 * NC), s1, c1, pair * (2 * NC) + i + 1)
                    body(pair, s, c, pair * (2 * NC) + i)
            with eng.Fori(0, E // 2 - 1) as pair:
                pair_of(pair, False)
            pair_of(E // 2 - 1, True)

        with nc.Block() as block:
            @block.sync
            def _(sp):
                def load(e, s):
                    sp.dma_start(wu[s][:].rearrange("p (k n) -> p k n", k=KD), up[ds(e, 1), :, :].rearrange("e (k p) n -> p (e k) n", p=P)).then_inc(loaded[s], 16)
                    sp.dma_start(wd[s][:], down[ds(e, 1), :, :].rearrange("e p n -> p (e n)")).then_inc(loaded[s], 16)
                for s in range(2):
                    load(s, s)
                with sp.Fori(0, E // 2 - 1) as pair:
                    for s in range(2):
                        sp.wait_ge(w_ok, 2 * (pair * 2 + s + 1))
                        load(pair * 2 + 2 + s, s)

            @block.gpsimd
            def _(pool):
                pool.sem_inc(y_done, 2)

                def split(pair, s):
                    e = pair * 2 + s
                    pool.wait_ge(loaded[s], 32 * (pair + 1))
                    if not isinstance(pair, int) or pair > 0:
                        pool.wait_ge(y_done, NC * (e - 1) + 2)
                    pool.tensor_tensor(wu_r[s][0][:], wu[s][:], K.zero[:], ALU.add).then_inc(w_hi, 1)
                    pool.tensor_tensor(wd_r[s][0][:], wd[s][:], K.zero[:], ALU.add).then_inc(w_hi, 1)
                    pool.wait_ge(w_hi, 2 * (e + 1))
                    pool.tensor_tensor(wu_r[s][1][:], wu[s][:], wu_r[s][0][:].bitcast(F32), ALU.subtract).then_inc(w_ok, 1)
                    pool.tensor_tensor(wd_r[s][1][:], wd[s][:], wd_r[s][0][:].bitcast(F32), ALU.subtract).then_inc(w_ok, 1)
                for s in range(2):
                    split(0, s)
                with pool.Fori(1, E // 2) as pair:
                    for s in range(2):
                        split(pair, s)

            @block.tensor
            def _(pe):
                def hidden(pair, s, c, n):
                    if c == 0:
                        pe.wait_ge(w_ok, 2 * (pair * 2 + s + 1))
                    pe.wait_ge(gelu_done, n + 1)
                    terms = [(w, x, k) for w, x in ((0, XH), (1, XH), (0, XL)) for k in range(KD)]
                    for i, (w, x, k) in enumerate(terms):
                        last = pe.matmul(bank[c % 2][:], wu_r[s][w][:, k * P:(k + 1) * P], x[:, k, c * CH:(c + 1) * CH],
                                         start=i == 0, stop=i == len(terms) - 1)
                    last.then_inc(up_done, 1)

                def outputs(pair, s, c, n):
                    pe.wait_ge(added, TPC * (n + 1))
                    pe.wait_ge(hi_done, n + 1)
                    pe.wait_ge(lo_done, n + 3)
                    for j in range(TPC):
                        y = YB[c % 2 * 2 + j // 2][:, j % 2 * D:(j % 2 + 1) * D]
                        w = slice(j * P, (j + 1) * P)
                        pe.matmul(y, h_hi[:, c % 2, w], wd_r[s][0][:], start=True, stop=False)
                        pe.matmul(y, h_hi[:, c % 2, w], wd_r[s][1][:], start=False, stop=False)
                        last = pe.matmul(y, h_lo[:, c % 2, w], wd_r[s][0][:], start=False, stop=True)
                    last.then_inc(y_done, 1)
                units(pe, outputs, hidden)

            @block.scalar
            def _(act):
                act.sem_inc(gelu_done, 2)

                def body(pair, s, c, n):
                    act.wait_ge(up_done, n + 1)
                    act.wait_ge(lo_done, n + 1)
                    act.activation(h[:, c % 2, :], bank[c % 2][:], ACT.Gelu).then_inc(gelu_done, 1)
                    act.wait_ge(gelu_done, n + 3)
                    act.wait_ge(y_done, n + 1)
                    act.activation(h_hi[:, c % 2, :], h[:, c % 2, :], ACT.Copy).then_inc(hi_done, 1)
                units(act, body)

            @block.vector
            def _(dve):
                dve.sem_inc(added, 2 * TPC)
                dve.sem_inc(lo_done, 2)

                def rest(pair, s, c, n):
                    dve.wait_ge(hi_done, n + 1)
                    dve.wait_ge(y_done, n + 1)
                    dve.tensor_tensor(h_lo[:, c % 2, :], h[:, c % 2, :], h_hi[:, c % 2, :].bitcast(F32), ALU.subtract).then_inc(lo_done, 1)

                def add(pair, s, c, n):
                    dve.wait_ge(y_done, n + 3)
                    dve.wait_ge(added, TPC * (n + 1))
                    for j in range(TPC):
                        t = c * TPC + j
                        dve.scalar_tensor_tensor(X[:, t, :], YB[c % 2 * 2 + j // 2][:, j % 2 * D:(j % 2 + 1) * D], gates(t, pair * 2 + s), X[:, t, :],
                                                 ALU.mult, ALU.add).then_inc(added, 1)
                    if isinstance(pair, int) and (pair, s) == (E // 2 - 1, 1):
                        dve.wait_ge(added, TPC * (n + 3))
                        for j in range(TPC):
                            token_stats(K, dve, c * TPC + j)
                units(dve, add, rest)


@stage
def l0_ffn(K):
    nc, a = K.nc, K.a
    E, NS = 16, 2
    with ExitStack() as ctx:
        w = ctx.enter_context(nc.sbuf_tensor("l0f_wr", [P, KD, E], F32))
        gates = ctx.enter_context(nc.sbuf_tensor("l0f_gates", [P, NT, NS + E], F32))
        XH, XL = (ctx.enter_context(nc.sbuf_tensor("l0f_" + n, [P, KD, T], F32R)) for n in ("xh", "xl"))
        loaded = K.sem("l0f_loaded")

        def load(sp):
            load_rows(sp, w, a["L0_ffn_router_wT"], loaded)
            sp.wait_ge(loaded, 16)
        layernorm(K, "ln0f", load, have_stats=K.first < 1)
        with nc.Block() as block:
            @block.gpsimd
            def _(pool):
                pool.memset(gates[:, :, 0:NS], 1.0)
        router(K, "l0r", E, 4, w, None, gates[:, :, NS:NS + E], None, True, split=(XH, XL))
        small_experts(K, "l0e", NS + E, XH, XL, a["L0_ffn_upT"], a["L0_ffn_downT"],
                      lambda t, e: gates[:, t, ds(e, 1)])


def split_weights(K, name, weights):
    nc = K.nc
    hi_ok, lo_ok = K.sem(name + "_hi"), K.sem(name + "_lo")
    tiles = [(w[:, k, :], hi[:, k, :], lo[:, k, :], stacked and k == 1)
             for w, (hi, lo), stacked in weights for k in range(w.shape[1])]
    with nc.Block() as block:
        @block.scalar
        def _(act):
            for w, hi, _, _ in tiles:
                act.activation(hi, w, ACT.Copy).then_inc(hi_ok, 1)
            act.wait_ge(lo_ok, len(tiles))
            for w, _, lo, stacked in tiles:
                if stacked:
                    for c in range(0, lo.shape[1], D):
                        act.activation(lo[HALF_C:P, c:c + D], K.zero[HALF_C:P, :], ACT.Copy)

        def rests(eng, mine):
            for n in [i for i in range(len(tiles)) if mine(i)]:
                w, hi, lo, _ = tiles[n]
                eng.wait_ge(hi_ok, n + 1)
                eng.tensor_tensor(lo, w, hi.bitcast(F32), ALU.subtract).then_inc(lo_ok, 1)

        @block.vector
        def _(dve):
            rests(dve, lambda i: i % 4 != 3)

        @block.gpsimd
        def _(pool):
            rests(pool, lambda i: i % 4 == 3)


def cross_attention(K, name, H, wq_d, wk_d, wv_d, wo_d, bo_d, have_stats):
    nc, a, X, XT, CT, bank = K.nc, K.a, K.X, K.XT, K.CT, K.bank
    DH = 64
    HP, G, QT = H // 2, H // 8, S // P
    Q = HP + 2 * G
    R = 2 * G + 1
    sc, tp, ob, pj = bank[0:3], bank[3], bank[4:6], bank[6:8]
    L = len(sc)
    with ExitStack() as ctx:
        def sb(n, shape, dt=F32):
            return ctx.enter_context(nc.sbuf_tensor(f"{name}_{n}", shape, dt))
        HD = H * DH
        wq, wk, wv, wo = ([sb(n + part, [P, kt, cols], F32R) for part in ("hi", "lo")]
                          for n, kt, cols in (("wq", KD, HD), ("wk", 2, HD), ("wv", 2, HD), ("wo", HP, D)))
        bo = sb("bo", [P, D])
        loaded = K.sem(name + "_loaded")
        with ExitStack() as wctx:
            raw = [wctx.enter_context(nc.sbuf_tensor(f"{name}_{n}", list(w[0].shape), F32)) for n, w in (("wq", wq), ("wk", wk), ("wv", wv), ("wo", wo))]

            def load(sp):
                n = 0
                for w, src in zip(raw, (wq_d, wk_d, wv_d, wo_d)):
                    n += load_rows(sp, w, src, loaded)
                    if src.shape[0] == DC:
                        sp.dma_start(w[HALF_C:P, 1, :], src[P:DC, :]).then_inc(loaded, 16)
                        n += 16
                sp.dma_start(bo[:], bo_d.rearrange("(a n) -> a n", a=1).partition_broadcast(P)).then_inc(loaded, 16)
                sp.wait_ge(loaded, n + 16)
            layernorm(K, name + "_ln", load, have_stats=have_stats)
            split_weights(K, name + "_split", list(zip(raw, (wq, wk, wv, wo), (False, True, True, False))))
        x, c = sb("x", [P, KD, S]), sb("c", [P, 2, S])
        xhi, xlo, chi, clo = (sb(n, [P, kt, S], F32R) for n, kt in (("xhi", KD), ("xlo", KD), ("chi", 2), ("clo", 1)))
        qk = sb("qk", [P, HP, 3 * S])
        v = sb("v", [P, 2, H * DH])
        nmax = sb("nmax", [P, L, QT])
        pr = sb("pr", [P, L, QT, S])
        pt = sb("pt", [P, 2, 2 * S])
        sums, rsum = sb("sums", [P, QT, H]), sb("rsum", [P, QT, 8])
        o, tmp = sb("o", [P, QT, H * DH]), sb("tmp", [P, QT, D])
        oT = [sb("oT" + part, [P, QT, HP, P], F32R) for part in ("hi", "lo")]

        in_copied, in_hi, in_ready, oT_hi = (K.sem(f"{name}_{x}") for x in ("incopied", "inhi", "inready", "othi"))
        pj_done, pj_read = (K.sem(f"{name}_{x}") for x in ("pjdone", "pjread"))
        s_done, max_done, exp_done, t_done, pt_ready, pv_done = (
            K.sem(f"{name}_{x}") for x in ("sdone", "maxdone", "expdone", "tdone", "ptready", "pvdone"))
        o_ready = [K.sem(f"{name}_oready{q}") for q in range(QT)]
        o_read = [K.sem(f"{name}_oread{q}") for q in range(QT)]
        rs_done, zeroed, x_added = (K.sem(f"{name}_{x}") for x in ("rsdone", "zeroed", "xadded"))
        EC, RC = 2 * (L - 1), G - 1

        def exps_of_slot(b, h):
            return 2 * (b * H + h) if h >= L else 2 * b * H + EC

        def schedule(eng, qkp, vp, main, drain, tail, order=None, per_trip=0):
            qkp(0)
            vp(0)
            with eng.Fori(0, B - 1) as b:
                if order:
                    order.begin(b, per_trip)
                main(b), qkp(b + 1), drain(b), vp(b + 1), tail(b)
                if order:
                    order.end(B - 1)
            main(B - 1), drain(B - 1), tail(B - 1)

        def nothing(b):
            pass

        with nc.Block() as block:
            @block.gpsimd
            def _(pool):
                def parts(b):
                    zeros = K.zero[:].unsqueeze(1).to_broadcast([P, 2, S])
                    pool.wait_ge(pj_done, Q * b)
                    pool.tensor_copy(x[:], XT[:, :, ds(b * S, S)]).then_inc(in_copied, 1)
                    pool.tensor_copy(c[:], CT[:, :, ds(b * S, S)]).then_inc(in_copied, 1)
                    pool.wait_ge(in_copied, 2 * (b + 1))
                    pool.tensor_tensor(xhi[:], x[:], zeros, ALU.add).then_inc(in_hi, 1)
                    pool.tensor_tensor(chi[:], c[:], zeros, ALU.add).then_inc(in_hi, 1)
                    pool.wait_ge(in_hi, 2 * (b + 1))
                    pool.tensor_tensor(xlo[:], x[:], xhi[:].bitcast(F32), ALU.subtract).then_inc(in_ready, 1)
                    pool.tensor_tensor(clo[:], c[:, 0:1, :], chi[:, 0:1, :].bitcast(F32), ALU.subtract).then_inc(in_ready, 1)
                    pool.wait_ge(in_ready, 3 * b + 2)
                    pool.tensor_tensor(chi[HALF_C:P, 1, :], c[HALF_C:P, 1, :], chi[HALF_C:P, 1, :].bitcast(F32), ALU.subtract).then_inc(in_ready, 1)
                with pool.Fori(0, B) as b:
                    parts(b)

            @block.tensor
            def _(pe):
                def qk_products(b):
                    pe.wait_ge(in_ready, 3 * (b + 1))
                    for p in range(HP):
                        pe.wait_ge(pj_read, b * Q + p)
                        t, w = pj[p % 2], slice(p * P, (p + 1) * P)
                        terms = [(wq[i][:, k, w], x[:, k, :]) for i, x in ((0, xhi), (0, xlo), (1, xhi)) for k in range(KD)]
                        for i, (wt, x) in enumerate(terms):
                            pe.matmul(t[:, 0:S], wt, x, start=i == 0, stop=i == len(terms) - 1)
                        terms = [(0, 0, chi[:, 0, :]), (0, 0, clo[:, 0, :]), (1, 0, chi[:, 0, :]), (0, 1, chi[:, 1, :]), (1, 1, chi[:, 1, :])]
                        for i, (part, k, c) in enumerate(terms):
                            last = pe.matmul(t[:, S:2 * S], wk[part][:, k, w], c, start=i == 0, stop=i == len(terms) - 1)
                        last.then_inc(pj_done, 1)

                def v_products(b):
                    for u in range(2 * G):
                        kt, g = u % 2, u // 2
                        n = HP + u
                        pe.wait_ge(pj_read, b * Q + n)
                        t, w = pj[n % 2], slice(g * CH, (g + 1) * CH)
                        keys = slice(kt * P, (kt + 1) * P)
                        terms = [(0, 0, chi[:, 0, keys]), (0, 0, clo[:, 0, keys]), (1, 0, chi[:, 0, keys]), (0, 1, chi[:, 1, keys]), (1, 1, chi[:, 1, keys])]
                        for i, (part, k, c) in enumerate(terms):
                            last = pe.matmul(t[:], c, wv[part][:, k, w], start=i == 0, stop=i == len(terms) - 1)
                        last.then_inc(pj_done, 1)

                def scores(b, h):
                    n = b * H + h
                    pe.wait_ge(pj_read, b * Q + h // 2 + 2)
                    pe.wait_ge(exp_done, exps_of_slot(b, h))
                    for q in range(QT):
                        last = pe.matmul(sc[h % L][:, q * S:(q + 1) * S], qk[:, h // 2, (h % 2) * S + q * P:(h % 2) * S + (q + 1) * P],
                                         qk[:, h // 2, 2 * S:3 * S], start=True, stop=True)
                    last.then_inc(s_done, 1)

                def turn(b, h):
                    n = b * H + h
                    pe.wait_ge(exp_done, 2 * (n + 1) + EC)
                    pe.wait_ge(pt_ready, n + 1)
                    for kt in range(2):
                        for q in range(QT):
                            c = (kt * QT + q) * P
                            last = pe.transpose(tp[:, c:c + P], pr[:, h % L, q, kt * P:(kt + 1) * P], K.ident[:])
                    last.then_inc(t_done, 1)

                def values(b, h):
                    n = b * H + h
                    g = h // 8
                    pe.wait_ge(pt_ready, n + 2)
                    if h == 0:
                        pe.wait_ge(pj_read, (b + 1) * Q + 1)
                    for q in range(QT):
                        if h % 8 == 0:
                            pe.wait_ge(o_read[q], b * R + g)
                        for kt in range(2):
                            c = (kt * QT + q) * P
                            last = pe.matmul(ob[q][:, (h % 8) * DH:(h % 8 + 1) * DH], pt[:, h % 2, c:c + P],
                                             v[:, kt, h * DH:(h + 1) * DH], start=kt == 0, stop=kt == 1)
                    last.then_inc(pv_done, 1)

                def main(b):
                    for h in range(H):
                        scores(b, h)
                        if h >= 2:
                            turn(b, h - 2)
                        if h >= 3:
                            values(b, h - 3)

                def drain(b):
                    turn(b, H - 2)
                    values(b, H - 3)
                    turn(b, H - 1)
                    values(b, H - 2)
                    values(b, H - 1)

                def tail(b):
                    for g in range(G):
                        for q in range(QT):
                            pe.wait_ge(o_read[q], b * R + G + g)
                            for i in range(4):
                                last = pe.transpose(ob[q][:, i * P:(i + 1) * P], o[:, q, (g * 4 + i) * P:(g * 4 + i + 1) * P], K.ident[:])
                            last.then_inc(o_ready[q], 1)
                    for q in range(QT):
                        pe.wait_ge(o_read[q], b * R + 2 * G)
                        terms = [(x, w, p) for p in range(HP) for x, w in ((0, 0), (0, 1), (1, 0))]
                        for i, (x, w, p) in enumerate(terms):
                            last = pe.matmul(ob[q][:, 0:D], oT[x][:, q, p, :], wo[w][:, p, :], start=i == 0, stop=i == len(terms) - 1)
                        last.then_inc(o_ready[q], 1)
                pe.wait_ge(zeroed, 2)
                schedule(pe, qk_products, v_products, main, drain, tail)

            @block.scalar
            def _(act):
                act.sem_inc(pj_read, 1)
                act.sem_inc(exp_done, EC)

                def copy_qk(b):
                    act.wait_ge(s_done, H * b)
                    for p in range(HP):
                        act.wait_ge(pj_done, b * Q + p + 1)
                        for i in range(2):
                            r = slice(i * DH, (i + 1) * DH)
                            act.activation(qk[r, p, i * S:(i + 1) * S], pj[p % 2][r, 0:S], ACT.Copy, scale=DH ** -0.5)
                        act.activation(qk[:, p, 2 * S:3 * S], pj[p % 2][:, S:2 * S], ACT.Copy).then_inc(pj_read, 1)

                def copy_v(b):
                    act.wait_ge(pv_done, H * b + 1)
                    for u in range(2 * G):
                        n = HP + u
                        act.wait_ge(pj_done, b * Q + n + 1)
                        act.activation(v[:, u % 2, (u // 2) * CH:(u // 2 + 1) * CH], pj[n % 2][:], ACT.Copy).then_inc(pj_read, 1)

                def main(b):
                    for h in range(H):
                        n = b * H + h
                        act.wait_ge(max_done, n + 1)
                        act.wait_ge(t_done, n - 1 if h >= L else b * H + 1)
                        if h % 8 == 0:
                            act.wait_ge(rs_done, b * G + h // 8)
                        for q in range(QT):
                            act.activation(pr[:, h % L, q, :], sc[h % L][:, q * S:(q + 1) * S], ACT.Exp, bias=nmax[:, h % L, q:q + 1],
                                           accum_out=sums[:, q, h:h + 1]).then_inc(exp_done, 1)

                def tail(b):
                    for g in range(G):
                        for q in range(QT):
                            act.wait_ge(o_ready[q], b * (G + 1) + g + 1)
                            act.activation(oT[0][:, q, g * 4:(g + 1) * 4, :], ob[q][:].rearrange("p (i n) -> p i n", i=4), ACT.Copy).then_inc(oT_hi, 1)
                schedule(act, copy_qk, copy_v, main, nothing, tail)

            @block.vector
            def _(dve):
                order = K.dve_order
                for i in range(2):
                    other = slice((1 - i) * DH, (2 - i) * DH)
                    dve.memset(qk[other, :, i * S:(i + 1) * S], 0.0).then_inc(zeroed, 1)
                dve.sem_inc(pt_ready, 1)
                dve.sem_inc(t_done, 1)
                dve.sem_inc(pv_done, 1)
                if RC:
                    dve.sem_inc(rs_done, RC)

                def maximum(b, h):
                    n = b * H + h
                    dve.wait_ge(s_done, n + 1)
                    dve.wait_ge(exp_done, exps_of_slot(b, h))
                    dve.tensor_reduce(nmax[:, h % L, :], sc[h % L][:].rearrange("p (q s) -> p q s", q=QT), AX, ALU.max,
                                      negate=True).then_inc(max_done, 1)

                def copy_turned(b, h):
                    n = b * H + h
                    dve.wait_ge(t_done, n + 2)
                    dve.wait_ge(pv_done, n)
                    dve.tensor_copy(pt[:, h % 2, :], tp[:]).then_inc(pt_ready, 1)

                def normalise(b, g):
                    dve.wait_ge(pv_done, b * H + 8 * (g + 1) + 1)
                    dve.wait_ge(o_read[QT - 1], b * R + g)
                    dve.reciprocal(rsum[:], sums[:, :, g * 8:(g + 1) * 8]).then_inc(rs_done, 1)
                    dve.wait_ge(rs_done, b * G + g + 1 + RC)
                    for q in range(QT):
                        dve.tensor_tensor(o[:, q, g * CH:(g + 1) * CH].rearrange("p (h d) -> p h d", d=DH),
                                          ob[q][:].rearrange("p (h d) -> p h d", d=DH),
                                          rsum[:, q, :].unsqueeze(2).to_broadcast([P, 8, DH]), ALU.mult).then_inc(o_read[q], 1)

                def main(b):
                    for h in range(H):
                        maximum(b, h)
                        if h >= 2:
                            copy_turned(b, h - 2)
                        if h >= 3 and (h - 3) % 8 == 7:
                            normalise(b, (h - 3) // 8)

                def drain(b):
                    copy_turned(b, H - 2)
                    copy_turned(b, H - 1)
                    normalise(b, G - 1)

                def tail(b):
                    for g in range(G):
                        for q in range(QT):
                            dve.wait_ge(oT_hi, b * G * QT + g * QT + q + 1)
                            w = slice(g * 4, (g + 1) * 4)
                            dve.tensor_tensor(oT[1][:, q, w, :], ob[q][:].rearrange("p (i n) -> p i n", i=4), oT[0][:, q, w, :].bitcast(F32),
                                              ALU.subtract).then_inc(o_read[q], 1)
                    for q in range(QT):
                        dve.wait_ge(o_ready[q], b * (G + 1) + G + 1)
                        dve.tensor_tensor(tmp[:, q, :], ob[q][:, 0:D], bo[:], ALU.add).then_inc(o_read[q], 1)
                    for q in range(QT):
                        dve.wait_ge(o_read[q], (b + 1) * R)
                        xt = X[:, ds(b * QT + q, 1), :]
                        dve.tensor_tensor(xt, xt, tmp[:, q:q + 1, :], ALU.add).then_inc(x_added, 1)
                    for q in range(QT):
                        dve.wait_ge(x_added, b * QT + q + 1)
                        token_stats(K, dve, b * QT + q)
                schedule(dve, nothing, nothing, main, drain, tail)


def l1_xattn(K):
    a = K.a
    cross_attention(K, "l1x", 16, a["L1_xattn_Wq"], a["L1_xattn_Wk"], a["L1_xattn_Wv"], a["L1_xattn_Wo"], a["L1_xattn_bo"], K.first < 2)


def l2_xattn(K):
    a = K.a
    cross_attention(K, "l2x", 8, a["L2_xattn_Wq"], a["L2_xattn_Wk"], a["L2_xattn_Wv"], a["L2_xattn_Wo"], a["L2_xattn_bo"], K.first < 4)


@stage
def l1_ffn(K):
    nc, a, X, bank = K.nc, K.a, K.X, K.bank
    N = 1024
    KN = N // P
    with ExitStack() as ctx:
        def sb(n, shape, dt=F32):
            return ctx.enter_context(nc.sbuf_tensor("l1f_" + n, shape, dt))
        q = sb("q", [P, TERNARY_AT[3]], BF16)
        qg, qu, qd = (q[:, TERNARY_AT[i]:TERNARY_AT[i + 1]].rearrange("p (k n) -> p k n", n=TERNARY[i][2]) for i in range(3))
        scale = K.wscale
        XQ, inv = sb("xq_t", [P, KD, T], BF16), sb("inv", [P, NT])
        loaded = K.sem("l1f_loaded")

        def load(sp):
            sp.dma_start(q[:], K.qweights[:, 0:TERNARY_AT[3]]).then_inc(loaded, 16)
            sp.wait_ge(loaded, 16)
        layernorm_quant(K, "l1f_ln", XQ, inv, load, have_stats=K.first < 3)
        sg, su = sb("sg", [P, NT]), sb("su", [P, NT])
        g, h, hq = sb("g", [P, N]), sb("h", [P, N]), sb("hq", [P, N], BF16)
        hT = sb("hT", [P, KN, P], BF16)
        amax, hinv, hscl, down = sb("amax", [P, 1]), sb("hinv", [P, 1]), sb("hscl", [P, 1]), sb("down", [P, 1])
        gate_done, up_done, gate_ok, h_ok, q_ok, turned, hT_ok, y_done, added, scl_ok, hscl_ok, rounded = (
            K.sem("l1f_" + n) for n in ("gate", "up", "gateok", "hok", "qok", "turned", "htok", "ydone", "added", "sclok", "hsclok", "rounded"))
        gb, ub, tb, yb = bank[0:2], bank[2:4], bank[4], bank[5]
        with nc.Block() as block:
            @block.tensor
            def _(pe):
                def products(out, q, t):
                    for half in range(2):
                        for k in range(KD):
                            last = pe.matmul(out[half][:], XQ[:, k, ds(t * P, P)], q[:, k, half * CH:(half + 1) * CH],
                                             start=k == 0, stop=k == KD - 1)
                    return last

                def up_products(t):
                    pe.wait_ge(h_ok, t)
                    products(ub, qu, t).then_inc(up_done, 1)

                def turn(t):
                    pe.wait_ge(q_ok, t + 1)
                    tbf = tb[:].bitcast(BF16)
                    for i in range(KN):
                        last = pe.transpose(tbf[:, i * P:(i + 1) * P], hq[:, i * P:(i + 1) * P], K.identb[:])
                    last.then_inc(turned, 1)

                def gate_products(t):
                    pe.wait_ge(gate_ok, t)
                    products(gb, qg, t).then_inc(gate_done, 1)

                def down_product(t):
                    pe.wait_ge(hT_ok, t + 1)
                    pe.wait_ge(added, t)
                    for i in range(KN):
                        last = pe.matmul(yb[:, 0:D], hT[:, i, :], qd[:, i, :], start=i == 0, stop=i == KN - 1)
                    last.then_inc(y_done, 1)
                products(gb, qg, 0).then_inc(gate_done, 1)
                products(ub, qu, 0).then_inc(up_done, 1)
                gate_products(1)
                with pe.Fori(0, NT - 2) as t:
                    up_products(t + 1)
                    turn(t)
                    gate_products(t + 2)
                    down_product(t)
                up_products(NT - 1)
                turn(NT - 2)
                down_product(NT - 2)
                turn(NT - 1)
                down_product(NT - 1)

            @block.scalar
            def _(act):
                act.wait_ge(scl_ok, 2)

                def gate(t):
                    act.wait_ge(gate_done, t + 1)
                    act.wait_ge(h_ok, t)
                    act.activation(g[:, 0:CH], gb[0][:], ACT.Silu, scale=sg[:, ds(t, 1)])
                    act.activation(g[:, CH:N], gb[1][:], ACT.Silu, scale=sg[:, ds(t, 1)]).then_inc(gate_ok, 1)

                def scale_hidden(t):
                    act.wait_ge(hscl_ok, t + 1)
                    act.activation(h[:], h[:], ACT.Identity, bias=K.round[:], scale=hscl[:]).then_inc(rounded, 1)

                def copy_turned(t):
                    act.wait_ge(turned, t + 1)
                    act.wait_ge(y_done, t)
                    act.activation(hT[:].rearrange("p i n -> p (i n)"), tb[:].bitcast(BF16), ACT.Copy).then_inc(hT_ok, 1)
                gate(0)
                with act.Fori(0, NT - 1) as t:
                    gate(t + 1)
                    scale_hidden(t)
                    copy_turned(t)
                scale_hidden(NT - 1)
                copy_turned(NT - 1)

            @block.vector
            def _(dve):
                o = K.dve_order
                dve.tensor_scalar(sg[:], inv[:], scale[:, 0:1], None, ALU.mult).then_inc(scl_ok, 1)
                dve.tensor_scalar(su[:], inv[:], scale[:, 1:2], None, ALU.mult).then_inc(scl_ok, 1)
                dve.wait_ge(scl_ok, 2)

                def hidden(t):
                    dve.wait_ge(up_done, t + 1)
                    dve.wait_ge(gate_ok, t + 1)
                    for half in range(2):
                        c = slice(half * CH, (half + 1) * CH)
                        ins = dve.scalar_tensor_tensor(h[:, c], ub[half][:], su[:, ds(t, 1)], g[:, c], ALU.mult, ALU.mult)
                    ins.then_inc(h_ok, 1)
                    dve.wait_ge(h_ok, t + 1)
                    o.step(dve, dve.tensor_reduce(amax[:], h[:], AX, ALU.max, apply_absolute_value=True))
                    o.step(dve, dve.tensor_scalar(hinv[:], amax[:], 1e-5, 1.0 / 127.0, ALU.max, ALU.mult))
                    dve.reciprocal(hscl[:], hinv[:]).then_inc(hscl_ok, 1)

                def add_output(t):
                    dve.wait_ge(y_done, t + 1)
                    xt = X[:, ds(t, 1), :].rearrange("p a d -> p (a d)")
                    dve.scalar_tensor_tensor(xt, yb[:, 0:D], down[:], xt, ALU.mult, ALU.add).then_inc(added, 1)

                def quantised(t):
                    dve.wait_ge(rounded, t + 1)
                    dve.wait_ge(turned, t)
                    dve.tensor_scalar(hq[:], h[:], ROUND, None, ALU.subtract).then_inc(q_ok, 1)
                hidden(0)
                dve.tensor_scalar(down[:], hinv[:], scale[:, 2:3], None, ALU.mult)
                quantised(0)
                dve.wait_ge(q_ok, 1)
                with dve.Fori(0, NT - 1) as t:
                    o.begin(t, 2)
                    hidden(t + 1)
                    add_output(t)
                    dve.wait_ge(added, t + 1)
                    dve.tensor_scalar(down[:], hinv[:], scale[:, 2:3], None, ALU.mult)
                    token_stats(K, dve, t)
                    quantised(t + 1)
                    dve.wait_ge(q_ok, t + 2)
                    o.end(NT - 1)
                add_output(NT - 1)
                dve.wait_ge(added, NT)
                token_stats(K, dve, NT - 1)


@stage
def l2_ffn(K):
    nc, a, X, XT, bank = K.nc, K.a, K.X, K.XT, K.bank
    E, INNER, PROJ, TOP = 8, 32, 8, 2
    NH = E * INNER
    N1 = E + NH + E * PROJ
    W = E + 8 - TOP
    with ExitStack() as ctx:
        def sb(n, shape, dt=F32):
            return ctx.enter_context(nc.sbuf_tensor("l2f_" + n, shape, dt))
        wv, w1, w2 = sb("wv", [P, KD, D]), sb("w1", [P, KD, N1]), sb("w2", [P, KD, D])
        bv, b1, b2 = sb("bv", [P, KD]), sb("b1", [P, N1]), sb("b2", [E, D])
        gb, alpha = sb("gb", [P, 2, 2, E]), sb("alpha", [P, 1])
        vT, r, pv2 = sb("vT", [P, 2, KD, CH]), sb("r", [P, TPC, N1]), sb("pv2", [P, TPC, E * PROJ])
        css = sb("css", [P, TPC * E])
        z, zc, mean, var = sb("z", [P, 2, TPC, E]), sb("zc", [P, 2, TPC, E]), sb("mean", [P, 2 * TPC]), sb("var", [P, 2 * TPC])
        vals, top, rep = sb("vals", [P, TPC, W]), sb("top", [P, TPC, 8]), sb("rep", [P, TPC, W])
        mask, ex, sm, we = sb("mask", [P, TPC, E]), sb("ex", [P, TPC, E]), sb("sm", [P, TPC, 1]), sb("we", [P, TPC, E])
        hid, hT, weT = sb("hid", [P, TPC, NH]), sb("hT", [P, 2, CH]), sb("weT", [E, CH])
        loaded = K.sem("l2f_loaded")

        def load(sp):
            n = load_rows(sp, wv, a["L2_ffn_WvT"], loaded) + load_rows(sp, w1, a["L2_ffn_W1cat"], loaded)
            n += load_rows(sp, w2, a["L2_ffn_W2cat"], loaded)
            small = [(bv[:], a["L2_ffn_bv"]), (b1[:, 0:E + NH], a["L2_ffn_b1cat"].partition_broadcast(P)), (b2[:], a["L2_ffn_b2"]),
                     (alpha[:], a["L2_ffn_alpha"].partition_broadcast(P)),
                     (gb[:].rearrange("p a b e -> p (a b e)"), a["L2_ffn_gb"].partition_broadcast(P))]
            for dst, src in small:
                sp.dma_start(dst, src).then_inc(loaded, 16)
            sp.wait_ge(loaded, n + 16 * len(small))
        layernorm(K, "l2f_ln", load, have_stats=K.first < 5)

        names = ("vdone", "vok", "sdone", "rok", "css", "cok", "var", "std", "sh", "xp", "silu", "hok", "turned", "tok", "ydone", "added", "alpha", "sig")
        v_done, v_ok, s_done, r_ok, css_ok, c_ok, var_ok, std_ok, sh, xp, silu, h_ok, turned, t_ok, y_done, added, al, sg = (
            K.sem("l2f_" + n) for n in names)
        with nc.Block() as block:
            @block.tensor
            def _(pe):
                def first_products(c):
                    if c >= 2:
                        pe.wait_ge(added, TPC * (c - 1))
                    for m in range(KD):
                        for k in range(KD):
                            last = pe.matmul(bank[m][:], wv[:, k, m * P:(m + 1) * P], XT[:, k, c * CH:(c + 1) * CH], start=k == 0, stop=k == KD - 1)
                        last.then_inc(v_done, 1)
                    pe.wait_ge(v_ok, KD * (c + 1))
                    if c:
                        pe.wait_ge(r_ok, TPC * c)
                    for j in range(TPC):
                        for k in range(KD):
                            last = pe.matmul(bank[2 + j][:, 0:N1], vT[:, c % 2, k, j * P:(j + 1) * P], w1[:, k, :], start=k == 0, stop=k == KD - 1)
                        last.then_inc(s_done, 1)
                first_products(0)
                for c in range(NC):
                    if c + 1 < NC:
                        first_products(c + 1)
                    else:
                        pe.wait_ge(added, TPC * (NC - 1))
                    pe.wait_ge(h_ok, c + 1)
                    for j in range(TPC):
                        pe.transpose(bank[0][0:E, j * P:(j + 1) * P], we[:, j, :], K.ident[:])
                    for k in range(2):
                        for j in range(TPC):
                            last = pe.transpose(bank[6 + k][:, j * P:(j + 1) * P], hid[:, j, k * P:(k + 1) * P], K.ident[:])
                    last.then_inc(turned, 1)
                    pe.wait_ge(t_ok, 3 * (c + 1))
                    for j in range(TPC):
                        w = slice(j * P, (j + 1) * P)
                        y = bank[j // 2][:, (j % 2) * D:(j % 2 + 1) * D]
                        pe.matmul(y, weT[:, w], b2[:], start=True, stop=False)
                        for k in range(2):
                            pe.matmul(y, hT[:, k, w], w2[:, k, :], start=False, stop=False)
                        for k in range(KD):
                            last = pe.matmul(y[:, k * P:(k + 1) * P], vT[:, c % 2, k, w], K.ident[:], start=False, stop=k == KD - 1)
                        last.then_inc(y_done, 1)

            @block.scalar
            def _(act):
                act.wait_ge(al, 1)
                act.activation(alpha[:], alpha[:], ACT.Sigmoid).then_inc(sg, 1)

                def copy_v(c):
                    if c >= 2:
                        act.wait_ge(y_done, TPC * (c - 1))
                    for m in range(KD):
                        act.wait_ge(v_done, KD * c + m + 1)
                        act.activation(vT[:, c % 2, m, :], bank[m][:], ACT.Identity, bias=bv[:, m:m + 1]).then_inc(v_ok, 1)
                copy_v(0)
                for c in range(NC):
                    act.wait_ge(css_ok, c + 1)
                    act.activation(z[:, 1, :, :].rearrange("p t e -> p (t e)"), css[:], ACT.Sqrt, scale=1.0 / PROJ).then_inc(c_ok, 1)
                    act.wait_ge(var_ok, c + 1)
                    act.activation(var[:], var[:], ACT.Sqrt).then_inc(std_ok, 1)
                    if c + 1 < NC:
                        copy_v(c + 1)
                    act.wait_ge(sh, c + 1)
                    act.activation(ex[:], ex[:], ACT.Exp).then_inc(xp, 1)
                    act.activation(hid[:], r[:, :, E:E + NH], ACT.Silu).then_inc(silu, 1)
                    act.wait_ge(turned, c + 1)
                    act.activation(weT[:], bank[0][0:E, :], ACT.Copy).then_inc(t_ok, 1)
                    act.activation(hT[:, 0, :], bank[6][:], ACT.Copy).then_inc(t_ok, 1)

            @block.vector
            def _(dve):
                o = K.dve_order
                o.mark(dve.memset(vals[:, :, E:W], NEG))
                o.step(dve, dve.memset(b1[:, E + NH:N1], 0.0))
                dve.sem_inc(al, 1)
                dve.wait_ge(sg, 1)
                bc = [P, 2, TPC, E]

                def add_bias(c):
                    for j in range(TPC):
                        dve.wait_ge(s_done, TPC * c + j + 1)
                        dve.tensor_tensor(r[:, j, :], bank[2 + j][:, 0:N1], b1[:], ALU.add).then_inc(r_ok, 1)

                def add_outputs(c):
                    for j in range(TPC):
                        dve.wait_ge(y_done, TPC * (c + 1))
                        xt = X[:, c * TPC + j, :]
                        dve.tensor_tensor(xt, xt, bank[j // 2][:, (j % 2) * D:(j % 2 + 1) * D], ALU.add).then_inc(added, 1)
                    for j in range(TPC):
                        dve.wait_ge(added, TPC * c + j + 1)
                        token_stats(K, dve, c * TPC + j)
                add_bias(0)
                for c in range(NC):
                    dve.wait_ge(r_ok, TPC * (c + 1))
                    pv = r[:, :, E + NH:N1]
                    o.step(dve, dve.tensor_tensor(pv2[:], pv, pv, ALU.mult))
                    dve.tensor_reduce(css[:], pv2[:].rearrange("p t (e q) -> p (t e) q", q=PROJ), AX, ALU.add).then_inc(css_ok, 1)
                    o.step(dve, dve.tensor_copy(z[:, 0, :, :], r[:, :, 0:E]))
                    dve.wait_ge(c_ok, c + 1)
                    zf, zcf = z[:].rearrange("p a t e -> p (a t) e"), zc[:].rearrange("p a t e -> p (a t) e")
                    b8 = [P, 2 * TPC, E]
                    o.step(dve, dve.tensor_reduce(mean[:], zf, AX, ALU.add))
                    o.step(dve, dve.tensor_scalar(mean[:], mean[:], 1.0 / E, None, ALU.mult))
                    o.step(dve, dve.tensor_tensor(zcf, zf, mean[:].unsqueeze(2).to_broadcast(b8), ALU.subtract))
                    o.step(dve, dve.tensor_tensor(zf, zcf, zcf, ALU.mult))
                    o.step(dve, dve.tensor_reduce(var[:], zf, AX, ALU.add))
                    dve.tensor_scalar(var[:], var[:], 1.0 / E, LN_EPS, ALU.mult, ALU.add).then_inc(var_ok, 1)
                    dve.wait_ge(std_ok, c + 1)
                    o.step(dve, dve.reciprocal(var[:], var[:]))
                    o.step(dve, dve.tensor_tensor(zcf, zcf, var[:].unsqueeze(2).to_broadcast(b8), ALU.mult))
                    o.step(dve, dve.tensor_tensor(zc[:], zc[:], gb[:, 0, :, :].unsqueeze(2).to_broadcast(bc), ALU.mult))
                    o.step(dve, dve.tensor_tensor(zc[:], zc[:], gb[:, 1, :, :].unsqueeze(2).to_broadcast(bc), ALU.add))
                    o.step(dve, dve.scalar_tensor_tensor(vals[:, :, 0:E], zc[:, 1, :, :], alpha[:], zc[:, 0, :, :], ALU.mult, ALU.add))
                    select_top(K, dve, o, vals, top, rep, mask[:], E, TOP)
                    dve.tensor_tensor(ex[:], vals[:, :, 0:E], top[:, :, 0:1].to_broadcast([P, TPC, E]), ALU.subtract).then_inc(sh, 1)
                    if c:
                        add_outputs(c - 1)
                    dve.wait_ge(xp, c + 1)
                    o.step(dve, dve.tensor_tensor(ex[:], ex[:], mask[:], ALU.mult))
                    o.step(dve, dve.tensor_reduce(sm[:], ex[:], AX, ALU.add))
                    o.step(dve, dve.reciprocal(sm[:], sm[:]))
                    o.step(dve, dve.tensor_tensor(we[:], ex[:], sm[:].to_broadcast([P, TPC, E]), ALU.mult))
                    dve.wait_ge(silu, c + 1)
                    hv = hid[:].rearrange("p t (e i) -> p (t e) i", i=INNER)
                    dve.tensor_tensor(hv, hv, we[:].rearrange("p t e -> p (t e)").unsqueeze(2).to_broadcast([P, TPC * E, INNER]), ALU.mult).then_inc(h_ok, 1)
                    if c + 1 < NC:
                        add_bias(c + 1)
                    dve.wait_ge(turned, c + 1)
                    dve.tensor_copy(hT[:, 1, :], bank[7][:]).then_inc(t_ok, 1)
                add_outputs(NC - 1)


def global_quant(K, name, items, maxima=None, inverse=None):
    nc = K.nc
    n_i = len(items)
    n_p = sum(len(parts) for parts, _ in items)
    with ExitStack() as ctx:
        def sb(n, shape, dt=F32):
            return ctx.enter_context(nc.sbuf_tensor(f"{name}_{n}", shape, dt))
        part_max, item_max = sb("pmax", [P, n_p]) if maxima is None else maxima, sb("imax", [P, n_i])
        top, inv = sb("top", [n_i, 1]), sb("inv", [P, n_i]) if inverse is None else inverse
        maxed, turned, topped, spread, inv_ok, scaled = (K.sem(f"{name}_{x}") for x in ("maxed", "turned", "topped", "spread", "inv", "scaled"))
        with nc.Block() as block:
            @block.vector
            def _(dve):
                o = K.dve_order
                if maxima is None:
                    o.step(dve, dve.memset(part_max[:], 0.0))
                    n = 0
                    for parts, _ in items:
                        for x, q in parts:
                            o.mark(dve.tensor_reduce(part_max[0:x.shape[0], n:n + 1], x, AX, ALU.max, apply_absolute_value=True))
                            n += 1
                    o.wait(dve)
                n = 0
                for i, (parts, _) in enumerate(items):
                    w = part_max[:, n:n + len(parts)] if maxima is None else maxima
                    dve.tensor_reduce(item_max[:, i:i + 1], w, AX, ALU.max).then_inc(maxed, 1)
                    n += len(parts)
                dve.wait_ge(turned, 1)
                dve.tensor_reduce(top[:], K.bank[0][0:n_i, 0:P], AX, ALU.max).then_inc(topped, 1)
                dve.wait_ge(spread, 1)
                for i, (_, s) in enumerate(items):
                    o.mark(dve.tensor_scalar(s, K.bank[1][:, i:i + 1], 1e-8, 1.0 / 127.0, ALU.max, ALU.mult))
                o.wait(dve)
                for i, (_, s) in enumerate(items):
                    dve.reciprocal(inv[:, i:i + 1], s).then_inc(inv_ok, 1)
                n = 0
                for parts, _ in items:
                    for x, q in parts:
                        n += 1
                        dve.wait_ge(scaled, n)
                        dve.tensor_scalar(q, x, ROUND, None, ALU.subtract)

            @block.tensor
            def _(pe):
                pe.wait_ge(maxed, n_i)
                pe.transpose(K.bank[0][0:n_i, 0:P], item_max[:], K.ident[:]).then_inc(turned, 1)
                pe.wait_ge(topped, 1)
                pe.matmul(K.bank[1][:, 0:n_i], top[:].to_broadcast([n_i, P]), K.ident[0:n_i, 0:n_i], start=True, stop=True).then_inc(spread, 1)

            @block.scalar
            def _(act):
                act.wait_ge(inv_ok, n_i)
                for i, (parts, _) in enumerate(items):
                    for x, q in parts:
                        p = x.shape[0]
                        act.activation(x, x, ACT.Identity, bias=K.round[0:p, :], scale=inv[0:p, i:i + 1]).then_inc(scaled, 1)


def bit_linear(K, name, jobs, relu=False, maxima=None):
    nc = K.nc
    units = [(j, m) for j, job in enumerate(jobs) for m in range(job[3].shape[1])]
    R = min(4, len(units))
    assert len(units) % R == 0
    with ExitStack() as ctx:
        scale = ctx.enter_context(nc.sbuf_tensor(name + "_scale", [P, len(jobs)], F32))
        scale_ok, done, read = K.sem(name + "_scale"), K.sem(name + "_done"), K.sem(name + "_read")
        with nc.Block() as block:
            @block.vector
            def _(dve):
                for j, job in enumerate(jobs):
                    dve.tensor_tensor(scale[:, j:j + 1], job[4], job[5], ALU.mult).then_inc(scale_ok, 1)
                if maxima is not None:
                    out = jobs[0][3]
                    with dve.Fori(0, NC) as c:
                        for m in range(out.shape[1]):
                            dve.wait_ge(read, c * len(units) + m + 1 + R)
                            dve.tensor_reduce(maxima[:, ds(c * out.shape[1] + m, 1)], out[:, m, ds(c * CH, CH)], AX, ALU.max,
                                              apply_absolute_value=True)

            @block.tensor
            def _(pe):
                with pe.Fori(0, NC) as c:
                    for u, (j, m) in enumerate(units):
                        q, qw, rows = jobs[j][:3]
                        pe.wait_ge(read, c * len(units) + u + 1)
                        kts = -(-rows // P)
                        for k in range(kts):
                            p = min(P, rows - k * P)
                            last = pe.matmul(K.bank[u % R][:], qw[0:p, k, m * P:(m + 1) * P], q[0:p, k, ds(c * CH, CH)], start=k == 0, stop=k == kts - 1)
                        last.then_inc(done, 1)

            @block.scalar
            def _(act):
                act.sem_inc(read, R)
                act.wait_ge(scale_ok, len(jobs))
                with act.Fori(0, NC) as c:
                    for u, (j, m) in enumerate(units):
                        out, bias = jobs[j][3], jobs[j][6]
                        act.wait_ge(done, c * len(units) + u + 1)
                        act.activation(out[:, m, ds(c * CH, CH)], K.bank[u % R][:], ACT.Relu if relu else ACT.Identity,
                                       bias=bias[:, m:m + 1], scale=scale[:, j:j + 1]).then_inc(read, 1)


def shared_key_attention(K, name, F, kv, area):
    nc, bank = K.nc, K.bank
    QT, A = S // P, kv.shape[1]
    R, L = 4, 3
    sc, tp, yb, kb_t = bank[0:3], bank[3:5], bank[5:7], bank[7]
    with ExitStack() as ctx:
        def sb(n, shape, dt=F32):
            return ctx.enter_context(nc.sbuf_tensor(f"{name}_{n}", shape, dt))
        nmax, sums, rs = sb("nmax", [P, R, QT]), sb("sums", [P, R, QT]), sb("rs", [P, R, QT])
        pr = area[0].rearrange("p (r q s) -> p r q s", r=R, q=QT)
        pt = area[1].rearrange("p (r s) -> p r s", r=R)
        fs, kb, kt = (area[2][:, at:at + n * w].rearrange("p (r s) -> p r s", r=n) for at, n, w in
                      ((0, 2, S), (2 * S, 2, S), (4 * S, R, S)))
        kb_ok, fs_ok, s_done, k_done, kt_ok, max_ok, exp_ok, rs_ok, pr_ok, t_done, pt_ok, y_done, added = (
            K.sem(f"{name}_{x}") for x in ("kb", "fs", "sdone", "kdone", "kt", "max", "exp", "rs", "pr", "tdone", "pt", "ydone", "added"))

        def exps_of_slot(i, b):
            return 2 * (B * i + b) if b >= L else 2 * B * i + 2 * (L - 1)

        with nc.Block() as block:
            @block.gpsimd
            def _(pool):
                with pool.Fori(0, A) as i:
                    for b in range(B):
                        pool.wait_ge(k_done, B * i + b)
                        pool.tensor_copy(kb[:, b % 2:b % 2 + 1, :], kv[:, ds(i, 1), b * S:(b + 1) * S]).then_inc(kb_ok, 1)

            @block.tensor
            def _(pe):
                def scores(i, b):
                    n = B * i + b
                    pe.wait_ge(kb_ok, n + 1)
                    pe.wait_ge(fs_ok, n + 1)
                    pe.wait_ge(exp_ok, exps_of_slot(i, b))
                    for q in range(QT):
                        last = pe.matmul(sc[b % L][:, q * S:(q + 1) * S], fs[:, b % 2, q * P:(q + 1) * P], kb[:, b % 2, :], start=True, stop=True)
                    last.then_inc(s_done, 1)
                    pe.wait_ge(kt_ok, n)
                    for k in range(2):
                        last = pe.transpose(kb_t[:, k * P:(k + 1) * P], kb[:, b % 2, k * P:(k + 1) * P], K.ident[:])
                    last.then_inc(k_done, 1)

                def turn(i, b):
                    n = B * i + b
                    pe.wait_ge(pr_ok, n + 1)
                    pe.wait_ge(pt_ok, n)
                    for k in range(2):
                        for q in range(QT):
                            c = (k * QT + q) * P
                            last = pe.transpose(tp[b % 2][:, c:c + P], pr[:, b % R, q, k * P:(k + 1) * P], K.ident[:])
                    last.then_inc(t_done, 1)

                def outputs(i, b):
                    n = B * i + b
                    pe.wait_ge(kt_ok, n + 1)
                    pe.wait_ge(pt_ok, n + 2)
                    pe.wait_ge(added, n)
                    for k in range(2):
                        last = pe.matmul(yb[b % 2][:, 0:S], kt[:, b % R, k * P:(k + 1) * P], pt[:, b % R, k * S:(k + 1) * S], start=k == 0, stop=k == 1)
                    last.then_inc(y_done, 1)
                with pe.Fori(0, A) as i:
                    for b in range(B):
                        scores(i, b)
                        if b >= 2:
                            turn(i, b - 2)
                        if b >= 3:
                            outputs(i, b - 3)
                    turn(i, B - 2)
                    outputs(i, B - 3)
                    turn(i, B - 1)
                    outputs(i, B - 2)
                    outputs(i, B - 1)

            @block.scalar
            def _(act):
                act.sem_inc(exp_ok, 2 * (L - 1))

                def exponentials(i, b):
                    n = B * i + b
                    act.wait_ge(max_ok, n + 1)
                    act.wait_ge(t_done, n)
                    for q in range(QT):
                        act.activation(pr[:, b % R, q, :], sc[b % L][:, q * S:(q + 1) * S], ACT.Exp, bias=nmax[:, b % R, q:q + 1],
                                       scale=D ** -0.5, accum_out=sums[:, b % R, q:q + 1]).then_inc(exp_ok, 1)

                def normalise(i, b):
                    act.wait_ge(rs_ok, B * i + b + 1)
                    for q in range(QT):
                        last = act.activation(pr[:, b % R, q, :], pr[:, b % R, q, :], ACT.Identity, scale=rs[:, b % R, q:q + 1])
                    last.then_inc(pr_ok, 1)

                def copy_keys(i, b):
                    n = B * i + b
                    act.wait_ge(k_done, n + 2)
                    act.wait_ge(y_done, n)
                    act.activation(kt[:, b % R, :], kb_t[:, 0:S], ACT.Copy).then_inc(kt_ok, 1)
                with act.Fori(0, A) as i:
                    for b in range(B):
                        exponentials(i, b)
                        if b >= 1:
                            normalise(i, b - 1)
                        copy_keys(i, b)
                    normalise(i, B - 1)

            @block.vector
            def _(dve):
                o = K.dve_order
                dve.sem_inc(t_done, R - 1)
                dve.sem_inc(y_done, R - 1)
                dve.sem_inc(k_done, 1)
                dve.sem_inc(pt_ok, 1)
                dve.sem_inc(added, 1)

                def sum_halves(i, b):
                    dve.wait_ge(s_done, B * i + b - 1) if b >= 2 else dve.wait_ge(s_done, B * i)
                    dve.wait_ge(added, B * i + 1)
                    dve.tensor_tensor(fs[:, b % 2, :], F[:, 0, b * S:(b + 1) * S], F[:, 1, b * S:(b + 1) * S], ALU.add).then_inc(fs_ok, 1)

                def maximum(i, b):
                    dve.wait_ge(s_done, B * i + b + 1)
                    dve.wait_ge(exp_ok, 2 * (B * i + b) - 2 if b >= R else 2 * B * i + 2 * (L - 1))
                    m = nmax[:, b % R, :]
                    o.step(dve, dve.tensor_reduce(m, sc[b % L][:].rearrange("p (q s) -> p q s", q=QT), AX, ALU.max, negate=True))
                    dve.tensor_scalar(m, m, D ** -0.5, None, ALU.mult).then_inc(max_ok, 1)

                def factors(i, b):
                    dve.wait_ge(exp_ok, 2 * (B * i + b + 1) + 2 * (L - 1))
                    dve.wait_ge(pr_ok, B * i + b - 3) if b >= R else dve.wait_ge(pr_ok, B * i)
                    o.step(dve, dve.reciprocal(rs[:, b % R, :], sums[:, b % R, :]))
                    dve.tensor_scalar(rs[:, b % R, :], rs[:, b % R, :], 0.1, None, ALU.mult).then_inc(rs_ok, 1)

                def copy_turned(i, b):
                    n = B * i + b
                    dve.wait_ge(t_done, n + R)
                    dve.wait_ge(y_done, n)
                    dve.tensor_copy(pt[:, b % R, :], tp[b % 2][:]).then_inc(pt_ok, 1)

                def add(i, b):
                    dve.wait_ge(y_done, B * i + b + R)
                    fb = F[:, :, b * S:(b + 1) * S]
                    dve.tensor_tensor(fb, fb, yb[b % 2][:, 0:S].unsqueeze(1).to_broadcast([P, KD, S]), ALU.add).then_inc(added, 1)
                with dve.Fori(0, A) as i:
                    o.begin(i, 2 * B)
                    sum_halves(i, 0)
                    for b in range(B):
                        if b + 1 < B:
                            sum_halves(i, b + 1)
                        maximum(i, b)
                        if b >= 1:
                            factors(i, b - 1)
                        if b >= 2:
                            copy_turned(i, b - 2)
                        if b >= 3:
                            add(i, b - 3)
                    factors(i, B - 1)
                    for b in (B - 3, B - 2, B - 1):
                        if b > B - 3:
                            copy_turned(i, b)
                        add(i, b)
                    o.end(A)


@stage
def l3_xattn(K):
    nc, a, X, XT, CT, bank = K.nc, K.a, K.X, K.XT, K.CT, K.bank
    N = 1024
    KN = N // P
    with ExitStack() as ctx:
        def sb(n, shape, dt=F32, c=ctx):
            return c.enter_context(nc.sbuf_tensor("l3x_" + n, shape, dt))
        first = 3
        ws = [(n[len("L3_xattn_W_"):-1], rows, cols) for n, rows, cols in TERNARY[first:]]
        qw = sb("qw", [P, TERNARY_AT[-1] - TERNARY_AT[first]], BF16)
        q, wsc, bias = {}, {}, {}
        for i, (n, rows, cols) in enumerate(ws, first):
            q[n] = qw[:, TERNARY_AT[i] - TERNARY_AT[first]:TERNARY_AT[i + 1] - TERNARY_AT[first]].rearrange("p (k n) -> p k n", n=cols)
            wsc[n] = K.wscale[:, i:i + 1]
            bias[n] = sb("b_" + n, [P, D if n == "f2" else cols // P])
        loaded = K.sem("l3x_loaded")

        def load(sp):
            for n, rows, cols in ws:
                src = a[f"L3_xattn_b_{n}"]
                sp.dma_start(bias[n][:], src.partition_broadcast(P) if n == "f2" else src).then_inc(loaded, 16)
            sp.dma_start(qw[:], K.qweights[:, TERNARY_AT[first]:]).then_inc(loaded, 16)
            sp.wait_ge(loaded, 16 * (len(ws) + 1))
        layernorm(K, "l3x_ln", load, have_stats=K.first < 6)

        s = sb("s", [P, 6])
        hctx = ExitStack()
        hid, hid_max = sb("hid", [P, KN, T], F32, hctx), sb("hid_max", [P, NC * KN], F32, hctx)
        with ExitStack() as c1:
            qa = sb("qa", [P, 4, T], BF16, c1)
            kv = sb("kv", [P, 2, T], F32, c1)
            avg = sb("avg", [P, KD, B], F32, c1)
            avg_q = sb("avgq", [P, KD, B], BF16, c1)
            global_quant(K, "l3q0", [([(CT[:, 0, :], qa[:, 0, :]), (CT[0:HALF_C, 1, :], qa[0:HALF_C, 1, :])], s[:, 0:1]),
                                     ([(XT[:, k, :], qa[:, 2 + k, :]) for k in range(KD)], s[:, 1:2])])
            vis_max, img_max = sb("vis_max", [P, NC * KD], F32, c1), sb("img_max", [P, NC * KD], F32, c1)
            VIS, FUSED = CT, XT
            bit_linear(K, "l3l0", [(qa[:, 0:2, :], q["d2v"], DC, VIS, s[:, 0:1], wsc["d2v"], bias["d2v"]),
                                   (qa[:, 2:4, :], q["txt"], D, FUSED, s[:, 1:2], wsc["txt"], bias["txt"])], maxima=vis_max)
            global_quant(K, "l3q1", [([(VIS[:, k, :], qa[:, k, :]) for k in range(KD)], s[:, 2:3])], maxima=vis_max[:])
            IMG = VIS
            bit_linear(K, "l3l1", [(qa[:, 0:2, :], q["img"], D, IMG, s[:, 2:3], wsc["img"], bias["img"])], maxima=img_max)
            with nc.Block() as block:
                @block.vector
                def _(dve):
                    for k in range(KD):
                        K.dve_order.step(dve, dve.tensor_reduce(avg[:, k, :], IMG[:, k, :].rearrange("p (b s) -> p b s", s=S), AX, ALU.add))
                    dve.tensor_scalar(avg[:], avg[:], 1.0 / S, None, ALU.mult)
            global_quant(K, "l3q2", [([(IMG[:, k, :], qa[:, k, :]) for k in range(KD)], s[:, 3:4])], maxima=img_max[:])
            bit_linear(K, "l3l2", [(qa[:, 0:2, :], q["att%d" % i], D, kv[:, i:i + 1, :], s[:, 3:4], wsc["att%d" % i], bias["att%d" % i])
                                   for i in range(2)])
            shared_key_attention(K, "l3a", FUSED, kv, [hid[:, i, :] for i in range(3)])
            flat = "p k b -> p (k b)"
            global_quant(K, "l3q3", [([(FUSED[:, k, :], qa[:, k, :]) for k in range(KD)]
                                      + [(avg[:].rearrange(flat), avg_q[:].rearrange(flat))], s[:, 4:5])])
            with nc.Block() as block:
                @block.vector
                def _(dve):
                    for k in range(KD):
                        dve.tensor_copy(qa[:, 2 + k, :].rearrange("p (b s) -> p b s", s=S), avg_q[:, k, :].unsqueeze(2).to_broadcast([P, B, S]))
            bit_linear(K, "l3l3", [(qa, q["f1"], 2 * D, hid, s[:, 4:5], wsc["f1"], bias["f1"])], relu=True, maxima=hid_max)
        inv = sb("inv", [P, 1], F32, hctx)
        global_quant(K, "l3q4", [([], s[:, 5:6])], maxima=hid_max[:], inverse=inv)
        qh, out_scale = sb("qh", [P, KN, T], BF16, hctx), sb("oscale", [P, 1], F32, hctx)
        tmp = sb("tmp", [P, 4, D], F32, hctx)
        scaled, quantised, y_done, y_read = (K.sem("l3x_" + n) for n in ("scaled", "quantised", "ydone", "yread"))
        y = bank[0:4]
        with nc.Block() as block:
            @block.scalar
            def _(act):
                with act.Fori(0, NC) as c:
                    for half in range(2):
                        x = hid[:, half * KN // 2:(half + 1) * KN // 2, ds(c * CH, CH)]
                        act.activation(x, x, ACT.Identity, bias=K.round[:], scale=inv[:]).then_inc(scaled, 1)

            @block.tensor
            def _(pe):
                with pe.Fori(0, NC) as c:
                    pe.wait_ge(quantised, 2 * (c + 1))
                    for j in range(TPC):
                        pe.wait_ge(y_read, TPC * c + j + 1)
                        for k in range(KN):
                            last = pe.matmul(y[j][:, 0:D], qh[:, k, ds(c * CH + j * P, P)], q["f2"][:, k, :], start=k == 0, stop=k == KN - 1)
                        last.then_inc(y_done, 1)

            @block.vector
            def _(dve):
                o = K.dve_order

                def quantise(c):
                    for half in range(2):
                        w = slice(half * KN // 2, (half + 1) * KN // 2)
                        dve.wait_ge(scaled, 2 * c + half + 1)
                        dve.tensor_scalar(qh[:, w, ds(c * CH, CH)], hid[:, w, ds(c * CH, CH)], ROUND, None, ALU.subtract).then_inc(quantised, 1)

                def add(c):
                    for j in range(TPC):
                        dve.wait_ge(y_done, TPC * c + j + 1)
                        dve.scalar_tensor_tensor(tmp[:, j, :], y[j][:, 0:D], out_scale[:], bias["f2"][:], ALU.mult, ALU.add).then_inc(y_read, 1)
                    dve.wait_ge(y_read, TPC * (c + 2))
                    xt = X[:, ds(c * TPC, TPC), :]
                    o.step(dve, dve.tensor_tensor(xt, xt, tmp[:], ALU.add))
                    for j in range(TPC):
                        token_stats(K, dve, c * TPC + j)
                dve.sem_inc(y_read, TPC)
                o.step(dve, dve.tensor_tensor(out_scale[:], s[:, 5:6], wsc["f2"], ALU.mult))
                quantise(0)
                with dve.Fori(0, NC - 1) as c:
                    o.begin(c, 1)
                    quantise(c + 1)
                    add(c)
                    o.end(NC - 1)
                add(NC - 1)
        hctx.close()


def place_tokens(K, name, mask, gates, slot, gate, tile_expert):
    nc, bank = K.nc, K.bank
    E = EXPERTS3
    FAR = 2.0 * SLOT_TILES * P
    with ExitStack() as ctx:
        def sb(n, shape, dt=F32):
            return ctx.enter_context(nc.sbuf_tensor(f"{name}_{n}", shape, dt))
        before, ones, chosen = sb("before", [P, P], BF16), sb("ones", [P, P], BF16), sb("chosen", [P, NT, E], BF16)
        pos, hit, pick, edge = sb("pos", [P, NT, E]), sb("hit", [P, NT, E]), sb("pick", [P, NT, E]), sb("edge", [P, NT, 1])
        ends, shifted = sb("ends", [P, E]), sb("shifted", [P, E])
        passed, te = sb("passed", [1, SLOT_TILES, E]), sb("te", [1, SLOT_TILES])
        tri, counted, chosen_ok = K.sem(name + "_tri"), K.sem(name + "_counted"), K.sem(name + "_chosen")
        with nc.Block() as block:
            @block.gpsimd
            def _(pool):
                pool.memset(ones[:], 1.0).then_inc(tri, 1)
                pool.wait_ge(tri, 1)
                pool.affine_select(out=before[:], in_=ones[:], compare_op=ALU.is_gt, fill=0.0, base=0,
                                   pattern=[[1, P]], channel_multiplier=-1).then_inc(tri, 1)

            @block.tensor
            def _(pe):
                pe.wait_ge(chosen_ok, 1)
                pe.wait_ge(tri, 2)
                for t in range(NT):
                    pe.matmul(bank[0][:, 0:E], ones[:], chosen[:, t, :], start=t == 0, stop=t == NT - 1)
                pe.matmul(bank[1][:, 0:NT * E], before[:], chosen[:].rearrange("p t e -> p (t e)"), start=True, stop=False)
                for u in range(1, NT):
                    pe.matmul(bank[1][:, u * E:NT * E], ones[:], chosen[:, 0:NT - u, :].rearrange("p t e -> p (t e)"),
                              start=False, stop=u == NT - 1)
                pe.matmul(bank[2][:, 0:P], ones[:], before[:], start=True, stop=True).then_inc(counted, 1)

            @block.vector
            def _(dve):
                o = K.dve_order
                dve.tensor_copy(chosen[:], mask).then_inc(chosen_ok, 1)
                dve.wait_ge(counted, 1)
                o.step(dve, dve.tensor_scalar(ends[:], bank[0][:, 0:E], 1.0 / P, 0.5 - 0.5 / P, ALU.mult, ALU.add))
                o.step(dve, dve.tensor_scalar(ends[:], ends[:], ROUND, None, ALU.add))
                o.step(dve, dve.tensor_scalar(ends[:], ends[:], ROUND, None, ALU.subtract))
                n = 1
                while n < E:
                    o.step(dve, dve.tensor_copy(shifted[:], ends[:]))
                    o.step(dve, dve.tensor_tensor(ends[:, n:E], ends[:, n:E], shifted[:, 0:E - n], ALU.add))
                    n *= 2
                o.mark(dve.memset(shifted[:, 0:1], 0.0))
                o.step(dve, dve.tensor_scalar(shifted[:, 1:E], ends[:, 0:E - 1], float(P), None, ALU.mult))
                every = [P, NT, E]
                o.mark(dve.tensor_tensor(pos[:], bank[1][:, 0:NT * E].rearrange("p (t e) -> p t e", e=E),
                                         shifted[:].unsqueeze(1).to_broadcast(every), ALU.add))
                o.mark(dve.tensor_tensor(passed[:], ends[0:1, :].unsqueeze(1).to_broadcast([1, SLOT_TILES, E]),
                                         bank[2][0:1, 0:SLOT_TILES].unsqueeze(2).to_broadcast([1, SLOT_TILES, E]), ALU.is_le))
                o.wait(dve)
                o.step(dve, dve.tensor_reduce(te[:], passed[:], AX, ALU.add))
                o.mark(dve.tensor_scalar(tile_expert, te[:], E - 1.0, None, ALU.min))
                for i, sign in enumerate((-1.0, 1.0)):
                    o.step(dve, dve.scalar_tensor_tensor(hit[:], mask, sign * FAR, pos[:], ALU.mult, ALU.add))
                    o.step(dve, dve.tensor_reduce(edge[:], hit[:], AX, ALU.min if i == 0 else ALU.max))
                    o.step(dve, dve.tensor_tensor(pick[:], hit[:], edge[:].to_broadcast(every), ALU.is_equal))
                    o.step(dve, dve.tensor_tensor(pick[:], pick[:], gates, ALU.mult))
                    o.mark(dve.tensor_reduce(gate[i], pick[:], AX, ALU.add))
                    o.step(dve, dve.tensor_scalar(slot[i], edge[:].rearrange("p t a -> p (t a)"), -sign * FAR, None, ALU.add))


def routed_tiles(K, name, E, N, wu, wd, b1, b2_src, tile_expert, weights, weights_n):
    nc, bank = K.nc, K.bank
    HT, U = N // P, 3
    assert SLOT_TILES % U == 0
    up_b, turn_b, x_b, y_b = bank[0:2], bank[2:4], bank[4], bank[5]
    area = K.XT[:].rearrange("p k t -> p (k t)")

    def part(at, n, k):
        return area[:, at:at + n * k].rearrange("p (k n) -> p k n", k=k)
    xs, ys, xT = part(0, D, U), part(U * D, D, U), part(2 * U * D, P, KD)
    h, hT = area[:, 7 * D:7 * D + N], part(7 * D + N, P, HT)
    b2 = K.CT[:].rearrange("p k t -> p (k t)")[:, 0:E * D].rearrange("p (e d) -> p e d", e=E)
    x_in = [K.sem(f"{name}_xin{u}") for u in range(U)]
    y_out = [K.sem(f"{name}_yout{u}") for u in range(U)]
    b2_in, x_turned, xT_ok, up_done, h_act, h_dve, turned, hT_act, hT_dve, y_done, y_ok = (
        K.sem(f"{name}_{n}") for n in ("b2in", "xturned", "xtok", "updone", "hact", "hdve", "turned", "htact", "htdve", "ydone", "yok"))
    G = SLOT_TILES // U

    def tiles(eng, body):
        for u in range(U):
            body(u, u, u == 0, False)
        with eng.Fori(1, G - 1) as g:
            for u in range(U):
                body(g * U + u, u, False, False)
        for u in range(U):
            body((G - 1) * U + u, u, False, u == U - 1)

    def expert(eng, i):
        at = tile_expert[:, i:i + 1] if isinstance(i, int) else tile_expert[:, ds(i, 1)]
        return eng.value_load(at, min_val=0, max_val=E - 1)

    with nc.Block() as block:
        @block.sync
        def _(sp):
            sp.dma_start(b2.rearrange("p e d -> p (e d)"), b2_src.partition_broadcast(P)).then_inc(b2_in, 16)

            def load(i, u):
                sp.dma_start(xs[:, u, :], K.slots[ds(i * P, P), :]).then_inc(x_in[u], 16)

            def store(i, u):
                sp.wait_ge(y_ok, i + 1)
                sp.dma_start(K.slot_out[ds(i * P, P), :], ys[:, u, :]).then_inc(y_out[u], 16)
            for u in range(U):
                load(u, u)
            with sp.Fori(0, G - 1) as g:
                for u in range(U):
                    i = g * U + u
                    sp.wait_ge(x_turned, i + 1)
                    load(i + U, u)
                    store(i, u)
            for u in range(U):
                store((G - 1) * U + u, u)
            for u in range(U):
                sp.wait_ge(y_out[u], 16 * G)

        @block.tensor
        def _(pe):
            def turn_input(i, u, n):
                pe.wait_ge(x_in[u], 16 * n)
                for k in range(KD):
                    last = pe.transpose(x_b[:, k * P:(k + 1) * P], xs[:, u, k * P:(k + 1) * P], K.ident[:])
                last.then_inc(x_turned, 1)

            def up(i):
                e = expert(pe, i)
                pe.wait_ge(xT_ok, i + 1)
                for half in range(2):
                    for k in range(KD):
                        last = pe.matmul(up_b[half][:], xT[:, k, :], wu[:, ds(e * KD + k, 1), half * CH:(half + 1) * CH].rearrange("p a n -> p (a n)"),
                                         start=k == 0, stop=k == KD - 1)
                    last.then_inc(up_done, 1)

            def down(i):
                e = expert(pe, i)
                pe.wait_ge(hT_act, i + 1)
                pe.wait_ge(hT_dve, i + 1)
                for m in range(HT):
                    last = pe.matmul(y_b[:, 0:D], hT[:, m, :], wd[:, ds(e * HT + m, 1), :].rearrange("p a n -> p (a n)"),
                                     start=m == 0, stop=m == HT - 1)
                last.then_inc(y_done, 1)

            def turn_hidden(i):
                for half in range(2):
                    pe.wait_ge(h_act if half == 0 else h_dve, i + 1)
                    for j in range(HT // 2):
                        m = half * (HT // 2) + j
                        last = pe.transpose(turn_b[half][:, j * P:(j + 1) * P], h[:, m * P:(m + 1) * P], K.ident[:])
                    last.then_inc(turned, 1)
            pe.wait_ge(weights, weights_n)
            turn_input(0, 0, 1)

            def body(i, u, n, first, last):
                up(i)
                if not last:
                    turn_input(i + 1, (u + 1) % U, n + (u + 1) // U)
                if not first:
                    down(i - 1)
                turn_hidden(i)
            for u in range(U):
                body(u, u, 1, u == 0, False)
            with pe.Fori(1, G - 1) as g:
                for u in range(U):
                    body(g * U + u, u, g + 1, False, False)
            for u in range(U):
                body((G - 1) * U + u, u, G, False, u == U - 1)
            down(SLOT_TILES - 1)

        @block.scalar
        def _(act):
            act.wait_ge(x_turned, 1)
            act.activation(xT.rearrange("p k n -> p (k n)"), x_b[:, 0:D], ACT.Copy).then_inc(xT_ok, 1)

            def body(i, u, first, last):
                e = expert(act, i)
                act.wait_ge(up_done, 2 * i + 1)
                act.activation(h[:, 0:CH], up_b[0][:], ACT.Copy).then_inc(h_act, 1)
                if not last:
                    act.wait_ge(x_turned, i + 2)
                    act.activation(xT.rearrange("p k n -> p (k n)"), x_b[:, 0:D], ACT.Copy).then_inc(xT_ok, 1)
                act.wait_ge(turned, 2 * i + 1)
                for m in range(HT // 2):
                    last_one = act.activation(hT[:, m, :], turn_b[0][:, m * P:(m + 1) * P], ACT.Relu, bias=b1[:, ds(e * HT + m, 1)])
                last_one.then_inc(hT_act, 1)
            tiles(act, body)

        @block.vector
        def _(dve):
            def output(i, u, n):
                e = expert(dve, i)
                dve.wait_ge(y_done, i + 1)
                if not isinstance(n, int) or n > 0:
                    dve.wait_ge(y_out[u], 16 * n)
                dve.tensor_tensor(ys[:, u, :], y_b[:, 0:D], b2[:, ds(e, 1), :].rearrange("p a n -> p (a n)"), ALU.add).then_inc(y_ok, 1)

            def body(i, u, n, first, last):
                e = expert(dve, i)
                dve.wait_ge(up_done, 2 * i + 2)
                dve.tensor_copy(h[:, CH:N], up_b[1][:]).then_inc(h_dve, 1)
                if not first:
                    output(i - 1, (u - 1) % U, n if u else n - 1)
                dve.wait_ge(turned, 2 * i + 2)
                for j in range(HT // 2):
                    m = HT // 2 + j
                    last_one = dve.tensor_scalar(hT[:, m, :], turn_b[1][:, j * P:(j + 1) * P], b1[:, ds(e * HT + m, 1)], 0.0, ALU.add, ALU.max)
                last_one.then_inc(hT_dve, 1)
            dve.wait_ge(b2_in, 16)
            for u in range(U):
                body(u, u, 0, u == 0, False)
            with dve.Fori(1, G - 1) as g:
                for u in range(U):
                    body(g * U + u, u, g, False, False)
            for u in range(U):
                body((G - 1) * U + u, u, G - 1, False, u == U - 1)
            output(SLOT_TILES - 1, U - 1, G - 1)


@stage
def l3_ffn(K):
    nc, a, X = K.nc, K.a, K.X
    E, N = EXPERTS3, 1024
    HT = N // P
    with ExitStack() as ctx:
        def sb(n, shape, dt=F32):
            return ctx.enter_context(nc.sbuf_tensor("l3f_" + n, shape, dt))
        wu, wd = sb("wu", [P, E * KD, N]), sb("wd", [P, E * HT, D])
        w, br, b1 = sb("wr", [P, KD, E]), sb("br", [P, E]), sb("b1", [P, E * HT])
        tile_expert = sb("tile_expert", [1, SLOT_TILES], I32)
        slot = [sb(f"slot{i}", [P, NT], I32) for i in range(TOP3)]
        gate = [sb(f"gate{i}", [P, NT]) for i in range(TOP3)]
        loaded, weights, scattered = K.sem("l3f_loaded"), K.sem("l3f_weights"), K.sem("l3f_scattered")
        gathered = [K.sem(f"l3f_gathered{i}") for i in range(NT)]
        XN = K.CT[:].rearrange("p k t -> p (k t)").rearrange("p (t d) -> p t d", d=D)

        def load(sp):
            load_rows(sp, w, a["L3_ffn_Wr"], loaded)
            sp.dma_start(br[:], a["L3_ffn_br"].partition_broadcast(P)).then_inc(loaded, 16)
            sp.dma_start(b1[:], a["L3_ffn_b1p"].rearrange("p e m -> p (e m)")).then_inc(loaded, 16)
            for e in range(E):
                sp.dma_start(wu[:, e * KD:(e + 1) * KD, :], a["L3_ffn_W1"][e].rearrange("(k p) n -> p k n", p=P)).then_inc(weights, 16)
                sp.dma_start(wd[:, e * HT:(e + 1) * HT, :], a["L3_ffn_W2"][e].rearrange("(k p) n -> p k n", p=P)).then_inc(weights, 16)
            sp.wait_ge(loaded, 48)
        layernorm(K, "l3f_ln", load, keep=XN, have_stats=K.first < 7)
        with ExitStack() as c1:
            gates, mask = (c1.enter_context(nc.sbuf_tensor("l3f_" + n, [P, NT, E], F32)) for n in ("gates", "mask"))
            router(K, "l3r", E, TOP3, w, br[:], gates[:], mask[:], False)
            place_tokens(K, "l3p", mask[:], gates[:], [s[:] for s in slot], [g[:] for g in gate], tile_expert[:])
        with nc.Block() as block:
            @block.gpsimd
            def _(pool):
                pool.wait_ge(K.slots_zeroed, 16)
                for t in range(NT):
                    for i in range(TOP3):
                        pool.indirect_dma_start(K.slots, bass.IndirectOffsetOnAxis(ap=slot[i][:, t:t + 1], axis=0),
                                                XN[:, t, :], None).then_inc(scattered, 16)
                pool.wait_ge(scattered, 16 * NT * TOP3)
        routed_tiles(K, "l3t", E, N, wu, wd, b1, a["L3_ffn_b2"], tile_expert, weights, 32 * E)
        YS = [XN, K.XT[:].rearrange("p k t -> p (k t)").rearrange("p (t d) -> p t d", d=D)]
        first = K.sem("l3f_first")
        with nc.Block() as block:
            @block.gpsimd
            def _(pool):
                for t in range(NT):
                    for i in range(TOP3):
                        pool.indirect_dma_start(YS[i][:, t, :], None, K.slot_out,
                                                bass.IndirectOffsetOnAxis(ap=slot[i][:, t:t + 1], axis=0)).then_inc(gathered[t], 16)

            @block.vector
            def _(dve):
                for t in range(NT):
                    dve.wait_ge(gathered[t], 16 * TOP3)
                    for i in range(TOP3):
                        dve.scalar_tensor_tensor(X[:, t, :], YS[i][:, t, :], gate[i][:, t:t + 1], X[:, t, :], ALU.mult, ALU.add).then_inc(first, 1)
                        dve.wait_ge(first, TOP3 * t + i + 1)


def build(nc, a, first=0, last=7):
    with ExitStack() as ctx:
        K = Shared()
        K.nc, K.a = nc, a
        K.sem = lambda n: ctx.enter_context(nc.semaphore(n))

        def sb(n, shape, dt=F32):
            return ctx.enter_context(nc.sbuf_tensor(n, shape, dt))
        K.first = first
        K.X, K.XT, K.CT = sb("X", [P, NT, D]), sb("XT", [P, KD, T]), sb("CT", [P, 2, T])
        K.ident, K.identb, K.ones = sb("ident", [P, P]), sb("identb", [P, P], BF16), sb("ones", [P, P])
        K.zero, K.slots_zeroed = sb("zero", [P, D]), K.sem("slots_zeroed")
        K.slots, K.slot_out = (nc.dram_tensor(n, (SLOT_TILES * P, D), F32, kind="Internal").ap() for n in ("slots", "slot_out"))
        K.ctx_loaded = K.sem("ctx_loaded")
        K.stats = sb("stats", [P, NT, 6])
        K.wscale = sb("wscale", [P, len(TERNARY)])
        K.qweights = nc.dram_tensor("qweights", (P, TERNARY_AT[-1]), BF16, kind="Internal").ap()
        K.round, K.carry = sb("round", [P, 1]), sb("carry", [P, 1])
        K.bank = [ctx.enter_context(nc.psum_tensor(f"bank{i}", [P, CH], F32)) for i in range(8)]
        K.dve_order, K.act_order, K.pool_order = (Order(K.sem(n)) for n in ("dve_order", "act_order", "pool_order"))
        stages = [l0_cosine, l0_ffn, l1_xattn, l1_ffn, l2_xattn, l2_ffn, l3_xattn, l3_ffn]
        start(K)
        if first > 0:
            with nc.Block() as block:
                @block.sync
                def _(sp):
                    sp.wait_ge(K.ctx_loaded, 48)
        for sublayer in stages[first:last + 1]:
            sublayer(K)
        finish(K)


def _t(w):
    import numpy as np
    return np.ascontiguousarray(np.swapaxes(w, -1, -2))


def arrays(inputs):
    import numpy as np
    i = {k: np.asarray(v) for k, v in inputs.items()}
    r = {"x": i["x"], "ctxT": _t(i["ctx_768"].reshape(T, DC))}
    r["L0_xattn_WvT"], r["L0_xattn_WtT"] = _t(i["L0_xattn_Wv"]), _t(i["L0_xattn_Wt"])
    r["L0_xattn_bv"], r["L0_xattn_bt"] = i["L0_xattn_bv"], i["L0_xattn_bt"]
    r["L0_ffn_router_wT"] = _t(i["L0_ffn_router_w"])
    r["L0_ffn_upT"] = _t(np.concatenate([i["L0_ffn_shared_up"], i["L0_ffn_routed_up"]]))
    r["L0_ffn_downT"] = _t(np.concatenate([i["L0_ffn_shared_down"], i["L0_ffn_routed_down"]]))
    for n in ("L1_xattn", "L2_xattn"):
        for w in ("Wq", "Wk", "Wv", "Wo", "bo"):
            r[f"{n}_{w}"] = i[f"{n}_{w}"]
    for w in ("w_gate", "w_up", "w_down"):
        r[f"L1_ffn_{w}T"] = _t(i[f"L1_ffn_{w}"])
    def feature_columns(b):
        return np.moveaxis(b.reshape(b.shape[:-1] + (-1, P)), -1, 0)
    n = "L2_ffn_"
    r[n + "WvT"], r[n + "bv"], r[n + "b2"] = _t(i[n + "Wv"]), feature_columns(i[n + "bv"]), i[n + "b2"]
    r[n + "W1cat"] = np.concatenate([_t(i[n + "Wg"]), _t(i[n + "W1"].reshape(-1, D)), _t(i[n + "Wp"].reshape(-1, D))], axis=1)
    r[n + "b1cat"] = np.concatenate([i[n + "bg"], i[n + "b1"].reshape(-1)])[None]
    r[n + "W2cat"] = _t(i[n + "W2"]).reshape(-1, D)
    r[n + "alpha"] = i[n + "alpha"].reshape(1, 1)
    r[n + "gb"] = np.concatenate([i[n + "g_r"], i[n + "g_c"], i[n + "b_r"], i[n + "b_c"]])[None]
    for w in ("d2v", "img", "txt", "att0", "att1", "f1", "f2"):
        r[f"L3_xattn_W_{w}T"] = _t(i["L3_xattn_W_" + w])
        b = i["L3_xattn_b_" + w]
        r["L3_xattn_b_" + w] = b[None] if w == "f2" else feature_columns(b)
    n = "L3_ffn_"
    for w in ("Wr", "br", "W1", "W2", "b2"):
        r[n + w] = i[n + w]
    r[n + "br"], r[n + "b2"] = i[n + "br"][None], i[n + "b2"].reshape(1, -1)
    r[n + "b1p"] = feature_columns(i[n + "b1"])
    return {k: np.ascontiguousarray(v) for k, v in r.items()}


def kernel(**inputs):
    import concourse.bacc as bacc
    from concourse.bass_utils import run_bass_kernel_spmd
    nc = bacc.Bacc("TRN2", target_bir_lowering=False, num_devices=1)
    data = arrays(inputs)
    aps = {n: nc.dram_tensor("in_" + n, v.shape, mybir.dt.from_np(v.dtype), kind="ExternalInput").ap() for n, v in data.items()}
    aps["out"] = nc.dram_tensor("out_x", (B, S, D), F32, kind="ExternalOutput").ap()
    build(nc, aps)
    r = run_bass_kernel_spmd(nc, [{"in_" + n: v for n, v in data.items()}], core_ids=[0])
    return r.results[0]["out_x"]
```
